# Optimizing a Trainium2 kernel written in Bass

```python
import numpy as np
import jax
import jax.numpy as jnp

def _softmax(x, axis=-1):
    return jax.nn.softmax(x, axis=axis)

def _gelu(x):
    return jax.nn.gelu(x, approximate=True)

def _silu(x):
    return jax.nn.silu(x)

def _sigmoid(x):
    return jax.nn.sigmoid(x)

def _layernorm(x, axis=-1, eps=1e-05):
    m = jnp.mean(x, axis=axis, keepdims=True)
    v = jnp.var(x, axis=axis, keepdims=True)
    return (x - m) / jnp.sqrt(v + eps)

def _scatter_add(tgt, idx, src, axis=0):
    return tgt.at[idx].add(src)

def _segment_sum(src, seg, n):
    return jax.ops.segment_sum(src, seg, n)
kernel_name = 'mk_adj_ffn_d2_adj_r2_ecdef1'

def setup_inputs(seed: int=0):
    np.random.seed(seed)
    _w = jnp.asarray

    def _rec_inputs():
        import jax
        import jax.numpy as jnp
        _gk = jax.random.key(seed)
        x = -0.0002928 + 1 * jax.random.normal(jax.random.fold_in(_gk, 1), (4096, 256), jnp.float32)
        _a = jax.random.bernoulli(jax.random.fold_in(_gk, 2), 0.000488281, (4096, 4096))
        _a = jnp.logical_or(_a, jnp.swapaxes(_a, -1, -2))
        _a = jnp.logical_or(_a, jnp.eye(4096, dtype=bool))
        _af = _a.astype(jnp.float32)
        _af = _af * jax.random.uniform(jax.random.fold_in(_gk, 3), (4096, 4096), jnp.float32, 0.05, 1)
        adj = _af
        return (x, adj)
    x, adj = _rec_inputs()

    def _L0_gnn_setup():
        import jax, jax.numpy as jnp
        import numpy as np

        def _bin_sign(v):
            return jnp.sign(v)

        def _bin_sign_z(v):
            return jnp.maximum(jnp.sign(v), 0.0)
        key = jax.random.key(seed)
        k1, k2, k3 = jax.random.split(key, 3)
        N, D_IN, D_OUT = (4096, 256, 256)
        x = jax.random.normal(k1, (N, D_IN), dtype=jnp.float32)
        support = jax.random.uniform(k2, (N, N), dtype=jnp.float32)
        weight = jax.random.normal(k3, (D_OUT, D_IN), dtype=jnp.float32)
        return {'x': x, 'support': support, 'weight': weight}
    _L0_gnn_all = _L0_gnn_setup()
    _L0_gnn_in = {k: v for k, v in _L0_gnn_all.items() if k in ('weight',)}
    del _L0_gnn_all

    def _L0_ffn_setup():
        import jax, jax.numpy as jnp
        import numpy as np
        TOP_K = 6
        CAP_FACTOR = 2.0
        key = jax.random.key(seed)
        ks = jax.random.split(key, 9)
        B, S, D, F, E, SH = (4, 1024, 256, 128, 64, 2)
        return {'x': jax.random.normal(ks[0], (B, S, D), jnp.float32), 'router_w': jax.random.normal(ks[1], (E, D), jnp.float32) * 0.02, 'bias': jnp.zeros((E,), jnp.float32), 'shared_w_gate': jax.random.normal(ks[2], (SH, F, D), jnp.float32) * 0.02, 'shared_w_up': jax.random.normal(ks[3], (SH, F, D), jnp.float32) * 0.02, 'shared_w_down': jax.random.normal(ks[4], (SH, D, F), jnp.float32) * 0.02, 'w_gate': jax.random.normal(ks[5], (E, F, D), jnp.float32) * 0.02, 'w_up': jax.random.normal(ks[6], (E, F, D), jnp.float32) * 0.02, 'w_down': jax.random.normal(ks[7], (E, D, F), jnp.float32) * 0.02}
    _L0_ffn_all = _L0_ffn_setup()
    _L0_ffn_in = {k: v for k, v in _L0_ffn_all.items() if k in ('router_w', 'bias', 'shared_w_gate', 'shared_w_up', 'shared_w_down', 'w_gate', 'w_up', 'w_down')}
    del _L0_ffn_all

    def _L1_gnn_setup():
        import jax, jax.numpy as jnp
        import numpy as np
        IN_F = 256
        OUT_F = 256
        N = 4096
        key = jax.random.key(seed)
        k1, k2, k3 = jax.random.split(key, 3)
        x = jax.random.normal(k1, (N, IN_F), dtype=jnp.float32)
        graph = jax.random.uniform(k2, (N, N), dtype=jnp.float32)
        std = float(np.sqrt(2.0 / (IN_F + OUT_F)))
        weight = jax.random.normal(k3, (IN_F, OUT_F), dtype=jnp.float32) * std
        bias = jnp.zeros((OUT_F,), dtype=jnp.float32)
        return {'x': x, 'graph': graph, 'weight': weight, 'bias': bias}
    _L1_gnn_all = _L1_gnn_setup()
    _L1_gnn_in = {k: v for k, v in _L1_gnn_all.items() if k in ('weight', 'bias')}
    del _L1_gnn_all

    def _L1_ffn_setup():
        import jax, jax.numpy as jnp
        import numpy as np
        B, S, D, F, E, K = (64, 256, 256, 1024, 8, 2)
        key = jax.random.key(seed)
        k0, k1, k2, k3 = jax.random.split(key, 4)
        x = jax.random.normal(k0, (B, S, D), dtype=jnp.float32)
        Wr = jax.random.normal(k1, (D, E), dtype=jnp.float32) * D ** (-0.5)
        br = jnp.zeros((E,), dtype=jnp.float32)
        W1 = jax.random.normal(k2, (E, D, F), dtype=jnp.float32) * D ** (-0.5)
        b1 = jnp.zeros((E, F), dtype=jnp.float32)
        W2 = jax.random.normal(k3, (E, F, D), dtype=jnp.float32) * F ** (-0.5)
        b2 = jnp.zeros((E, D), dtype=jnp.float32)
        return {'x': x, 'Wr': Wr, 'br': br, 'W1': W1, 'b1': b1, 'W2': W2, 'b2': b2}
    _L1_ffn_all = _L1_ffn_setup()
    _L1_ffn_in = {k: v for k, v in _L1_ffn_all.items() if k in ('Wr', 'br', 'W1', 'b1', 'W2', 'b2')}
    del _L1_ffn_all
    return {'x': x, 'adj': adj, 'L0_gnn_weight': _L0_gnn_in['weight'], 'L0_ffn_router_w': _L0_ffn_in['router_w'], 'L0_ffn_bias': _L0_ffn_in['bias'], 'L0_ffn_shared_w_gate': _L0_ffn_in['shared_w_gate'], 'L0_ffn_shared_w_up': _L0_ffn_in['shared_w_up'], 'L0_ffn_shared_w_down': _L0_ffn_in['shared_w_down'], 'L0_ffn_w_gate': _L0_ffn_in['w_gate'], 'L0_ffn_w_up': _L0_ffn_in['w_up'], 'L0_ffn_w_down': _L0_ffn_in['w_down'], 'L1_gnn_weight': _L1_gnn_in['weight'], 'L1_gnn_bias': _L1_gnn_in['bias'], 'L1_ffn_Wr': _L1_ffn_in['Wr'], 'L1_ffn_br': _L1_ffn_in['br'], 'L1_ffn_W1': _L1_ffn_in['W1'], 'L1_ffn_b1': _L1_ffn_in['b1'], 'L1_ffn_W2': _L1_ffn_in['W2'], 'L1_ffn_b2': _L1_ffn_in['b2']}

def reference(x, adj, L0_gnn_weight, L0_ffn_router_w, L0_ffn_bias, L0_ffn_shared_w_gate, L0_ffn_shared_w_up, L0_ffn_shared_w_down, L0_ffn_w_gate, L0_ffn_w_up, L0_ffn_w_down, L1_gnn_weight, L1_gnn_bias, L1_ffn_Wr, L1_ffn_br, L1_ffn_W1, L1_ffn_b1, L1_ffn_W2, L1_ffn_b2):
    import jax
    import jax.numpy as jnp

    def _L0_gnn_ref(x, support, weight):
        import jax, jax.numpy as jnp
        import numpy as np

        def _bin_sign(v):
            return jnp.sign(v)

        def _bin_sign_z(v):
            return jnp.maximum(jnp.sign(v), 0.0)
        bw = _bin_sign(weight)
        ba = _bin_sign_z(x)
        xw = ba @ bw.T
        out = support @ xw
        return jax.nn.relu(out)

    def _L0_ffn_ref(x, router_w, bias, shared_w_gate, shared_w_up, shared_w_down, w_gate, w_up, w_down):
        import jax, jax.numpy as jnp
        import numpy as np
        TOP_K = 6
        CAP_FACTOR = 2.0
        B, S, D = x.shape
        E = router_w.shape[0]
        K = TOP_K
        N = B * S
        C = max(1, int(N * K * CAP_FACTOR / E))
        router_logits = jnp.einsum('bsd,ed->bse', x, router_w) + bias
        hg = jnp.einsum('bsd,efd->bsef', x, shared_w_gate)
        hu = jnp.einsum('bsd,efd->bsef', x, shared_w_up)
        shared_out = jnp.einsum('bsef,edf->bsd', jax.nn.silu(hg) * hu, shared_w_down)
        shared_out = shared_out / shared_w_gate.shape[0]
        router_probs = jax.nn.softmax(router_logits, axis=-1)
        topk_p, topk_i = jax.lax.top_k(router_probs, K)
        topk_p = topk_p / (jnp.sum(topk_p, axis=-1, keepdims=True) + 1e-09)
        x_flat = x.reshape(N, D)
        flat_e = topk_i.reshape(-1)
        flat_g = topk_p.reshape(-1)
        token_ids = jnp.repeat(jnp.arange(N), K)
        order = jnp.argsort(flat_e)
        se = flat_e[order]
        st = token_ids[order]
        sg = flat_g[order]
        M = se.shape[0]
        pos = jnp.arange(M)
        is_first = jnp.concatenate([jnp.ones((1,), bool), se[1:] != se[:-1]])
        group_starts = jax.lax.cummax(pos * is_first.astype(pos.dtype))
        slot = pos - group_starts
        valid = slot < C
        safe_slot = jnp.where(valid, slot, C)
        expert_in = jnp.zeros((E, C + 1, D), x.dtype).at[se, safe_slot].set(x_flat[st])
        expert_gate = jnp.zeros((E, C + 1), x.dtype).at[se, safe_slot].set(sg)
        expert_tok = jnp.full((E, C + 1), N, jnp.int32).at[se, safe_slot].set(st.astype(jnp.int32))
        expert_mask = jnp.zeros((E, C + 1), bool).at[se, safe_slot].set(valid)
        expert_in = expert_in[:, :C]
        expert_gate = expert_gate[:, :C]
        expert_tok = expert_tok[:, :C]
        expert_mask = expert_mask[:, :C]
        hg = jnp.einsum('ecd,efd->ecf', expert_in, w_gate)
        hu = jnp.einsum('ecd,efd->ecf', expert_in, w_up)
        expert_out = jnp.einsum('ecf,edf->ecd', jax.nn.silu(hg) * hu, w_down)
        fm = expert_mask.reshape(-1)
        dst = jnp.where(fm, expert_tok.reshape(-1), N)
        fg = jnp.where(fm, expert_gate.reshape(-1), jnp.zeros((), x.dtype))
        sparse = jax.ops.segment_sum(fg[:, None] * expert_out.reshape(-1, D), dst, num_segments=N + 1)[:N]
        return shared_out + sparse.reshape(B, S, D)

    def _L1_gnn_ref(x, graph, weight, bias):
        import jax, jax.numpy as jnp
        import numpy as np
        IN_F = 256
        OUT_F = 256
        N = 4096
        gt = graph.T
        deg = jnp.sum(gt, axis=1)
        d_inv_sqrt = deg ** (-0.5)
        norm = d_inv_sqrt[:, None] * gt * d_inv_sqrt[None, :]
        h = x @ weight
        y = norm @ h + bias
        return y

    def _L1_ffn_ref(x, Wr, br, W1, b1, W2, b2):
        import jax, jax.numpy as jnp
        import numpy as np
        B, S, D, F, E, K = (64, 256, 256, 1024, 8, 2)
        orig_shape = x.shape
        t = x.reshape(-1, orig_shape[-1])
        logits = t @ Wr + br
        gates = jax.nn.softmax(logits, axis=-1)
        top_vals, top_idx = jax.lax.top_k(gates, K)
        top_vals = top_vals / top_vals.sum(axis=-1, keepdims=True)
        onehot = jax.nn.one_hot(top_idx, E, dtype=t.dtype)
        combine = jnp.einsum('tk,tke->te', top_vals, onehot)
        out = jnp.zeros_like(t)
        for e in range(E):
            h = jax.nn.relu(t @ W1[e] + b1[e])
            y = h @ W2[e] + b2[e]
            out = out + combine[:, e:e + 1] * y
        return out.reshape(orig_shape)
    x = x + _L0_gnn_ref(_layernorm(x, axis=-1), adj, L0_gnn_weight)
    x = x + _L0_ffn_ref(_layernorm(x, axis=-1)[None], L0_ffn_router_w, L0_ffn_bias, L0_ffn_shared_w_gate, L0_ffn_shared_w_up, L0_ffn_shared_w_down, L0_ffn_w_gate, L0_ffn_w_up, L0_ffn_w_down)[0]
    x = x + _L1_gnn_ref(_layernorm(x, axis=-1), adj, L1_gnn_weight, L1_gnn_bias)
    x = x + _L1_ffn_ref(_layernorm(x, axis=-1)[None], L1_ffn_Wr, L1_ffn_br, L1_ffn_W1, L1_ffn_b1, L1_ffn_W2, L1_ffn_b2)[0]
    return x

_drawn_inputs = setup_inputs


def setup_inputs(seed=0):
    import zlib

    import numpy as np

    out = dict(_drawn_inputs(seed))
    spreads = {'L0_ffn_bias': (0.0, 0.8),
     'L1_gnn_bias': (0.0, 0.8),
     'L1_ffn_br': (0.0, 0.8),
     'L1_ffn_b1': (0.0, 2.0),
     'L1_ffn_b2': (0.0, 0.8)}
    factors = {'L0_ffn_router_w': 8.0,
     'L0_ffn_shared_w_gate': 8.0,
     'L0_ffn_shared_w_up': 8.0,
     'L0_ffn_shared_w_down': 8.0,
     'L0_ffn_w_gate': 8.0,
     'L0_ffn_w_up': 8.0,
     'L0_ffn_w_down': 8.0}
    for name, (base, spread) in spreads.items():
        noise = np.random.default_rng([zlib.crc32(name.encode()), seed]).standard_normal(out[name].shape)
        drawn = base * np.exp(spread * noise) if base else spread * noise
        out[name] = jnp.asarray(drawn.astype(out[name].dtype))
    for name, factor in factors.items():
        out[name] = (out[name] * factor).astype(out[name].dtype)
    return out
```

```python
from contextlib import ExitStack

import numpy as np
import concourse.bass as bass
from concourse import mybir

F32 = mybir.dt.float32
F32R = mybir.dt.float32r
BF16 = mybir.dt.bfloat16
I32 = mybir.dt.int32
U32 = mybir.dt.uint32
ACT = mybir.ActivationFunctionType
ALU = mybir.AluOpType
AX = mybir.AxisListType
ds = bass.ds

P = 128
N, D = 4096, 256
NT = N // P
DC = D // P
EPS = 1e-5

E0, F0, K0 = 64, 128, 6
CAP = N * K0 * 2 // E0
RPP = CAP // P
HALF = CAP // 2
SLOTS0 = E0 * CAP
SKIP = 1 << 16
E1, F1, K1 = 8, 1024, 2
FB1 = F1 // P
T1 = 256
NT1 = N * K1 // T1 + E1
SLOTS1 = NT1 * T1

QW = 1024
NQ = N // QW
JS = 2
STEPS = NT // JS
RAW = 4
GR = STEPS // RAW
GT = QW // P


class Kernel:

    def __init__(self, nc, ctx):
        self.nc, self.ctx = nc, ctx

    def sem(self, name):
        return self.ctx.enter_context(self.nc.semaphore(name))


def wait_apart(eng, sem, value, passed):
    eng.wait_ge(sem, value)
    eng.sem_inc(passed, 1)


def make_constants(k):
    nc, c = k.nc, k.ctx
    sb = lambda n, s, d: c.enter_context(nc.sbuf_tensor(n, s, d))
    k.ident = sb("ident", [P, P], F32)
    k.identb = sb("identb", [P, P], BF16)
    k.tri = sb("tri", [P, P], BF16)
    k.onesb = sb("onesb", [P, P], BF16)
    k.iota = sb("iota", [P, E0], F32)
    k.x = sb("x", [P, NT, D], F32)
    k.deg = sb("deg", [P, NT], F32)
    k.dinv = sb("dinv", [P, NT], F32)
    k.minus_half = sb("minus_half", [P, NT], F32)
    k.passed = k.sem("passed")


def sign_features(k, x_in, w_t, xs0, xs1, y0):
    nc = k.nc
    G = NT // GT
    with ExitStack() as c:
        sb = lambda n, s, d: c.enter_context(nc.sbuf_tensor(n, s, d))
        ps = lambda n, s, d: c.enter_context(nc.psum_tensor(n, s, d))
        w_raw = sb("p1_w", [P, DC, D], F32)
        neg = sb("p1_neg", [P, DC, D], F32)
        sign_w = sb("p1_sign_w", [P, DC, D], BF16)
        total = sb("p1_total", [P, GT], F32)
        mean = sb("p1_mean", [P, GT], F32)
        pos = sb("p1_pos", [P, GT, D], BF16)
        pos_t = sb("p1_pos_t", [P, DC, GT * P], BF16)
        t_ps = ps("p1_t_ps", [P, DC, GT * P], BF16)
        xw_ps = ps("p1_xw_ps", [P, GT, D], F32)
        x_in_sem, w_sem, consts, fill = k.sem("x_loaded"), k.sem("p1_w_loaded"), k.sem("consts"), k.sem("p1_fill")
        signed, summed, averaged, positive = k.sem("p1_signed"), k.sem("p1_summed"), k.sem("p1_averaged"), k.sem("p1_positive")
        turned, turned_out, multiplied, xw_out = k.sem("p1_turned"), k.sem("p1_turned_out"), k.sem("p1_multiplied"), k.sem("p1_xw_out")

        with nc.Block() as block:
            @block.sync
            def _(sp):
                sp.dma_start(w_raw[:], w_t.rearrange("(c p) o -> p c o", p=P)).then_inc(w_sem, 16)
                for g in range(G):
                    sp.dma_start(k.x[:, g * GT:(g + 1) * GT, :],
                                 x_in[g * GT * P:(g + 1) * GT * P, :].rearrange("(t p) d -> p t d", p=P)).then_inc(x_in_sem, 16)

            @block.gpsimd
            def _(pool):
                pool.memset(k.ident[:], 0.0).then_inc(fill, 1)
                pool.memset(k.identb[:], 0.0).then_inc(fill, 1)
                pool.memset(k.tri[:], 0.0).then_inc(fill, 1)
                pool.memset(k.onesb[:], 1.0).then_inc(consts, 1)
                pool.memset(k.minus_half[:], -0.5).then_inc(consts, 1)
                pool.iota(k.iota[:], pattern=[[1, E0]], base=0, channel_multiplier=0,
                          allow_small_or_imprecise_dtypes=True).then_inc(consts, 1)
                pool.wait_ge(fill, 3)
                for m in (k.ident, k.identb):
                    pool.affine_select(out=m[:], in_=m[:], compare_op=ALU.not_equal, fill=1.0, base=0,
                                       pattern=[[-1, P]], channel_multiplier=1).then_inc(consts, 1)
                pool.affine_select(out=k.tri[:], in_=k.tri[:], compare_op=ALU.is_ge, fill=1.0, base=0,
                                   pattern=[[-1, P]], channel_multiplier=1).then_inc(consts, 1)

            @block.vector
            def _(dve):
                dve.wait_ge(w_sem, 16)
                dve.tensor_scalar(neg[:], w_raw[:], 0.0, None, ALU.is_lt).then_inc(signed, 1)
                dve.wait_ge(signed, 1)
                dve.scalar_tensor_tensor(out=sign_w[:], in0=w_raw[:], scalar=0.0, in1=neg[:],
                                         op0=ALU.is_gt, op1=ALU.subtract).then_inc(signed, 1)
                dve.wait_ge(x_in_sem, 16 * G)
                with dve.Fori(0, G) as g:
                    x = k.x[:, ds(g * GT, GT), :]
                    dve.tensor_reduce(total[:], x, AX.X, ALU.add).then_inc(summed, 1)
                    dve.wait_ge(summed, g + 1)
                    dve.tensor_scalar(mean[:], total[:], 1.0 / D, None, ALU.mult).then_inc(averaged, 1)
                    dve.wait_ge(averaged, g + 1)
                    dve.wait_ge(turned, g)
                    dve.tensor_tensor(pos[:], x, mean[:, :, None].to_broadcast([P, GT, D]), ALU.is_gt).then_inc(positive, 1)
                    dve.wait_ge(multiplied, g + 1)
                    dve.tensor_copy(k.xw[:, ds(g * GT, GT), :], xw_ps[:]).then_inc(xw_out, 1)

            @block.tensor
            def _(pe):
                pe.wait_ge(consts, 6)
                pe.wait_ge(signed, 2)
                with pe.Fori(0, G) as g:
                    pe.wait_ge(positive, g + 1)
                    for t in range(GT):
                        for d in range(DC):
                            m = pe.transpose(t_ps[:, d, t * P:(t + 1) * P], pos[:, t, d * P:(d + 1) * P], k.identb[:])
                    m.then_inc(turned, 1)
                    pe.wait_ge(turned_out, g + 1)
                    pe.wait_ge(xw_out, g)
                    for t in range(GT):
                        for d in range(DC):
                            m = pe.matmul(xw_ps[:, t, :], pos_t[:, d, t * P:(t + 1) * P], sign_w[:, d, :],
                                          start=(d == 0 and t % 2 == 0), stop=(d == DC - 1), skip_group_check=True)
                    m.then_inc(multiplied, 1)

            @block.scalar
            def _(act):
                with act.Fori(0, G) as g:
                    act.wait_ge(turned, g + 1)
                    act.wait_ge(multiplied, g)
                    act.activation(pos_t[:], t_ps[:], ACT.Copy).then_inc(turned_out, 1)


def gnn(k, name, graph, features, finish, sum_degrees, fill=None):
    nc = k.nc
    passes = [(f, part) for f in range(len(features)) for part in range(2) if f + part < 2]
    with ExitStack() as c:
        sb = lambda n, s, d: c.enter_context(nc.sbuf_tensor(f"{name}_{n}", s, d))
        ps = lambda n, s, d: c.enter_context(nc.psum_tensor(f"{name}_{n}", s, d))
        sem = lambda n: k.sem(f"{name}_{n}")
        raw = sb("raw", [P, RAW, JS, QW], F32)
        high = sb("high", [P, 2, JS, QW], F32R)
        low = sb("low", [P, 2, JS, QW], F32R)
        out_t = sb("out_t", [P, DC, QW], F32)
        sums = sb("sums", [P, NT, NQ], F32) if sum_degrees else None
        junk = sb("junk", [P, 2, JS, QW], BF16) if sum_degrees else None
        if fill is not None:
            zero = sb("zero", [P, 12 * D], F32)
        acc = ps("acc", [P, 2, 4, 512], F32)
        loaded = [sem(f"loaded{s}") for s in range(RAW)]
        summed, low_done, multiplied = sem("summed"), sem("low_done"), sem("multiplied")
        high_done, taken, turned, finished = sem("high_done"), sem("taken"), sem("turned"), sem("finished")
        halfway, zero_set, zero_stored = sem("halfway"), sem("zero_set"), sem("zero_stored")

        with nc.Block() as block:
            @block.sync
            def _(sp):
                with sp.Fori(0, NQ) as q, sp.Fori(0, GR) as g:
                    for s in range(RAW):
                        sp.wait_ge(low_done, (q * GR + g) * RAW + (s + 1))
                        if sum_degrees:
                            sp.wait_ge(summed, (q * GR + g) * RAW + (s + 1))
                        sp.dma_start(raw[:, s, :, :],
                                     graph.rearrange("(j p) i -> p j i", p=P)[:, ds((g * RAW + s) * JS, JS), ds(q * QW, QW)]
                                     ).then_inc(loaded[s], 16)

            @block.scalar
            def _(act):
                if sum_degrees:
                    act.sem_inc(summed, RAW)
                for q in range(NQ):
                    with act.Fori(0, GR) as g:
                        for s in range(RAW):
                            act.wait_ge(loaded[s], (g + (q * GR + 1)) * 16)
                            act.wait_ge(multiplied, g * RAW + (q * STEPS + s + 1))
                            act.activation(high[:, s % 2, :, :], raw[:, s, :, :], ACT.Copy).then_inc(high_done, 1)
                            if sum_degrees:
                                act.wait_ge(summed, g * RAW + (q * STEPS + s + RAW - 1))
                                for j in range(JS):
                                    act.activation(junk[:, s % 2, j, :], raw[:, s, j, :], ACT.Copy,
                                                   accum_out=sums[:, ds(g * (RAW * JS) + (s * JS + j), 1), q]).then_inc(summed if j else halfway, 1)

            @block.vector
            def _(dve):
                dve.sem_inc(low_done, RAW)

                def take_quarter(q):
                    dve.wait_ge(multiplied, 2 + (q + 1) * STEPS)
                    if q:
                        dve.wait_ge(turned, q)
                    half = acc[:, q % 2, :, :].rearrange("p (d b) n -> p d (b n)", d=DC)
                    if sum_degrees:
                        dve.tensor_scalar(out_t[:], half, 0.0, None, ALU.max).then_inc(taken, 1)
                    else:
                        dve.tensor_copy(out_t[:], half).then_inc(taken, 1)

                def finish_quarter(q):
                    dve.wait_ge(turned, q + 1)
                    finish(dve, q, acc[:, q % 2, :, :].rearrange("p b (t d) -> p (b t) d", d=D), finished)

                def low_parts(q, g, s, n):
                    dve.wait_ge(high_done, n + 1)
                    m = dve.tensor_tensor(low[:, s % 2, :, :], raw[:, s, :, :], high[:, s % 2, :, :].bitcast(F32), ALU.subtract)
                    m.then_inc(low_done, 1)

                for q in range(NQ):
                    if q:
                        for g, then in ((0, take_quarter), (1, finish_quarter)):
                            for s in range(RAW):
                                low_parts(q, g, s, g * RAW + q * STEPS + s)
                            then(q - 1)
                    with dve.Fori(2 if q else 0, GR) as g:
                        for s in range(RAW):
                            low_parts(q, g, s, g * RAW + (q * STEPS + s))
                take_quarter(NQ - 1)
                finish_quarter(NQ - 1)
                if sum_degrees:
                    dve.wait_ge(summed, RAW + NQ * STEPS)
                    dve.wait_ge(halfway, NQ * STEPS)
                    dve.tensor_reduce(k.deg[:], sums[:], AX.X, ALU.add).then_inc(finished, 1)

            @block.tensor
            def _(pe):
                def turn_back(q):
                    pe.wait_ge(taken, q + 1)
                    rows = acc[:, q % 2, :, :].rearrange("p b (t d) -> p (b t) d", d=D)
                    for t in range(GT):
                        for d in range(DC):
                            m = pe.transpose(rows[:, t, d * P:(d + 1) * P], out_t[:, d, t * P:(t + 1) * P], k.ident[:])
                    m.then_inc(turned, 1)

                pe.sem_inc(multiplied, 2)
                for q in range(NQ):
                    if q >= 2:
                        pe.wait_ge(finished, q - 1)
                    for n in range(STEPS):
                        pe.wait_ge(low_done, RAW + q * STEPS + n + 1)
                        for j in range(JS):
                            for d in range(DC):
                                for i, (f, part) in enumerate(passes):
                                    graph_part = (high, low)[part]
                                    for b in range(2):
                                        m = pe.matmul(acc[:, q % 2, d * 2 + b, :],
                                                      features[f][:, n * JS + j, d * P:(d + 1) * P],
                                                      graph_part[:, n % 2, j, b * 512:(b + 1) * 512],
                                                      start=(n == 0 and j == 0 and i == 0),
                                                      stop=(n == STEPS - 1 and j == JS - 1 and i == len(passes) - 1),
                                                      skip_group_check=True)
                        m.then_inc(multiplied, 1)
                        if n == 5 and q:
                            turn_back(q - 1)
                turn_back(NQ - 1)

            @block.gpsimd
            def _(pool):
                if fill is not None:
                    pool.memset(zero[:], 0.0).then_inc(zero_set, 1)
                    pool.wait_ge(zero_set, 1)
                    n = 0
                    for target in fill:
                        rows = target.shape[0]
                        while rows:
                            r = min(rows // P, 12)
                            pool.dma_start(target[target.shape[0] - rows:target.shape[0] - rows + r * P, :].rearrange("(p r) d -> p (r d)", p=P),
                                           zero[:, 0:r * D]).then_inc(zero_stored, 16)
                            rows -= r * P
                            n += 1
                    pool.wait_ge(zero_stored, 16 * n)


def spreads(k, name):
    nc = k.nc
    with ExitStack() as c:
        sb = lambda n, s, d: c.enter_context(nc.sbuf_tensor(f"{name}_{n}", s, d))
        sem = lambda n: k.sem(f"{name}_{n}")
        neg, squares, junk, var = sb("neg", [P, NT], F32), sb("squares", [P, NT], F32), sb("junk", [P, 4, D], F32), sb("var", [P, NT], F32)
        summed, averaged, squared, scaled, rooted = sem("summed"), sem("averaged"), sem("squared"), sem("scaled"), sem("rooted")
        with nc.Block() as block:
            @block.vector
            def _(dve):
                for g in range(NQ):
                    dve.tensor_reduce(k.mean[:, g * GT:(g + 1) * GT], k.x[:, g * GT:(g + 1) * GT, :], AX.X, ALU.add).then_inc(summed, 1)
                dve.wait_ge(summed, NQ)
                dve.tensor_scalar(neg[:], k.mean[:], -1.0 / D, None, ALU.mult).then_inc(averaged, 1)
                dve.wait_ge(averaged, 1)
                dve.tensor_scalar(k.mean[:], neg[:], -1.0, None, ALU.mult).then_inc(averaged, 1)
                dve.wait_ge(squared, 4 + NT)
                dve.tensor_scalar(var[:], squares[:], 1.0 / D, EPS, ALU.mult, ALU.add).then_inc(scaled, 1)

            @block.scalar
            def _(act):
                act.wait_ge(averaged, 1)
                act.sem_inc(squared, 4)
                with act.Fori(0, NT // 4) as it:
                    for s in range(4):
                        act.wait_ge(squared, it * 4 + (s + 1))
                        act.sem_inc(k.passed, 1)
                        act.activation(junk[:, s, :], k.x[:, it * 4 + s, :], ACT.Square, bias=neg[:, ds(it * 4 + s, 1)],
                                       accum_out=squares[:, ds(it * 4 + s, 1)]).then_inc(squared, 1)

            @block.gpsimd
            def _(pool):
                pool.wait_ge(scaled, 1)
                pool.tensor_tensor(k.rstd[:], var[:], k.minus_half[:], ALU.pow).then_inc(rooted, 1)


def route0(k, router_t, bias, shared, xs0, y0):
    nc = k.nc
    GTR = 4
    TOK = GTR * P
    KG = K0 * GTR
    with ExitStack() as c:
        sb = lambda n, s, d: c.enter_context(nc.sbuf_tensor(f"p3_{n}", s, d))
        ps = lambda n, s, d: c.enter_context(nc.psum_tensor(f"p3_{n}", s, d))
        sem = lambda n: k.sem(f"p3_{n}")
        wr = sb("wr", [P, DC, E0], F32)
        bias_sb = sb("bias", [P, E0], F32)
        wsh = sb("wsh", [P, 2, 3 * D], F32)
        zrow = sb("zrow", [P, D], F32)
        xn = sb("xn", [P, 2, GTR, D], F32)
        xt = sb("xt", [P, 2, DC, TOK], F32)
        logits = sb("logits", [P, NT, E0], F32)
        lg = sb("lg", [P, GTR, E0], F32)
        top = sb("top", [P, GTR, 8], F32)
        topi = sb("topi", [P, GTR, 8], U32)
        tops = sb("tops", [P, NT, K0], F32)
        idx = sb("idx", [P, K0, GTR], F32)
        onehot = sb("onehot", [P, K0, GTR, E0], F32)
        prod = sb("prod", [P, K0, GTR, E0], F32)
        mask = sb("mask", [P, GTR, E0], BF16)
        before = sb("before", [P, GTR + 1, E0], BF16)
        rank = sb("rank", [P, K0, GTR], F32)
        slot = sb("slot", [P, K0, GTR], F32)
        full = sb("full", [P, K0, GTR], F32)
        slot_i = sb("slot_i", [P, 2, K0, GTR], U32)
        sg = sb("sg", [P, 2, TOK], F32)
        hid = sb("hid", [P, 2, TOK], F32)
        es = sb("es", [P, NT, E0], F32)
        z = sb("z", [P, NT], F32)
        t_ps, lg_ps, rank_ps = ps("t_ps", [P, DC, TOK], F32), ps("lg_ps", [P, 512], F32), ps("rank_ps", [P, 512], F32)
        gate_ps, up_ps, down_ps = ps("gate_ps", [P, TOK], F32), ps("up_ps", [P, TOK], F32), ps("down_ps", [P, GTR, D], F32)
        lgv = lg_ps[:, 0:GTR * E0].rearrange("p (t e) -> p t e", e=E0)
        rkv = rank_ps[:, 0:GTR * E0].rearrange("p (t e) -> p t e", e=E0)
        w_loaded, zeroed, zero_out = sem("w_loaded"), sem("zeroed"), sem("zero_out")
        normed, turned, xt_out, logged, ranked, scored = sem("normed"), sem("turned"), sem("xt_out"), sem("logged"), sem("ranked"), sem("scored")
        gated, lifted, silu_out, hidden, lowered, shared_in = sem("gated"), sem("lifted"), sem("silu_out"), sem("hidden"), sem("lowered"), sem("shared_in")
        chain, maxed, masked, slotted, scattered = sem("chain"), sem("maxed"), sem("masked"), sem("slotted"), [sem("scattered0"), sem("scattered1")]
        shifted, exped = sem("shifted"), sem("exped")
        NG = NT // GTR
        LINKS = 9 + GTR
        MASKED = 5 + GTR

        with nc.Block() as block:
            @block.sync
            def _(sp):
                sp.dma_start(wr[:], router_t.rearrange("(c p) e -> p c e", p=P)).then_inc(w_loaded, 16)
                sp.dma_start(bias_sb[:], bias.rearrange("(a e) -> a e", a=1).to_broadcast([P, E0])).then_inc(w_loaded, 16)
                sp.dma_start(wsh[:], shared.rearrange("s p n -> p s n")).then_inc(w_loaded, 16)
                sp.wait_ge(zeroed, 1)
                sp.dma_start(y0[SLOTS0:SLOTS0 + P, :], zrow[:]).then_inc(zero_out, 16)
                sp.wait_ge(zero_out, 16)

            @block.vector
            def _(dve):
                dve.memset(zrow[:], 0.0).then_inc(zeroed, 1)
                dve.memset(before[:, GTR, :], 0.0).then_inc(zeroed, 1)
                dve.wait_ge(zeroed, 2)
                dve.wait_ge(w_loaded, 48)
                with dve.Fori(0, NG // 2) as it:
                    for s in range(2):
                        n = it * 2 + s
                        links = n * LINKS
                        count = 0

                        def link(ins):
                            nonlocal count
                            count += 1
                            ins.then_inc(chain, 1)
                            dve.wait_ge(chain, links + count)

                        wait_apart(dve, scattered[s], it * (16 * KG), k.passed)
                        for t in range(GTR):
                            tile = n * GTR + t
                            dve.tensor_scalar(xn[:, s, t, :], k.x[:, tile, :], k.mean[:, ds(tile, 1)], k.rstd[:, ds(tile, 1)],
                                              ALU.subtract, ALU.mult).then_inc(normed, 1)
                        dve.wait_ge(logged, n + 1)
                        link(dve.tensor_tensor(lg[:], lgv, bias_sb[:, None, :].to_broadcast([P, GTR, E0]), ALU.add))
                        dve.tensor_copy(logits[:, ds(n * GTR, GTR), :], lg[:]).then_inc(scored, 1)
                        for t in range(GTR):
                            m = dve.max(top[:, t, :], lg[:, t, :])
                            m.then_inc(maxed, 1)
                        wait_apart(dve, maxed, n * (2 * GTR) + GTR, k.passed)
                        for t in range(GTR):
                            dve.max_index(topi[:, t, :], top[:, t, :], lg[:, t, :]).then_inc(maxed, 1)
                        dve.tensor_copy(tops[:, ds(n * GTR, GTR), :], top[:, :, 0:K0]).then_inc(scored, 1)
                        dve.wait_ge(maxed, (n + 1) * (2 * GTR))
                        link(dve.tensor_copy(idx[:], topi[:, :, 0:K0].rearrange("p t k -> p k t")))
                        link(dve.tensor_tensor(onehot[:], k.iota[:, None, None, :].to_broadcast([P, K0, GTR, E0]),
                                               idx[:, :, :, None].to_broadcast([P, K0, GTR, E0]), ALU.is_equal))
                        with nc.allow_low_precision(reason="zeros and ones are exact"):
                            link(dve.tensor_reduce(mask[:], onehot[:].rearrange("p k t e -> p t e k"), AX.X, ALU.add))
                        link(dve.tensor_copy(before[:, 0, :], before[:, GTR, :]))
                        for t in range(GTR):
                            link(dve.tensor_tensor(before[:, t + 1, :], before[:, t, :], mask[:, t, :], ALU.add))
                        assert count == MASKED
                        dve.wait_ge(ranked, n + 1)
                        link(dve.tensor_tensor(prod[:], onehot[:], rkv[:, None, :, :].to_broadcast([P, K0, GTR, E0]), ALU.mult))
                        link(dve.tensor_reduce(rank[:], prod[:], AX.X, ALU.add))
                        dve.tensor_scalar(full[:], rank[:], float(CAP), float(SKIP), ALU.is_ge, ALU.mult).then_inc(chain, 1)
                        link(dve.scalar_tensor_tensor(out=slot[:], in0=idx[:], scalar=float(CAP), in1=rank[:], op0=ALU.mult, op1=ALU.add))
                        assert count == LINKS - 1
                        dve.wait_ge(chain, links + LINKS)
                        dve.tensor_tensor(slot[:], slot[:], full[:], ALU.add).then_inc(slotted, 1)
                        dve.wait_ge(slotted, n * 3 + 1)
                        dve.tensor_copy(slot_i[:, s, :, :], slot[:]).then_inc(slotted, 1)
                        dve.tensor_scalar(k.slots0[:, ds(n * GTR, GTR), :].rearrange("p t k -> p k t"), slot[:], float(SLOTS0), None, ALU.min).then_inc(slotted, 1)
                        for h in range(2):
                            dve.wait_ge(silu_out, n * 2 + h + 1)
                            dve.wait_ge(lowered, n)
                            dve.tensor_tensor(hid[:, h, :], sg[:, h, :], up_ps[:], ALU.mult).then_inc(hidden, 1)
                        dve.wait_ge(lowered, n + 1)
                        dve.scalar_tensor_tensor(out=k.x[:, ds(n * GTR, GTR), :], in0=down_ps[:], scalar=0.5, in1=k.x[:, ds(n * GTR, GTR), :],
                                                 op0=ALU.mult, op1=ALU.add).then_inc(shared_in, 1)
                link_n = NG * LINKS

                def link2(ins):
                    nonlocal link_n
                    link_n += 1
                    ins.then_inc(chain, 1)
                    dve.wait_ge(chain, link_n)

                dve.wait_ge(scored, 2 * NG)
                first = tops[:, :, 0:1]
                link2(dve.tensor_tensor(logits[:], logits[:], first.to_broadcast([P, NT, E0]), ALU.subtract))
                dve.tensor_tensor(k.gates0[:], tops[:], first.to_broadcast([P, NT, K0]), ALU.subtract).then_inc(shifted, 1)
                dve.wait_ge(exped, 2)
                link2(dve.tensor_reduce(z[:], es[:], AX.X, ALU.add))
                link2(dve.reciprocal(z[:], z[:]))
                link2(dve.tensor_tensor(k.gates0[:], k.gates0[:], z[:, :, None].to_broadcast([P, NT, K0]), ALU.mult))
                link2(dve.tensor_reduce(z[:], k.gates0[:], AX.X, ALU.add))
                link2(dve.tensor_scalar(z[:], z[:], 1e-9, None, ALU.add))
                link2(dve.reciprocal(z[:], z[:]))
                link2(dve.tensor_tensor(k.gates0[:], k.gates0[:], z[:, :, None].to_broadcast([P, NT, K0]), ALU.mult))

            @block.scalar
            def _(act):
                with act.Fori(0, NG // 2) as it:
                    for s in range(2):
                        n = it * 2 + s
                        act.wait_ge(turned, n + 1)
                        act.activation(xt[:, s, :, :], t_ps[:], ACT.Copy).then_inc(xt_out, 1)
                        for h in range(2):
                            act.wait_ge(gated, n * 2 + h + 1)
                            act.wait_ge(hidden, n * 2)
                            act.activation(sg[:, h, :], gate_ps[:], ACT.Silu).then_inc(silu_out, 1)
                act.wait_ge(shifted, 1)
                act.activation(es[:], logits[:], ACT.Exp).then_inc(exped, 1)
                act.activation(k.gates0[:], k.gates0[:], ACT.Exp).then_inc(exped, 1)

            @block.tensor
            def _(pe):
                pe.wait_ge(w_loaded, 48)
                with pe.Fori(0, NG // 2) as it:
                    for s in range(2):
                        n = it * 2 + s
                        pe.wait_ge(normed, (n + 1) * GTR)
                        pe.wait_ge(xt_out, n)
                        for t in range(GTR):
                            for d in range(DC):
                                m = pe.transpose(t_ps[:, d, t * P:(t + 1) * P], xn[:, s, t, d * P:(d + 1) * P], k.ident[:])
                        m.then_inc(turned, 1)
                        pe.wait_ge(xt_out, n + 1)
                        pe.wait_ge(scored, n * 2)
                        for t in range(GTR):
                            for d in range(DC):
                                m = pe.matmul(lgv[:, t, :], xt[:, s, d, t * P:(t + 1) * P], wr[:, d, :],
                                              start=(t == 0 and d == 0), stop=(d == DC - 1), skip_group_check=True)
                        m.then_inc(logged, 1)
                        for h in range(2):
                            pe.wait_ge(hidden, n * 2 + h)
                            for (out, at) in ((gate_ps, 0), (up_ps, DC * F0)):
                                for d in range(DC):
                                    m = pe.matmul(out[:], wsh[:, h, at + d * F0:at + (d + 1) * F0], xt[:, s, d, :],
                                                  start=(d == 0), stop=(d == DC - 1))
                            m.then_inc(gated, 1)
                            if h:
                                continue
                            pe.wait_ge(chain, n * LINKS + MASKED)
                            pe.wait_ge(slotted, n * 3)
                            pe.matmul(rank_ps[:, 0:GTR * E0], k.tri[:], mask[:].rearrange("p t e -> p (t e)"), start=True, stop=False)
                            pe.matmul(rank_ps[:, 0:GTR * E0], k.onesb[:], before[:, 0:GTR, :].rearrange("p t e -> p (t e)"),
                                      start=False, stop=True).then_inc(ranked, 1)
                        pe.wait_ge(hidden, n * 2 + 2)
                        pe.wait_ge(shared_in, n)
                        for t in range(GTR):
                            for h in range(2):
                                m = pe.matmul(down_ps[:, t, :], hid[:, h, t * P:(t + 1) * P], wsh[:, h, 2 * DC * F0:],
                                              start=(h == 0 and t % 2 == 0), stop=(h == 1), skip_group_check=True)
                        m.then_inc(lowered, 1)

            @block.gpsimd
            def _(pool):
                with pool.Fori(0, NG // 2) as it:
                    for s in range(2):
                        n = it * 2 + s
                        wait_apart(pool, slotted, (n + 1) * 3, k.passed)
                        for kk in range(K0):
                            for t in range(GTR):
                                pool.indirect_dma_start(xs0, bass.IndirectOffsetOnAxis(ap=slot_i[:, s, kk, t:t + 1], axis=0),
                                                        xn[:, s, t, :], None, bounds_check=SLOTS0 - 1, oob_is_err=False
                                                        ).then_inc(scattered[s], 16)
                for s in range(2):
                    pool.wait_ge(scattered[s], NG // 2 * KG * 16)


UN = 8


def units(eng, total):
    yield 0, 0
    with eng.Fori(0, total // UN - 1) as it:
        for j in range(1, UN):
            yield it, j
        yield it + 1, 0
    for j in range(1, UN):
        yield total // UN - 1, j


def at(r, j):
    return r * UN + j


def moved(r, j, by):
    return r + (j + by) // UN, (j + by) % UN


def experts0(k, weights, xs0, y0):
    nc = k.nc
    U = 2 * E0
    RH = RPP // 2
    WN = 3 * D
    XR = 4
    with ExitStack() as c:
        sb = lambda n, s, d: c.enter_context(nc.sbuf_tensor(f"p4_{n}", s, d))
        ps = lambda n, s, d: c.enter_context(nc.psum_tensor(f"p4_{n}", s, d))
        sem = lambda n: k.sem(f"p4_{n}")
        xe = sb("xe", [P, XR, RPP, D], F32)
        we = sb("we", [P, XR, WN], F32)
        xt = sb("xt", [P, 2, DC, HALF], F32)
        sg = sb("sg", [P, 2, HALF], F32)
        hid = sb("hid", [P, 2, HALF], F32)
        ye = sb("ye", [P, 4, RH, D], F32)
        t_ps = ps("t_ps", [P, DC, 512], F32)
        gate_ps, up_ps = ps("gate_ps", [P, 2, 512], F32), ps("up_ps", [P, 2, 512], F32)
        down_ps = ps("down_ps", [P, 4, D], F32)
        loaded = [sem(f"loaded{s}") for s in range(XR)]
        stored = [sem(f"stored{s}") for s in range(4)]
        turned, xt_out, lifted, silu_out, hidden, lowered, y_out = [sem(n) for n in ("turned", "xt_out", "lifted", "silu_out", "hidden", "lowered", "y_out")]
        xs_v = xs0.rearrange("(e p r) d -> e p r d", p=P, r=RPP)
        y_v = y0[0:SLOTS0, :].rearrange("(e p r) d -> e p r d", p=P, r=RPP)

        with nc.Block() as block:
            @block.sync
            def _(sp):
                with sp.Fori(0, E0 // XR) as it:
                    for s in range(XR):
                        sp.wait_ge(lowered, it * (2 * XR) + (2 * s + 2))
                        sp.dma_start(xe[:, s, :, :], xs_v[ds(it * XR + s, 1), :, :, :].rearrange("a p r d -> p (a r) d")).then_inc(loaded[s], 16)
                        sp.dma_start(we[:, s, :], weights[ds(it * XR + s, 1), :, :].rearrange("a p n -> p (a n)")).then_inc(loaded[s], 16)

            def last(r, j):
                return isinstance(r, int) and at(r, j) == U - 1

            @block.tensor
            def _(pe):
                pe.sem_inc(lowered, 2 * XR)

                def turn(r, j):
                    e = j // 2
                    if j % 2 == 0:
                        pe.wait_ge(loaded[e], (r + 1) * 32)
                    pe.wait_ge(xt_out, at(r, j))
                    for i in range(RH):
                        for d in range(DC):
                            m = pe.transpose(t_ps[:, d, i * P:(i + 1) * P], xe[:, e, (j % 2) * RH + i, d * P:(d + 1) * P], k.ident[:])
                    m.then_inc(turned, 1)

                def lift(r, j):
                    e = j // 2
                    pe.wait_ge(xt_out, at(r, j) + 1)
                    for out, w0 in ((gate_ps, 0), (up_ps, DC * F0)):
                        for d in range(DC):
                            m = pe.matmul(out[:, j % 2, 0:HALF], we[:, e, w0 + d * F0:w0 + (d + 1) * F0], xt[:, j % 2, d, :],
                                          start=(d == 0), stop=(d == DC - 1))
                    m.then_inc(lifted, 1)

                def lower(r, j):
                    pe.wait_ge(hidden, at(r, j) + 1)
                    pe.wait_ge(y_out, at(r, j))
                    for i in range(RH):
                        m = pe.matmul(down_ps[:, i, :], hid[:, j % 2, i * P:(i + 1) * P], we[:, j // 2, 2 * DC * F0:],
                                      start=(i % 2 == 0), stop=True, skip_group_check=True)
                    m.then_inc(lowered, 1)

                turn(0, 0)
                for r, j in units(pe, U):
                    if not last(r, j):
                        turn(*moved(r, j, 1))
                    lift(r, j)
                    if not (isinstance(r, int) and at(r, j) == 0):
                        lower(*moved(r, j, -1))
                lower(U // UN - 1, UN - 1)

            @block.vector
            def _(dve):
                def take_turned(r, j):
                    dve.wait_ge(turned, at(r, j) + 1)
                    dve.tensor_copy(xt[:, j % 2, :, :], t_ps[:, :, 0:HALF]).then_inc(xt_out, 1)

                def hide(r, j):
                    dve.wait_ge(silu_out, at(r, j) + 1)
                    dve.tensor_tensor(hid[:, j % 2, :], sg[:, j % 2, :], up_ps[:, j % 2, 0:HALF], ALU.mult).then_inc(hidden, 1)

                take_turned(0, 0)
                for r, j in units(dve, U):
                    if not last(r, j):
                        take_turned(*moved(r, j, 1))
                    hide(r, j)

            @block.scalar
            def _(act):
                def take_lowered(r, j):
                    act.wait_ge(lowered, at(r, j) + (2 * XR + 1))
                    act.wait_ge(stored[j % 4], (r * 2 + j // 4) * 16)
                    act.activation(ye[:, j % 4, :, :], down_ps[:, 0:RH, :], ACT.Copy).then_inc(y_out, 1)

                for r, j in units(act, U):
                    act.wait_ge(lifted, at(r, j) + 1)
                    act.activation(sg[:, j % 2, :], gate_ps[:, j % 2, 0:HALF], ACT.Silu).then_inc(silu_out, 1)
                    if not (isinstance(r, int) and at(r, j) == 0):
                        take_lowered(*moved(r, j, -1))
                take_lowered(U // UN - 1, UN - 1)

            @block.gpsimd
            def _(pool):
                with pool.Fori(0, U // UN) as it:
                    for j in range(UN):
                        pool.wait_ge(y_out, at(it, j) + 1)
                        pool.sem_inc(k.passed, 1)
                        pool.dma_start(y_v[ds(it * (UN // 2) + j // 2, 1), :, (j % 2) * RH:(j % 2 + 1) * RH, :].rearrange("a p r d -> p (a r) d"),
                                       ye[:, j % 4, :, :]).then_inc(stored[j % 4], 16)
                for s in range(4):
                    pool.wait_ge(stored[s], U // 4 * 16)


def combine(k, name, y, slots, gates, kn, bias=None, out=None):
    nc = k.nc
    R = 4
    with ExitStack() as c:
        sb = lambda n, s, d: c.enter_context(nc.sbuf_tensor(f"{name}_{n}", s, d))
        sem = lambda n: k.sem(f"{name}_{n}")
        rows = sb("rows", [P, R, kn, D], F32)
        at_i = sb("at", [P, R, kn], U32)
        copied, added, stored = sem("copied"), sem("added"), sem("stored")
        gathered = [sem(f"gathered{s}") for s in range(R)]
        with nc.Block() as block:
            @block.gpsimd
            def _(pool):
                with pool.Fori(0, NT // R) as it:
                    for s in range(R):
                        n = it * R + s
                        wait_apart(pool, added, n * kn + kn, k.passed)
                        pool.tensor_copy(at_i[:, s, :], slots[:, n, :]).then_inc(copied, 1)
                        wait_apart(pool, copied, n + 1, k.passed)
                        for i in range(kn):
                            pool.indirect_dma_start(rows[:, s, i, :], None, y, bass.IndirectOffsetOnAxis(ap=at_i[:, s, i:i + 1], axis=0)
                                                    ).then_inc(gathered[s], 16)

            @block.vector
            def _(dve):
                dve.sem_inc(added, R * kn)
                with dve.Fori(0, NT // R) as it:
                    for s in range(R):
                        n = it * R + s
                        dve.wait_ge(gathered[s], (it + 1) * (16 * kn))
                        for i in range(kn):
                            if i:
                                dve.wait_ge(added, n * kn + (R * kn + i))
                            dve.scalar_tensor_tensor(out=k.x[:, n, :], in0=rows[:, s, i, :], scalar=gates[:, n, i:i + 1], in1=k.x[:, n, :],
                                                     op0=ALU.mult, op1=ALU.add).then_inc(added, 1)

            @block.sync
            def _(sp):
                if out is not None:
                    with sp.Fori(0, NT // R) as it:
                        sp.wait_ge(added, (it + 1) * (R * kn) + R * kn)
                        sp.dma_start(out.rearrange("(t p) d -> p t d", p=P)[:, ds(it * R, R), :], k.x[:, ds(it * R, R), :]).then_inc(stored, 16)
                    sp.wait_ge(stored, NT // R * 16)


def project(k, weight, bias):
    nc = k.nc
    GTR = 4
    NG = NT // GTR
    with ExitStack() as c:
        sb = lambda n, s, d: c.enter_context(nc.sbuf_tensor(f"p5b_{n}", s, d))
        ps = lambda n, s, d: c.enter_context(nc.psum_tensor(f"p5b_{n}", s, d))
        sem = lambda n: k.sem(f"p5b_{n}")
        w = sb("w", [P, DC, D], F32)
        b = sb("b", [P, D], F32)
        xn = sb("xn", [P, 2, GTR, D], F32)
        xt = sb("xt", [P, 2, DC, GTR * P], F32)
        g32 = sb("g32", [P, 2, GTR, D], F32)
        t_ps = ps("t_ps", [P, 2, DC, GTR * P], F32)
        h_ps = ps("h_ps", [P, 2, GTR, D], F32)
        loaded, normed, turned, xt_out, made, scaled, high, low, biased, rooted = [
            sem(n) for n in ("loaded", "normed", "turned", "xt_out", "made", "scaled", "high", "low", "biased", "rooted")]
        with nc.Block() as block:
            @block.sync
            def _(sp):
                sp.dma_start(w[:], weight.rearrange("(c p) o -> p c o", p=P)).then_inc(loaded, 16)
                sp.dma_start(b[:], bias.rearrange("(a e) -> a e", a=1).to_broadcast([P, D])).then_inc(loaded, 16)

            @block.gpsimd
            def _(pool):
                pool.tensor_tensor(k.dinv[:], k.deg[:], k.minus_half[:], ALU.pow).then_inc(rooted, 1)

            @block.vector
            def _(dve):
                dve.wait_ge(loaded, 32)
                dve.wait_ge(rooted, 1)
                with dve.Fori(0, NG // 2) as it:
                    for s in range(2):
                        n = it * 2 + s
                        dve.wait_ge(turned, n)
                        for t in range(GTR):
                            tile = n * GTR + t
                            dve.tensor_scalar(xn[:, s, t, :], k.x[:, tile, :], k.mean[:, ds(tile, 1)], k.rstd[:, ds(tile, 1)],
                                              ALU.subtract, ALU.mult).then_inc(normed, 1)
                        dve.wait_ge(normed, (n + 1) * GTR)
                        dve.tensor_tensor(k.x[:, ds(n * GTR, GTR), :], k.x[:, ds(n * GTR, GTR), :],
                                          b[:, None, :].to_broadcast([P, GTR, D]), ALU.add).then_inc(biased, 1)
                        dve.wait_ge(made, n + 1)
                        dve.tensor_tensor(g32[:, s, :, :], h_ps[:, s, :, :], k.dinv[:, ds(n * GTR, GTR), None].to_broadcast([P, GTR, D]),
                                          ALU.mult).then_inc(scaled, 1)
                        dve.wait_ge(high, n + 1)
                        dve.tensor_tensor(k.g_low[:, ds(n * GTR, GTR), :], g32[:, s, :, :], k.g_high[:, ds(n * GTR, GTR), :].bitcast(F32),
                                          ALU.subtract).then_inc(low, 1)

            @block.scalar
            def _(act):
                with act.Fori(0, NG // 2) as it:
                    for s in range(2):
                        n = it * 2 + s
                        act.wait_ge(turned, n + 1)
                        act.activation(xt[:, s, :, :], t_ps[:, s, :, :], ACT.Copy).then_inc(xt_out, 1)
                        wait_apart(act, scaled, n + 1, k.passed)
                        act.activation(k.g_high[:, ds(n * GTR, GTR), :], g32[:, s, :, :], ACT.Copy).then_inc(high, 1)

            @block.tensor
            def _(pe):
                pe.wait_ge(loaded, 32)
                with pe.Fori(0, NG // 2) as it:
                    for s in range(2):
                        n = it * 2 + s
                        pe.wait_ge(normed, (n + 1) * GTR)
                        for t in range(GTR):
                            for d in range(DC):
                                m = pe.transpose(t_ps[:, s, d, t * P:(t + 1) * P], xn[:, s, t, d * P:(d + 1) * P], k.ident[:])
                        m.then_inc(turned, 1)
                        pe.wait_ge(xt_out, n + 1)
                        for t in range(GTR):
                            for d in range(DC):
                                m = pe.matmul(h_ps[:, s, t, :], xt[:, s, d, t * P:(t + 1) * P], w[:, d, :],
                                              start=(d == 0 and t % 2 == 0), stop=(d == DC - 1), skip_group_check=True)
                        m.then_inc(made, 1)


def route1(k, router, bias, xs1):
    nc = k.nc
    GTR = 4
    NG = NT // GTR
    with ExitStack() as c:
        sb = lambda n, s, d: c.enter_context(nc.sbuf_tensor(f"p7_{n}", s, d))
        ps = lambda n, s, d: c.enter_context(nc.psum_tensor(f"p7_{n}", s, d))
        sem = lambda n: k.sem(f"p7_{n}")
        wr = sb("wr", [P, DC, E1], F32)
        bias_sb = sb("bias", [P, E1], F32)
        xn = sb("xn", [P, NT, D], F32)
        xt = sb("xt", [P, 2, DC, GTR * P], F32)
        logits = sb("logits", [P, NT, E1], F32)
        top = sb("top", [P, NT, 8], F32)
        topi = sb("topi", [P, NT, 8], U32)
        idx = sb("idx", [P, NT, K1], F32)
        onehot = sb("onehot", [P, K1, NT, E1], F32)
        prod = sb("prod", [P, K1, NT, E1], F32)
        mask = sb("mask", [P, NT, E1], BF16)
        prefix = [sb(f"prefix{i}", [P, NT + 1, E1], BF16) for i in range(2)]
        count = sb("count", [P, E1], F32)
        count_i = sb("count_i", [P, E1], I32)
        tiles_i = sb("tiles_i", [P, E1], I32)
        ends = [sb(f"ends{i}", [P, E1 + 1], F32) for i in range(2)]
        ordinal = sb("ordinal", [P, NT1], F32)
        beyond = sb("beyond", [P, NT1, E1], F32)
        owner = sb("owner", [P, NT1], F32)
        base = sb("base", [P, E1], F32)
        place = sb("place", [P, NT, E1], F32)
        slot = sb("slot", [P, NT, K1], F32)
        z = sb("z", [P, NT], F32)
        t_ps = ps("t_ps", [P, 2, DC, GTR * P], F32)
        lg_ps = ps("lg_ps", [P, 2, 512], F32)
        rank_ps, count_ps = ps("rank_ps", [P, 512], F32), ps("count_ps", [P, 512], F32)
        loaded, normed, turned, xt_out, logged, scored = [sem(n) for n in ("loaded", "normed", "turned", "xt_out", "logged", "scored")]
        chain, masked, ranked, placed, scattered, numbered, shifted, exped = [
            sem(n) for n in ("chain", "masked", "ranked", "placed", "scattered", "numbered", "shifted", "exped")]
        with nc.Block() as block:
            MASKED = 2 * NT + 1 + K1 + 5 + 1 + 2 * 5

            @block.sync
            def _(sp):
                sp.dma_start(wr[:], router.rearrange("(c p) e -> p c e", p=P)).then_inc(loaded, 16)
                sp.dma_start(bias_sb[:], bias.rearrange("(a e) -> a e", a=1).to_broadcast([P, E1])).then_inc(loaded, 16)

            @block.scalar
            def _(act):
                with act.Fori(0, NG // 2) as it:
                    for s in range(2):
                        n = it * 2 + s
                        act.wait_ge(turned, n + 1)
                        act.activation(xt[:, s, :, :], t_ps[:, s, :, :], ACT.Copy).then_inc(xt_out, 1)
                act.wait_ge(shifted, 1)
                act.activation(k.gates1[:], k.gates1[:], ACT.Exp).then_inc(exped, 1)

            @block.tensor
            def _(pe):
                pe.wait_ge(loaded, 32)
                with pe.Fori(0, NG // 2) as it:
                    for s in range(2):
                        n = it * 2 + s
                        pe.wait_ge(normed, (n + 1) * GTR)
                        for t in range(GTR):
                            for d in range(DC):
                                m = pe.transpose(t_ps[:, s, d, t * P:(t + 1) * P], k.xring[:, s, t, d * P:(d + 1) * P], k.ident[:])
                        m.then_inc(turned, 1)
                        pe.wait_ge(xt_out, n + 1)
                        for t in range(GTR):
                            for d in range(DC):
                                m = pe.matmul(lg_ps[:, s, t * E1:(t + 1) * E1], xt[:, s, d, t * P:(t + 1) * P], wr[:, d, :],
                                              start=(t == 0 and d == 0), stop=(d == DC - 1), skip_group_check=True)
                        m.then_inc(logged, 1)
                pe.wait_ge(chain, MASKED)
                flat = lambda a: a.rearrange("p t e -> p (t e)")
                pe.matmul(rank_ps[:, 0:NT * E1], k.tri[:], flat(mask[:]), start=True, stop=False)
                pe.matmul(rank_ps[:, 0:NT * E1], k.onesb[:], flat(prefix[1][:, 0:NT, :]), start=False, stop=True).then_inc(ranked, 1)
                pe.matmul(count_ps[:, 0:E1], k.onesb[:], prefix[1][:, NT, :], start=True, stop=True).then_inc(ranked, 1)

            @block.vector
            def _(dve):
                dve.wait_ge(loaded, 32)
                with dve.Fori(0, NG // 2) as it:
                    for s in range(2):
                        n = it * 2 + s
                        dve.wait_ge(turned, n)
                        for t in range(GTR):
                            tile = n * GTR + t
                            dve.tensor_scalar(k.xring[:, s, t, :], k.x[:, tile, :], k.mean[:, ds(tile, 1)], k.rstd[:, ds(tile, 1)],
                                              ALU.subtract, ALU.mult).then_inc(normed, 1)
                        dve.wait_ge(normed, (n + 1) * GTR)
                        dve.tensor_copy(xn[:, ds(n * GTR, GTR), :], k.xring[:, s, :, :]).then_inc(scored, 1)
                        dve.wait_ge(logged, n + 1)
                        dve.tensor_tensor(logits[:, ds(n * GTR, GTR), :], lg_ps[:, s, 0:GTR * E1].rearrange("p (t e) -> p t e", e=E1),
                                          bias_sb[:, None, :].to_broadcast([P, GTR, E1]), ALU.add).then_inc(scored, 1)
                dve.wait_ge(scored, 2 * NG)
                links = 0

                def link(*steps):
                    nonlocal links
                    for step in steps:
                        step.then_inc(chain, 1)
                    links += len(steps)
                    dve.wait_ge(chain, links)

                link(*[dve.max(top[:, t, :], logits[:, t, :]) for t in range(NT)])
                link(*[dve.max_index(topi[:, t, :], top[:, t, :], logits[:, t, :]) for t in range(NT)])
                link(dve.tensor_copy(idx[:], topi[:, :, 0:K1]))
                link(*[dve.tensor_tensor(onehot[:, i, :, :], k.iota[:, None, 0:E1].to_broadcast([P, NT, E1]),
                                         idx[:, :, i:i + 1].to_broadcast([P, NT, E1]), ALU.is_equal) for i in range(K1)])
                link(dve.tensor_tensor(mask[:], onehot[:, 0, :, :], onehot[:, 1, :, :], ALU.add), dve.memset(prefix[0][:, 0:1, :], 0.0),
                     dve.memset(prefix[1][:, 0:1, :], 0.0), dve.memset(ends[0][:, 0:1], 0.0), dve.memset(ends[1][:, 0:1], 0.0))
                link(dve.tensor_copy(prefix[0][:, 1:, :], mask[:]))
                for b in range(5):
                    a, z2, by = prefix[b % 2], prefix[(b + 1) % 2], 1 << b
                    link(dve.tensor_copy(z2[:, 1:1 + by, :], a[:, 1:1 + by, :]),
                         dve.tensor_tensor(z2[:, 1 + by:, :], a[:, 1 + by:, :], a[:, 1:NT + 1 - by, :], ALU.add))
                assert links == MASKED
                dve.wait_ge(ranked, 2)
                link(dve.tensor_scalar(count[:], count_ps[:, 0:E1], float(T1 - 1), None, ALU.add))
                link(dve.tensor_copy(count_i[:], count[:]))
                link(dve.tensor_single_scalar(tiles_i[:], count_i[:], T1.bit_length() - 1, ALU.arith_shift_right))
                link(dve.tensor_copy(ends[0][:, 1:], tiles_i[:]))
                for b in range(3):
                    a, z2, by = ends[b % 2], ends[(b + 1) % 2], 1 << b
                    link(dve.tensor_copy(z2[:, 1:1 + by], a[:, 1:1 + by]),
                         dve.tensor_tensor(z2[:, 1 + by:], a[:, 1 + by:], a[:, 1:E1 + 1 - by], ALU.add))
                end = ends[1]
                dve.wait_ge(numbered, 1)
                link(dve.tensor_tensor(beyond[:], ordinal[:, :, None].to_broadcast([P, NT1, E1]), end[:, None, 1:].to_broadcast([P, NT1, E1]), ALU.is_ge),
                     dve.tensor_scalar(base[:], end[:, 0:E1], float(T1), None, ALU.mult))
                link(dve.tensor_reduce(owner[:], beyond[:], AX.X, ALU.add),
                     dve.tensor_tensor(place[:], rank_ps[:, 0:NT * E1].rearrange("p (t e) -> p t e", e=E1),
                                       base[:, None, :].to_broadcast([P, NT, E1]), ALU.add))
                link(dve.tensor_scalar(owner[:], owner[:], float(E1 - 1), None, ALU.min),
                     dve.tensor_tensor(prod[:], onehot[:], place[:, None, :, :].to_broadcast([P, K1, NT, E1]), ALU.mult))
                link(dve.tensor_copy(k.owner1[:], owner[:]), dve.tensor_reduce(slot[:].rearrange("p t k -> p k t"), prod[:], AX.X, ALU.add))
                dve.tensor_copy(k.slots1[:], slot[:]).then_inc(placed, 1)
                dve.tensor_tensor(k.gates1[:], top[:, :, 0:K1], top[:, :, 0:1].to_broadcast([P, NT, K1]), ALU.subtract).then_inc(shifted, 1)
                dve.wait_ge(exped, 1)
                link(dve.tensor_reduce(z[:], k.gates1[:], AX.X, ALU.add))
                link(dve.reciprocal(z[:], z[:]))
                link(dve.tensor_tensor(k.gates1[:], k.gates1[:], z[:, :, None].to_broadcast([P, NT, K1]), ALU.mult))

            @block.gpsimd
            def _(pool):
                pool.iota(ordinal[:], pattern=[[1, NT1]], base=0, channel_multiplier=0, allow_small_or_imprecise_dtypes=True).then_inc(numbered, 1)
                pool.wait_ge(placed, 1)
                for t in range(NT):
                    for i in range(K1):
                        pool.indirect_dma_start(xs1, bass.IndirectOffsetOnAxis(ap=k.slots1[:, t, i:i + 1], axis=0), xn[:, t, :], None,
                                                bounds_check=SLOTS1 - 1, oob_is_err=False).then_inc(scattered, 16)
                pool.wait_ge(scattered, 16 * NT * K1)


def experts1(k, weights, b1, b2, xs1, y1):
    nc = k.nc
    R = 2
    TR = T1 // P
    WN = DC * F1 + FB1 * D
    with ExitStack() as c:
        sb = lambda n, s, d: c.enter_context(nc.sbuf_tensor(f"p8_{n}", s, d))
        ps = lambda n, s, d: c.enter_context(nc.psum_tensor(f"p8_{n}", s, d))
        sem = lambda n: k.sem(f"p8_{n}")
        w = sb("w", [P, R, WN], F32)
        bias1, bias2 = sb("bias1", [P, R, FB1], F32), sb("bias2", [P, R, D], F32)
        x = sb("x", [P, R, TR, D], F32)
        xt = sb("xt", [P, R, DC, T1], F32)
        h = sb("h", [P, R, FB1, T1], F32)
        y = sb("y", [P, R, TR, D], F32)
        t_ps, h_ps, down_ps = ps("t_ps", [P, DC, T1], F32), ps("h_ps", [P, FB1, T1], F32), ps("down_ps", [P, 2, TR, D], F32)
        loaded, stored = [sem(f"loaded{s}") for s in range(R)], [sem(f"stored{s}") for s in range(R)]
        turned, xt_out, lifted, relu_out, lowered, y_out = [sem(n) for n in ("turned", "xt_out", "lifted", "relu_out", "lowered", "y_out")]
        xs_v = xs1.rearrange("(n p r) d -> n p (r d)", p=P, r=TR)
        y_v = y1.rearrange("(n p r) d -> n p (r d)", p=P, r=TR)
        with nc.Block() as block:
            @block.sync
            def _(sp):
                with sp.Fori(0, NT1 // R) as it:
                    for s in range(R):
                        sp.wait_ge(y_out, it * R + (s + 1))
                        e = sp.value_load(k.owner1[0:1, ds(it * R + s, 1)], min_val=0, max_val=E1 - 1)
                        sp.dma_start(x[:, s, :, :].rearrange("p r d -> p (r d)"), xs_v[ds(it * R + s, 1), :, :].rearrange("a p n -> p (a n)")).then_inc(loaded[s], 16)
                        sp.dma_start(w[:, s, :], weights[ds(e, 1), :, :].rearrange("a p n -> p (a n)")).then_inc(loaded[s], 16)
                        sp.dma_start(bias1[:, s, :], b1[ds(e, 1), :, :].rearrange("a p n -> p (a n)")).then_inc(loaded[s], 16)
                        sp.dma_start(bias2[:, s, :], b2[ds(e, 1), :].to_broadcast([P, D])).then_inc(loaded[s], 16)

            @block.tensor
            def _(pe):
                with pe.Fori(0, NT1 // R) as it:
                    for s in range(R):
                        n = it * R + s
                        pe.wait_ge(loaded[s], (it + 1) * 64)
                        pe.wait_ge(xt_out, n)
                        for r in range(TR):
                            for d in range(DC):
                                m = pe.transpose(t_ps[:, d, r * P:(r + 1) * P], x[:, s, r, d * P:(d + 1) * P], k.ident[:])
                        m.then_inc(turned, 1)
                        pe.wait_ge(xt_out, n + 1)
                        for f in range(FB1):
                            for d in range(DC):
                                m = pe.matmul(h_ps[:, f, :], w[:, s, d * F1 + f * P:d * F1 + (f + 1) * P], xt[:, s, d, :],
                                              start=(d == 0 and f % 2 == 0), stop=(d == DC - 1), skip_group_check=True)
                            if f % 2:
                                m.then_inc(lifted, 1)
                        pe.wait_ge(y_out, n + 1)
                        for f in range(FB1):
                            pe.wait_ge(relu_out, n * FB1 + (f + 1))
                            for r in range(TR):
                                m = pe.matmul(down_ps[:, s, r, :], h[:, s, f, r * P:(r + 1) * P],
                                              w[:, s, DC * F1 + f * D:DC * F1 + (f + 1) * D],
                                              start=(f == 0 and r == 0), stop=(f == FB1 - 1), skip_group_check=True)
                        m.then_inc(lowered, 1)

            @block.scalar
            def _(act):
                with act.Fori(0, NT1 // R) as it:
                    for s in range(R):
                        n = it * R + s
                        for f in range(FB1):
                            act.wait_ge(lifted, n * (FB1 // 2) + (f // 2 + 1))
                            act.activation(h[:, s, f, :], h_ps[:, f, :], ACT.Relu, bias=bias1[:, s, f:f + 1]).then_inc(relu_out, 1)

            @block.vector
            def _(dve):
                dve.sem_inc(y_out, R)
                with dve.Fori(0, NT1 // R) as it:
                    for s in range(R):
                        n = it * R + s
                        dve.wait_ge(turned, n + 1)
                        dve.tensor_copy(xt[:, s, :, :], t_ps[:]).then_inc(xt_out, 1)
                        dve.wait_ge(lowered, n + 1)
                        dve.wait_ge(stored[s], it * 16)
                        dve.tensor_tensor(y[:, s, :, :], down_ps[:, s, :, :], bias2[:, s, None, :].to_broadcast([P, TR, D]), ALU.add).then_inc(y_out, 1)

            @block.gpsimd
            def _(pool):
                with pool.Fori(0, NT1 // R) as it:
                    for s in range(R):
                        wait_apart(pool, y_out, it * R + (R + s + 1), k.passed)
                        pool.dma_start(y_v[ds(it * R + s, 1), :, :].rearrange("a p n -> p (a n)"), y[:, s, :, :].rearrange("p r d -> p (r d)")).then_inc(stored[s], 16)
                for s in range(R):
                    pool.wait_ge(stored[s], NT1 // R * 16)


def build(nc, a, out, stop=99):
    xs0 = nc.dram_tensor("rows0", [SLOTS0, D], F32).ap()
    y0 = nc.dram_tensor("results0", [SLOTS0 + P, D], F32).ap()
    xs1 = nc.dram_tensor("rows1", [SLOTS1, D], F32).ap()
    y1 = nc.dram_tensor("results1", [SLOTS1, D], F32).ap()
    with ExitStack() as ctx:
        k = Kernel(nc, ctx)
        make_constants(k)
        sb = lambda c, n, s, d: c.enter_context(nc.sbuf_tensor(n, s, d))
        k.mean, k.rstd = sb(ctx, "mean", [P, NT], F32), sb(ctx, "rstd", [P, NT], F32)
        with ExitStack() as c:
            k.xw = sb(c, "xw", [P, NT, D], F32R)
            sign_features(k, a["x"], a["gnn0_t"], xs0, xs1, y0)

            def add_rows(dve, q, rows, finished):
                x = k.x[:, q * GT:(q + 1) * GT, :]
                dve.tensor_tensor(x, x, rows, ALU.add).then_inc(finished, 1)

            gnn(k, "p2", a["adj_t"], [k.xw], add_rows, True, fill=[xs0, xs1])
        with ExitStack() as c:
            k.slots0, k.gates0 = sb(c, "slots0", [P, NT, K0], U32), sb(c, "gates0", [P, NT, K0], F32)
            spreads(k, "p3a")
            route0(k, a["router0_t"], a["bias0"], a["shared0"], xs0, y0)
            experts0(k, a["experts0"], xs0, y0)
            combine(k, "p5", y0, k.slots0, k.gates0, K0)
        with ExitStack() as c:
            k.g_high, k.g_low = sb(c, "g_high", [P, NT, D], F32R), sb(c, "g_low", [P, NT, D], F32R)
            spreads(k, "p5a")
            project(k, a["gnn1"], a["gnn1_bias"])

            def add_scaled(dve, q, rows, finished):
                for t in range(GT):
                    tile = q * GT + t
                    m = dve.scalar_tensor_tensor(out=k.x[:, tile, :], in0=rows[:, t, :], scalar=k.dinv[:, tile:tile + 1], in1=k.x[:, tile, :],
                                                 op0=ALU.mult, op1=ALU.add)
                m.then_inc(finished, 1)

            gnn(k, "p6", a["adj"], [k.g_high, k.g_low], add_scaled, False)
        with ExitStack() as c:
            k.slots1, k.gates1 = sb(c, "slots1", [P, NT, K1], U32), sb(c, "gates1", [P, NT, K1], F32)
            k.owner1, k.xring = sb(c, "owner1", [P, NT1], I32), sb(c, "xring", [P, 2, 4, D], F32)
            spreads(k, "p7a")
            route1(k, a["router1"], a["bias1"], xs1)
            experts1(k, a["experts1"], a["b1"], a["b2"], xs1, y1)
            combine(k, "p9", y1, k.slots1, k.gates1, K1, out=out)


def kernel(**inputs):
    import concourse.bacc as bacc
    from concourse.bass_utils import run_bass_kernel_spmd

    i = {name: np.asarray(v) for name, v in inputs.items()}
    chunks = lambda w: w.transpose(0, 2, 1).reshape(w.shape[0], DC, P, -1).transpose(0, 2, 1, 3).reshape(w.shape[0], P, -1)
    swiglu = lambda g, u, d: np.concatenate([chunks(i[g]), chunks(i[u]), i[d].transpose(0, 2, 1)], axis=2)
    w1, w2 = i["L1_ffn_W1"], i["L1_ffn_W2"]
    arrays = {
        "x": i["x"],
        "adj": i["adj"],
        "adj_t": i["adj"].T,
        "gnn0_t": i["L0_gnn_weight"].T,
        "router0_t": i["L0_ffn_router_w"].T,
        "bias0": i["L0_ffn_bias"],
        "shared0": swiglu("L0_ffn_shared_w_gate", "L0_ffn_shared_w_up", "L0_ffn_shared_w_down"),
        "experts0": swiglu("L0_ffn_w_gate", "L0_ffn_w_up", "L0_ffn_w_down"),
        "gnn1": i["L1_gnn_weight"],
        "gnn1_bias": i["L1_gnn_bias"],
        "router1": i["L1_ffn_Wr"],
        "bias1": i["L1_ffn_br"],
        "experts1": np.concatenate([
            w1.reshape(E1, DC, P, F1).transpose(0, 2, 1, 3).reshape(E1, P, -1),
            w2.reshape(E1, FB1, P, D).transpose(0, 2, 1, 3).reshape(E1, P, -1)], axis=2),
        "b1": i["L1_ffn_b1"].reshape(E1, FB1, P).transpose(0, 2, 1),
        "b2": i["L1_ffn_b2"],
    }
    arrays = {f"in_{n}": np.ascontiguousarray(v) for n, v in arrays.items()}
    nc = bacc.Bacc("TRN2", target_bir_lowering=False, num_devices=1)
    aps = {n[3:]: nc.dram_tensor(n, v.shape, mybir.dt.from_np(v.dtype), kind="ExternalInput").ap() for n, v in arrays.items()}
    out = nc.dram_tensor("out", (N, D), F32, kind="ExternalOutput").ap()
    build(nc, aps, out)
    r = run_bass_kernel_spmd(nc, [arrays], core_ids=[0])
    return r.results[0]["out"]
```

```python
from contextlib import ExitStack

import numpy as np
import concourse.bass as bass
from concourse import mybir

F32 = mybir.dt.float32
F32R = mybir.dt.float32r
BF16 = mybir.dt.bfloat16
I32 = mybir.dt.int32
U32 = mybir.dt.uint32
ACT = mybir.ActivationFunctionType
ALU = mybir.AluOpType
AX = mybir.AxisListType
ds = bass.ds

P = 128
N, D = 4096, 256
NT = N // P
DC = D // P
EPS = 1e-5

E0, F0, K0 = 64, 128, 6
CAP = N * K0 * 2 // E0
RPP = CAP // P
HALF = CAP // 2
SPAN = CAP + P
SLOTS0 = E0 * SPAN
RESULTS0 = E0 * CAP
SKIP = 1 << 17
E1, F1, K1 = 8, 1024, 2
FB1 = F1 // P
T1 = 256
NT1 = N * K1 // T1 + E1
SLOTS1 = NT1 * T1

QW = 1024
NQ = N // QW
JS = 2
STEPS = NT // JS
RAW = 4
GR = STEPS // RAW
GT = QW // P


class Kernel:

    def __init__(self, nc, ctx):
        self.nc, self.ctx = nc, ctx

    def sem(self, name):
        return self.ctx.enter_context(self.nc.semaphore(name))


def wait_apart(eng, sem, value, passed):
    if not (isinstance(value, int) and value <= 0):
        eng.wait_ge(sem, value)
        eng.sem_inc(passed, 1)


def wait_from(eng, sem, value):
    if not (isinstance(value, int) and value <= 0):
        eng.wait_ge(sem, value)


def passes(eng, count):
    yield 0
    with eng.Fori(1, count) as it:
        yield it


def make_constants(k):
    nc, c = k.nc, k.ctx
    sb = lambda n, s, d: c.enter_context(nc.sbuf_tensor(n, s, d))
    k.ident = sb("ident", [P, P], F32)
    k.identb = sb("identb", [P, P], BF16)
    k.tri = sb("tri", [P, P], BF16)
    k.onesb = sb("onesb", [P, P], BF16)
    k.iota = sb("iota", [P, E0], F32)
    k.x = sb("x", [P, NT, D], F32)
    k.deg = sb("deg", [P, NT], F32)
    k.dinv = sb("dinv", [P, NT], F32)
    k.minus_half = sb("minus_half", [P, NT], F32)
    k.passed = k.sem("passed")


def sign_features(k, x_in, w_t, xs0, xs1, y0):
    nc = k.nc
    G = NT // GT
    with ExitStack() as c:
        sb = lambda n, s, d: c.enter_context(nc.sbuf_tensor(n, s, d))
        ps = lambda n, s, d: c.enter_context(nc.psum_tensor(n, s, d))
        w_raw = sb("p1_w", [P, DC, D], F32)
        neg = sb("p1_neg", [P, DC, D], F32)
        sign_w = sb("p1_sign_w", [P, DC, D], BF16)
        total = sb("p1_total", [P, GT], F32)
        mean = sb("p1_mean", [P, GT], F32)
        pos = sb("p1_pos", [P, GT, D], BF16)
        pos_t = sb("p1_pos_t", [P, DC, GT * P], BF16)
        t_ps = ps("p1_t_ps", [P, DC, GT * P], BF16)
        xw_ps = ps("p1_xw_ps", [P, GT, D], F32)
        x_in_sem, w_sem, consts, fill = k.sem("x_loaded"), k.sem("p1_w_loaded"), k.sem("consts"), k.sem("p1_fill")
        signed, summed, averaged, positive = k.sem("p1_signed"), k.sem("p1_summed"), k.sem("p1_averaged"), k.sem("p1_positive")
        turned, turned_out, multiplied, xw_out = k.sem("p1_turned"), k.sem("p1_turned_out"), k.sem("p1_multiplied"), k.sem("p1_xw_out")

        with nc.Block() as block:
            @block.sync
            def _(sp):
                sp.dma_start(w_raw[:], w_t.rearrange("(c p) o -> p c o", p=P)).then_inc(w_sem, 16)
                for g in range(G):
                    sp.dma_start(k.x[:, g * GT:(g + 1) * GT, :],
                                 x_in[g * GT * P:(g + 1) * GT * P, :].rearrange("(t p) d -> p t d", p=P)).then_inc(x_in_sem, 16)

            @block.gpsimd
            def _(pool):
                pool.memset(k.ident[:], 0.0).then_inc(fill, 1)
                pool.memset(k.identb[:], 0.0).then_inc(fill, 1)
                pool.memset(k.tri[:], 0.0).then_inc(fill, 1)
                pool.memset(k.onesb[:], 1.0).then_inc(consts, 1)
                pool.memset(k.minus_half[:], -0.5).then_inc(consts, 1)
                pool.iota(k.iota[:], pattern=[[1, E0]], base=0, channel_multiplier=0,
                          allow_small_or_imprecise_dtypes=True).then_inc(consts, 1)
                pool.wait_ge(fill, 3)
                for m in (k.ident, k.identb):
                    pool.affine_select(out=m[:], in_=m[:], compare_op=ALU.not_equal, fill=1.0, base=0,
                                       pattern=[[-1, P]], channel_multiplier=1).then_inc(consts, 1)
                pool.affine_select(out=k.tri[:], in_=k.tri[:], compare_op=ALU.is_ge, fill=1.0, base=0,
                                   pattern=[[-1, P]], channel_multiplier=1).then_inc(consts, 1)

            @block.vector
            def _(dve):
                dve.wait_ge(w_sem, 16)
                dve.tensor_scalar(neg[:], w_raw[:], 0.0, None, ALU.is_lt).then_inc(signed, 1)
                dve.wait_ge(signed, 1)
                dve.scalar_tensor_tensor(out=sign_w[:], in0=w_raw[:], scalar=0.0, in1=neg[:],
                                         op0=ALU.is_gt, op1=ALU.subtract).then_inc(signed, 1)
                dve.wait_ge(x_in_sem, 16 * G)
                for g in passes(dve, G):
                    x = k.x[:, ds(g * GT, GT), :]
                    dve.tensor_reduce(total[:], x, AX.X, ALU.add).then_inc(summed, 1)
                    dve.wait_ge(summed, g + 1)
                    dve.tensor_scalar(mean[:], total[:], 1.0 / D, None, ALU.mult).then_inc(averaged, 1)
                    dve.wait_ge(averaged, g + 1)
                    wait_from(dve, turned, g)
                    dve.tensor_tensor(pos[:], x, mean[:, :, None].to_broadcast([P, GT, D]), ALU.is_gt).then_inc(positive, 1)
                    dve.wait_ge(multiplied, g + 1)
                    dve.tensor_copy(k.xw[:, ds(g * GT, GT), :], xw_ps[:]).then_inc(xw_out, 1)

            @block.tensor
            def _(pe):
                pe.wait_ge(consts, 6)
                pe.wait_ge(signed, 2)
                for g in passes(pe, G):
                    pe.wait_ge(positive, g + 1)
                    for t in range(GT):
                        for d in range(DC):
                            m = pe.transpose(t_ps[:, d, t * P:(t + 1) * P], pos[:, t, d * P:(d + 1) * P], k.identb[:])
                    m.then_inc(turned, 1)
                    pe.wait_ge(turned_out, g + 1)
                    wait_from(pe, xw_out, g)
                    for t in range(GT):
                        for d in range(DC):
                            m = pe.matmul(xw_ps[:, t, :], pos_t[:, d, t * P:(t + 1) * P], sign_w[:, d, :],
                                          start=(d == 0 and t % 2 == 0), stop=(d == DC - 1), skip_group_check=True)
                    m.then_inc(multiplied, 1)

            @block.scalar
            def _(act):
                for g in passes(act, G):
                    act.wait_ge(turned, g + 1)
                    wait_from(act, multiplied, g)
                    act.activation(pos_t[:], t_ps[:], ACT.Copy).then_inc(turned_out, 1)


def gnn(k, name, graph, features, finish, sum_degrees, fill=None):
    nc = k.nc
    passes = [(f, part) for f in range(len(features)) for part in range(2) if f + part < 2]
    with ExitStack() as c:
        sb = lambda n, s, d: c.enter_context(nc.sbuf_tensor(f"{name}_{n}", s, d))
        ps = lambda n, s, d: c.enter_context(nc.psum_tensor(f"{name}_{n}", s, d))
        sem = lambda n: k.sem(f"{name}_{n}")
        raw = sb("raw", [P, RAW, JS, QW], F32)
        high = sb("high", [P, 2, JS, QW], F32R)
        low = sb("low", [P, 2, JS, QW], F32R)
        out_t = sb("out_t", [P, DC, QW], F32)
        sums = sb("sums", [P, NT, NQ], F32) if sum_degrees else None
        junk = sb("junk", [P, 2, JS, QW], BF16) if sum_degrees else None
        if fill is not None:
            zero = sb("zero", [P, 12 * D], F32)
            zero_set, zero_stored = sem("zero_set"), sem("zero_stored")
        acc = ps("acc", [P, 2, 4, 512], F32)
        loaded = [sem(f"loaded{s}") for s in range(RAW)]
        summed, low_done, multiplied = sem("summed"), sem("low_done"), sem("multiplied")
        high_done, taken, turned, finished = sem("high_done"), sem("taken"), sem("turned"), sem("finished")
        if sum_degrees:
            halfway = sem("halfway")

        with nc.Block() as block:
            @block.sync
            def _(sp):
                with sp.Fori(0, NQ) as q, sp.Fori(0, GR) as g:
                    for s in range(RAW):
                        sp.wait_ge(low_done, (q * GR + g) * RAW + (s + 1))
                        if sum_degrees:
                            sp.wait_ge(summed, (q * GR + g) * RAW + (s + 1))
                        sp.dma_start(raw[:, s, :, :],
                                     graph.rearrange("(j p) i -> p j i", p=P)[:, ds((g * RAW + s) * JS, JS), ds(q * QW, QW)]
                                     ).then_inc(loaded[s], 16)

            @block.scalar
            def _(act):
                if sum_degrees:
                    act.sem_inc(summed, RAW)
                for q in range(NQ):
                    with act.Fori(0, GR) as g:
                        for s in range(RAW):
                            act.wait_ge(loaded[s], (g + (q * GR + 1)) * 16)
                            act.wait_ge(multiplied, g * RAW + (q * STEPS + s + 1))
                            act.activation(high[:, s % 2, :, :], raw[:, s, :, :], ACT.Copy).then_inc(high_done, 1)
                            if sum_degrees:
                                act.wait_ge(summed, g * RAW + (q * STEPS + s + RAW - 1))
                                for j in range(JS):
                                    act.activation(junk[:, s % 2, j, :], raw[:, s, j, :], ACT.Copy,
                                                   accum_out=sums[:, ds(g * (RAW * JS) + (s * JS + j), 1), q]).then_inc(summed if j else halfway, 1)

            @block.vector
            def _(dve):
                dve.sem_inc(low_done, RAW)

                def take_quarter(q):
                    dve.wait_ge(multiplied, 2 + (q + 1) * STEPS)
                    if q:
                        dve.wait_ge(turned, q)
                    half = acc[:, q % 2, :, :].rearrange("p (d b) n -> p d (b n)", d=DC)
                    if sum_degrees:
                        dve.tensor_scalar(out_t[:], half, 0.0, None, ALU.max).then_inc(taken, 1)
                    else:
                        dve.tensor_copy(out_t[:], half).then_inc(taken, 1)

                def finish_quarter(q):
                    dve.wait_ge(turned, q + 1)
                    finish(dve, q, acc[:, q % 2, :, :].rearrange("p b (t d) -> p (b t) d", d=D), finished)

                def low_parts(q, g, s, n):
                    dve.wait_ge(high_done, n + 1)
                    m = dve.tensor_tensor(low[:, s % 2, :, :], raw[:, s, :, :], high[:, s % 2, :, :].bitcast(F32), ALU.subtract)
                    m.then_inc(low_done, 1)

                for q in range(NQ):
                    if q:
                        for g, then in ((0, take_quarter), (1, finish_quarter)):
                            for s in range(RAW):
                                low_parts(q, g, s, g * RAW + q * STEPS + s)
                            then(q - 1)
                    with dve.Fori(2 if q else 0, GR) as g:
                        for s in range(RAW):
                            low_parts(q, g, s, g * RAW + (q * STEPS + s))
                take_quarter(NQ - 1)
                finish_quarter(NQ - 1)
                if sum_degrees:
                    dve.wait_ge(summed, RAW + NQ * STEPS)
                    dve.wait_ge(halfway, NQ * STEPS)
                    dve.tensor_reduce(k.deg[:], sums[:], AX.X, ALU.add).then_inc(finished, 1)

            @block.tensor
            def _(pe):
                def turn_back(q):
                    pe.wait_ge(taken, q + 1)
                    rows = acc[:, q % 2, :, :].rearrange("p b (t d) -> p (b t) d", d=D)
                    for t in range(GT):
                        for d in range(DC):
                            m = pe.transpose(rows[:, t, d * P:(d + 1) * P], out_t[:, d, t * P:(t + 1) * P], k.ident[:])
                    m.then_inc(turned, 1)

                pe.sem_inc(multiplied, 2)
                for q in range(NQ):
                    if q >= 2:
                        pe.wait_ge(finished, q - 1)
                    for n in range(STEPS):
                        pe.wait_ge(low_done, RAW + q * STEPS + n + 1)
                        for j in range(JS):
                            for d in range(DC):
                                for i, (f, part) in enumerate(passes):
                                    graph_part = (high, low)[part]
                                    for b in range(2):
                                        m = pe.matmul(acc[:, q % 2, d * 2 + b, :],
                                                      features[f][:, n * JS + j, d * P:(d + 1) * P],
                                                      graph_part[:, n % 2, j, b * 512:(b + 1) * 512],
                                                      start=(n == 0 and j == 0 and i == 0),
                                                      stop=(n == STEPS - 1 and j == JS - 1 and i == len(passes) - 1),
                                                      skip_group_check=True)
                        m.then_inc(multiplied, 1)
                        if n == 5 and q:
                            turn_back(q - 1)
                turn_back(NQ - 1)

            @block.gpsimd
            def _(pool):
                if fill is not None:
                    pool.memset(zero[:], 0.0).then_inc(zero_set, 1)
                    pool.wait_ge(zero_set, 1)
                    n = 0
                    for target in fill:
                        rows = target.shape[0]
                        while rows:
                            r = min(rows // P, 12)
                            pool.dma_start(target[target.shape[0] - rows:target.shape[0] - rows + r * P, :].rearrange("(p r) d -> p (r d)", p=P),
                                           zero[:, 0:r * D]).then_inc(zero_stored, 16)
                            rows -= r * P
                            n += 1
                    pool.wait_ge(zero_stored, 16 * n)


def spreads(k, name):
    nc = k.nc
    call = k.spread_calls
    k.spread_calls += 1
    if not call:
        k.spread_sems = [k.sem(f"spread_{n}") for n in ("summed", "averaged", "squared", "scaled", "rooted")]
    summed, averaged, squared, scaled, rooted = k.spread_sems
    with ExitStack() as c:
        sb = lambda n, s, d: c.enter_context(nc.sbuf_tensor(f"{name}_{n}", s, d))
        neg, squares, junk, var = sb("neg", [P, NT], F32), sb("squares", [P, NT], F32), sb("junk", [P, 4, D], F32), sb("var", [P, NT], F32)
        with nc.Block() as block:
            @block.vector
            def _(dve):
                for q in range(NQ):
                    tiles = slice(q * GT, (q + 1) * GT)
                    dve.tensor_reduce(k.mean[:, tiles], k.x[:, tiles, :], AX.X, ALU.add).then_inc(summed, 1)
                    dve.wait_ge(summed, call * NQ + q + 1)
                    dve.tensor_scalar(neg[:, tiles], k.mean[:, tiles], -1.0 / D, None, ALU.mult).then_inc(averaged, 1)
                dve.wait_ge(averaged, (call + 1) * NQ)
                dve.tensor_scalar(k.mean[:], neg[:], -1.0, None, ALU.mult)
                dve.wait_ge(squared, (call + 1) * (4 + NT))
                dve.tensor_scalar(var[:], squares[:], 1.0 / D, EPS, ALU.mult, ALU.add).then_inc(scaled, 1)

            @block.scalar
            def _(act):
                act.sem_inc(squared, 4)
                for it in passes(act, NQ):
                    act.wait_ge(averaged, it + (call * NQ + 1))
                    for s in range(GT):
                        act.wait_ge(squared, it * GT + (call * (4 + NT) + s + 1))
                        act.sem_inc(k.passed, 1)
                        act.activation(junk[:, s % 4, :], k.x[:, it * GT + s, :], ACT.Square, bias=neg[:, ds(it * GT + s, 1)],
                                       accum_out=squares[:, ds(it * GT + s, 1)]).then_inc(squared, 1)

            @block.gpsimd
            def _(pool):
                pool.wait_ge(scaled, call + 1)
                pool.tensor_tensor(k.rstd[:], var[:], k.minus_half[:], ALU.pow).then_inc(rooted, 1)


def route0(k, router_t, bias, shared, xs0, y0):
    nc = k.nc
    GTR = 4
    TOK = GTR * P
    KG = K0 * GTR
    with ExitStack() as c:
        sb = lambda n, s, d: c.enter_context(nc.sbuf_tensor(f"p3_{n}", s, d))
        ps = lambda n, s, d: c.enter_context(nc.psum_tensor(f"p3_{n}", s, d))
        sem = lambda n: k.sem(f"p3_{n}")
        wr = sb("wr", [P, DC, E0], F32)
        bias_sb = sb("bias", [P, E0], F32)
        wsh = sb("wsh", [P, 2, 3 * D], F32)
        counted = sb("counted", [P, E0], F32)
        xn = sb("xn", [P, 2, GTR, D], F32)
        xt = sb("xt", [P, 2, DC, TOK], F32)
        lg = sb("lg", [P, GTR, E0], F32)
        top = sb("top", [P, GTR, 8], F32)
        topi = sb("topi", [P, GTR, 8], U32)
        idx = sb("idx", [P, K0, GTR], F32)
        onehot = sb("onehot", [P, K0, GTR, E0], F32)
        prod = sb("prod", [P, K0, GTR, E0], F32)
        mask = sb("mask", [P, GTR, E0], BF16)
        before = sb("before", [P, GTR + 1, E0], BF16)
        rank = sb("rank", [P, K0, GTR], F32)
        slot = sb("slot", [P, K0, GTR], F32)
        full = sb("full", [P, K0, GTR], F32)
        where = sb("where", [P, K0, GTR], F32)
        slot_i = sb("slot_i", [P, 2, K0, GTR], U32)
        sg = sb("sg", [P, 2, TOK], F32)
        hid = sb("hid", [P, 2, TOK], F32)
        t_ps, lg_ps, rank_ps = ps("t_ps", [P, DC, TOK], F32), ps("lg_ps", [P, 512], F32), ps("rank_ps", [P, 512], F32)
        gate_ps, up_ps, down_ps = ps("gate_ps", [P, TOK], F32), ps("up_ps", [P, TOK], F32), ps("down_ps", [P, GTR, D], F32)
        lgv = lg_ps[:, 0:GTR * E0].rearrange("p (t e) -> p t e", e=E0)
        rkv = rank_ps[:, 0:GTR * E0].rearrange("p (t e) -> p t e", e=E0)
        w_loaded, zeroed, zero_out = sem("w_loaded"), sem("zeroed"), sem("zero_out")
        normed, turned, xt_out, logged, ranked, scored = sem("normed"), sem("turned"), sem("xt_out"), sem("logged"), sem("ranked"), sem("scored")
        gated, lifted, silu_out, hidden, lowered, shared_in = sem("gated"), sem("lifted"), sem("silu_out"), sem("hidden"), sem("lowered"), sem("shared_in")
        chain, maxed, slotted, placed, scattered = sem("chain"), sem("maxed"), sem("slotted"), sem("placed"), [sem("scattered0"), sem("scattered1")]
        totals = sem("totals")
        NG = NT // GTR
        LINKS = 11 + GTR
        MASKED = 5 + GTR

        def last(r, j):
            return isinstance(r, int) and r * 2 + j == NG - 1

        with nc.Block() as block:
            @block.sync
            def _(sp):
                sp.dma_start(wr[:], router_t.rearrange("(c p) e -> p c e", p=P)).then_inc(w_loaded, 16)
                sp.dma_start(bias_sb[:], bias.rearrange("(a e) -> a e", a=1).to_broadcast([P, E0])).then_inc(w_loaded, 16)
                sp.dma_start(wsh[:], shared.rearrange("s p n -> p s n")).then_inc(w_loaded, 16)
                sp.wait_ge(zeroed, 1)
                sp.dma_start(y0[RESULTS0:RESULTS0 + P, :], k.zrow[:]).then_inc(zero_out, 16)
                sp.wait_ge(zero_out, 16)

            @block.vector
            def _(dve):
                dve.memset(k.zrow[:], 0.0).then_inc(zeroed, 1)
                dve.memset(before[:, GTR, :], 0.0).then_inc(zeroed, 1)
                dve.wait_ge(zeroed, 2)
                dve.wait_ge(w_loaded, 48)

                def layer_norm(r, j):
                    wait_apart(dve, scattered[j], r * (16 * KG), k.passed)
                    for t in range(GTR):
                        tile = (r * 2 + j) * GTR + t
                        dve.tensor_scalar(xn[:, j, t, :], k.x[:, tile, :], k.mean[:, ds(tile, 1)], k.rstd[:, ds(tile, 1)],
                                          ALU.subtract, ALU.mult).then_inc(normed, 1)

                def linker(links):
                    count = 0

                    def link(ins):
                        nonlocal count
                        count += 1
                        ins.then_inc(chain, 1)
                        dve.wait_ge(chain, links + count)
                    return link, lambda: count

                def choose(r, j):
                    n = r * 2 + j
                    link, count = linker(n * LINKS)
                    dve.wait_ge(logged, n + 1)
                    link(dve.tensor_tensor(lg[:], lgv, bias_sb[:, None, :].to_broadcast([P, GTR, E0]), ALU.add))
                    dve.tensor_copy(k.logits0[:, ds(n * GTR, GTR), :], lg[:]).then_inc(scored, 1)
                    for t in range(GTR):
                        dve.max(top[:, t, :], lg[:, t, :]).then_inc(maxed, 1)
                    wait_apart(dve, maxed, n * (2 * GTR) + GTR, k.passed)
                    for t in range(GTR):
                        dve.max_index(topi[:, t, :], top[:, t, :], lg[:, t, :]).then_inc(maxed, 1)
                    dve.tensor_copy(k.tops0[:, ds(n * GTR, GTR), :], top[:, :, 0:K0]).then_inc(scored, 1)
                    dve.wait_ge(maxed, (n + 1) * (2 * GTR))
                    link(dve.tensor_copy(idx[:], topi[:, :, 0:K0].rearrange("p t k -> p k t")))
                    link(dve.tensor_tensor(onehot[:], k.iota[:, None, None, :].to_broadcast([P, K0, GTR, E0]),
                                           idx[:, :, :, None].to_broadcast([P, K0, GTR, E0]), ALU.is_equal))
                    with nc.allow_low_precision(reason="zeros and ones are exact"):
                        link(dve.tensor_reduce(mask[:], onehot[:].rearrange("p k t e -> p t e k"), AX.X, ALU.add))
                    link(dve.tensor_copy(before[:, 0, :], before[:, GTR, :]))
                    for t in range(GTR):
                        link(dve.tensor_tensor(before[:, t + 1, :], before[:, t, :], mask[:, t, :], ALU.add))
                    assert count() == MASKED

                def place(r, j):
                    n = r * 2 + j
                    link, count = linker(n * LINKS + MASKED)
                    dve.wait_ge(ranked, n + 1)
                    link(dve.tensor_tensor(prod[:], onehot[:], rkv[:, None, :, :].to_broadcast([P, K0, GTR, E0]), ALU.mult))
                    link(dve.tensor_reduce(rank[:], prod[:], AX.X, ALU.add))
                    link(dve.tensor_scalar(full[:], rank[:], float(CAP), float(SKIP), ALU.is_ge, ALU.mult))
                    link(dve.tensor_tensor(rank[:], rank[:], full[:], ALU.add))
                    link(dve.scalar_tensor_tensor(out=slot[:], in0=idx[:], scalar=float(SPAN), in1=rank[:], op0=ALU.mult, op1=ALU.add))
                    dve.tensor_copy(slot_i[:, j, :, :], slot[:]).then_inc(slotted, 1)
                    link(dve.scalar_tensor_tensor(out=where[:], in0=idx[:], scalar=float(CAP), in1=rank[:], op0=ALU.mult, op1=ALU.add))
                    assert count() == LINKS - MASKED
                    dve.tensor_scalar(k.slots0[:, ds(n * GTR, GTR), :].rearrange("p t k -> p k t"), where[:], float(RESULTS0), None, ALU.min).then_inc(placed, 1)

                def hide(r, j, h):
                    n = r * 2 + j
                    dve.wait_ge(silu_out, n * 2 + (h + 1))
                    wait_from(dve, lowered, n)
                    dve.tensor_tensor(hid[:, h, :], sg[:, h, :], up_ps[:], ALU.mult).then_inc(hidden, 1)

                def add_shared(r, j):
                    n = r * 2 + j
                    dve.wait_ge(lowered, n + 1)
                    dve.scalar_tensor_tensor(out=k.x[:, ds(n * GTR, GTR), :], in0=down_ps[:], scalar=0.5, in1=k.x[:, ds(n * GTR, GTR), :],
                                             op0=ALU.mult, op1=ALU.add).then_inc(shared_in, 1)

                layer_norm(0, 0)
                for r, j in units(dve, NG, 2):
                    choose(r, j)
                    if not (isinstance(r, int) and r * 2 + j == 0):
                        add_shared(*moved(r, j, -1, 2))
                    place(r, j)
                    hide(r, j, 0)
                    if not last(r, j):
                        layer_norm(*moved(r, j, 1, 2))
                    hide(r, j, 1)
                add_shared(NG // 2 - 1, 1)
                dve.wait_ge(totals, 1)
                dve.tensor_scalar(counted[:], rank_ps[:, 0:E0], float(CAP), None, ALU.min).then_inc(chain, 1)
                dve.wait_ge(chain, NG * LINKS + 1)
                dve.tensor_copy(k.rows0[:], counted[:])

            @block.scalar
            def _(act):
                def out_turned(r, j):
                    act.wait_ge(turned, r * 2 + (j + 1))
                    act.activation(xt[:, j, :, :], t_ps[:], ACT.Copy).then_inc(xt_out, 1)

                out_turned(0, 0)
                for r, j in units(act, NG, 2):
                    n = r * 2 + j
                    for h in range(2):
                        act.wait_ge(gated, n * 2 + (h + 1))
                        wait_from(act, hidden, n * 2)
                        act.activation(sg[:, h, :], gate_ps[:], ACT.Silu).then_inc(silu_out, 1)
                    if not last(r, j):
                        out_turned(*moved(r, j, 1, 2))

            @block.tensor
            def _(pe):
                def turn(r, j):
                    n = r * 2 + j
                    pe.wait_ge(normed, n * GTR + GTR)
                    wait_from(pe, xt_out, n)
                    for t in range(GTR):
                        for d in range(DC):
                            m = pe.transpose(t_ps[:, d, t * P:(t + 1) * P], xn[:, j, t, d * P:(d + 1) * P], k.ident[:])
                    m.then_inc(turned, 1)

                def logits(r, j):
                    n = r * 2 + j
                    pe.wait_ge(xt_out, n + 1)
                    wait_from(pe, scored, n * 2)
                    for t in range(GTR):
                        for d in range(DC):
                            m = pe.matmul(lgv[:, t, :], xt[:, j, d, t * P:(t + 1) * P], wr[:, d, :],
                                          start=(t == 0 and d == 0), stop=(d == DC - 1), skip_group_check=True)
                    m.then_inc(logged, 1)

                def lift(r, j, h):
                    wait_from(pe, hidden, (r * 2 + j) * 2 + h)
                    for (out, at) in ((gate_ps, 0), (up_ps, DC * F0)):
                        for d in range(DC):
                            m = pe.matmul(out[:], wsh[:, h, at + d * F0:at + (d + 1) * F0], xt[:, j, d, :],
                                          start=(d == 0), stop=(d == DC - 1))
                    m.then_inc(gated, 1)

                def ranks(r, j):
                    n = r * 2 + j
                    pe.wait_ge(chain, n * LINKS + MASKED)
                    wait_from(pe, placed, n)
                    pe.matmul(rank_ps[:, 0:GTR * E0], k.tri[:], mask[:].rearrange("p t e -> p (t e)"), start=True, stop=False)
                    pe.matmul(rank_ps[:, 0:GTR * E0], k.onesb[:], before[:, 0:GTR, :].rearrange("p t e -> p (t e)"),
                              start=False, stop=True).then_inc(ranked, 1)

                def lower(r, j):
                    n = r * 2 + j
                    pe.wait_ge(hidden, n * 2 + 2)
                    wait_from(pe, shared_in, n)
                    for t in range(GTR):
                        for h in range(2):
                            m = pe.matmul(down_ps[:, t, :], hid[:, h, t * P:(t + 1) * P], wsh[:, h, 2 * DC * F0:],
                                          start=(h == 0 and t % 2 == 0), stop=(h == 1), skip_group_check=True)
                    m.then_inc(lowered, 1)

                pe.wait_ge(w_loaded, 48)
                turn(0, 0)
                logits(0, 0)
                for r, j in units(pe, NG, 2):
                    lift(r, j, 0)
                    ranks(r, j)
                    lift(r, j, 1)
                    if not last(r, j):
                        turn(*moved(r, j, 1, 2))
                        logits(*moved(r, j, 1, 2))
                    lower(r, j)
                pe.wait_ge(placed, NG)
                pe.matmul(rank_ps[:, 0:E0], k.onesb[:], before[:, GTR, :], start=True, stop=True).then_inc(totals, 1)

            @block.gpsimd
            def _(pool):
                for it in passes(pool, NG // 2):
                    for s in range(2):
                        n = it * 2 + s
                        wait_apart(pool, slotted, n + 1, k.passed)
                        for kk in range(K0):
                            for t in range(GTR):
                                pool.indirect_dma_start(xs0, bass.IndirectOffsetOnAxis(ap=slot_i[:, s, kk, t:t + 1], axis=0),
                                                        xn[:, s, t, :], None, bounds_check=SLOTS0 - 1, oob_is_err=False
                                                        ).then_inc(scattered[s], 16)
                for s in range(2):
                    pool.wait_ge(scattered[s], NG // 2 * KG * 16)


UN = 8


def units(eng, total, un=UN):
    for j in range(un):
        yield 0, j
    with eng.Fori(1, total // un - 1) as it:
        for j in range(un):
            yield it, j
    for j in range(un):
        yield total // un - 1, j


def at(r, j):
    return r * UN + j


def moved(r, j, by, un=UN):
    return r + (j + by) // un, (j + by) % un


def split_products(pe, out, left, right, first, last):
    for n, (a, b) in enumerate(((0, 0), (0, 1), (1, 0))):
        m = pe.matmul(out, left[a], right[b], start=(first and n == 0), stop=(last and n == 2), skip_group_check=True)
    return m


def experts0(k, weights, xs0, y0):
    nc = k.nc
    U = 2 * E0
    RH = RPP // 2
    WN = 3 * D
    XR = 4
    LOADS = (1 + 2 * RH) * 16
    with ExitStack() as c:
        sb = lambda n, s, d: c.enter_context(nc.sbuf_tensor(f"p4_{n}", s, d))
        ps = lambda n, s, d: c.enter_context(nc.psum_tensor(f"p4_{n}", s, d))
        sem = lambda n: k.sem(f"p4_{n}")
        pair = lambda n, s: [sb(n + "_high", s, F32R), sb(n + "_low", s, F32R)]
        xe = sb("xe", [P, XR, 2, RH, D], F32)
        we = sb("we", [P, XR, WN], F32)
        w = pair("w", [P, XR, WN])
        xt = pair("xt", [P, 2, DC, HALF])
        sg = sb("sg", [P, 2, HALF], F32)
        hid = sb("hid", [P, 2, HALF], F32)
        hid_parts = pair("hid_parts", [P, 2, HALF])
        ye = sb("ye", [P, 4, RH, D], F32)
        t_ps = ps("t_ps", [P, DC, 512], F32)
        gate_ps, up_ps = ps("gate_ps", [P, 2, 512], F32), ps("up_ps", [P, 2, 512], F32)
        down_ps = ps("down_ps", [P, 4, D], F32)
        loaded, padded = [[sem(f"{n}{s}") for s in range(XR)] for n in ("loaded", "padded")]
        stored = [sem(f"stored{s}") for s in range(4)]
        turned, xt_high, xt_low, w_high, w_low, lifted, silu_out, hidden, hid_high, hid_low, lowered, y_out, cleared = [
            sem(n) for n in ("turned", "xt_high", "xt_low", "w_high", "w_low", "lifted", "silu_out", "hidden", "hid_high",
                             "hid_low", "lowered", "y_out", "cleared")]
        xs_v = xs0.rearrange("(e i p) d -> e i p d", i=SPAN // P, p=P)
        y_v = y0[0:RESULTS0, :].rearrange("(e b i p) d -> e b p i d", b=2, i=RH, p=P)

        def last(r, j):
            return isinstance(r, int) and at(r, j) == U - 1

        def is_first(r, j):
            return isinstance(r, int) and at(r, j) == 0

        with nc.Block() as block:
            @block.sync
            def _(sp):
                sp.wait_ge(cleared, 1)

                def pad(r, j):
                    e = r * XR + j
                    rows = sp.value_load(k.rows0[0:1, ds(e, 1)], min_val=0, max_val=CAP)
                    sp.dma_start(xs0[ds(e * SPAN + rows, P), :], k.zrow[:]).then_inc(padded[j], 16)

                for j in range(XR):
                    pad(0, j)
                for r, j in units(sp, E0, XR):
                    e = r * XR + j
                    wait_apart(sp, lowered, r * (2 * XR) + (2 * j + 2), k.passed)
                    sp.dma_start(we[:, j, :], weights[ds(e, 1), :, :].rearrange("a p n -> p (a n)")).then_inc(loaded[j], 16)
                    rows = sp.value_load(k.rows0[0:1, ds(e, 1)], min_val=0, max_val=CAP)
                    wait_apart(sp, padded[j], r * 16 + 16, k.passed)
                    for i in range(2 * RH):
                        cond = dict(bounds_check="skip_entire_dma", cond=(rows > i * P)) if i else {}
                        sp.dma_start(xe[:, j, i // RH, i % RH, :], xs_v[ds(e, 1), i, :, :].rearrange("a p n -> p (a n)"), **cond).then_inc(loaded[j], 16)
                    if not (isinstance(r, int) and r == E0 // XR - 1):
                        pad(r + 1, j)

            @block.tensor
            def _(pe):
                pe.sem_inc(lowered, 2 * XR)

                def turn(r, j):
                    e = j // 2
                    if j % 2 == 0:
                        pe.wait_ge(loaded[e], r * LOADS + LOADS)
                    wait_from(pe, xt_high, at(r, j))
                    wait_from(pe, xt_low, at(r, j))
                    for i in range(RH):
                        for d in range(DC):
                            m = pe.transpose(t_ps[:, d, i * P:(i + 1) * P], xe[:, e, j % 2, i, d * P:(d + 1) * P], k.ident[:])
                    m.then_inc(turned, 1)

                def lift(r, j):
                    e = j // 2
                    if j % 2 == 0:
                        pe.wait_ge(w_low, r * (UN // 2) + j // 2 + 1)
                    pe.wait_ge(xt_low, at(r, j) + 1)
                    pe.wait_ge(xt_high, at(r, j) + 1)
                    for out, w0 in ((gate_ps, 0), (up_ps, DC * F0)):
                        for d in range(DC):
                            m = split_products(pe, out[:, j % 2, 0:HALF], [a[:, e, w0 + d * F0:w0 + (d + 1) * F0] for a in w],
                                               [a[:, j % 2, d, :] for a in xt], d == 0, d == DC - 1)
                    m.then_inc(lifted, 1)

                def lower(r, j):
                    pe.wait_ge(hid_low, at(r, j) + 1)
                    wait_from(pe, y_out, at(r, j))
                    for i in range(RH):
                        m = split_products(pe, down_ps[:, i, :], [a[:, j % 2, i * P:(i + 1) * P] for a in hid_parts],
                                           [a[:, j // 2, 2 * DC * F0:] for a in w], i % 2 == 0, True)
                    m.then_inc(lowered, 1)

                turn(0, 0)
                for r, j in units(pe, U):
                    if not last(r, j):
                        turn(*moved(r, j, 1))
                    lift(r, j)
                    if not is_first(r, j):
                        lower(*moved(r, j, -1))
                lower(U // UN - 1, UN - 1)

            @block.vector
            def _(dve):
                dve.memset(xe[:], 0.0).then_inc(cleared, 1)

                def low_turned(r, j):
                    dve.wait_ge(xt_high, at(r, j) + 1)
                    dve.tensor_tensor(xt[1][:, j % 2, :, :], t_ps[:, :, 0:HALF], xt[0][:, j % 2, :, :].bitcast(F32), ALU.subtract).then_inc(xt_low, 1)

                def low_weights(r, j):
                    dve.wait_ge(w_high, r * (UN // 2) + j // 2 + 1)
                    dve.tensor_tensor(w[1][:, j // 2, :], we[:, j // 2, :], w[0][:, j // 2, :].bitcast(F32), ALU.subtract).then_inc(w_low, 1)

                low_weights(0, 0)
                low_turned(0, 0)
                for r, j in units(dve, U):
                    if not last(r, j):
                        low_turned(*moved(r, j, 1))
                    dve.wait_ge(silu_out, at(r, j) + 1)
                    dve.tensor_tensor(hid[:, j % 2, :], sg[:, j % 2, :], up_ps[:, j % 2, 0:HALF], ALU.mult).then_inc(hidden, 1)
                    dve.wait_ge(hidden, at(r, j) + 1)
                    dve.tensor_copy(hid_parts[0][:, j % 2, :], hid[:, j % 2, :]).then_inc(hid_high, 1)
                    dve.wait_ge(hid_high, at(r, j) + 1)
                    dve.tensor_tensor(hid_parts[1][:, j % 2, :], hid[:, j % 2, :], hid_parts[0][:, j % 2, :].bitcast(F32), ALU.subtract).then_inc(hid_low, 1)
                    if j % 2 == 0 and not last(r, j + 1):
                        low_weights(*moved(r, j, 2))

            @block.scalar
            def _(act):
                def high_turned(r, j):
                    act.wait_ge(turned, at(r, j) + 1)
                    act.activation(xt[0][:, j % 2, :, :], t_ps[:, :, 0:HALF], ACT.Copy).then_inc(xt_high, 1)

                def high_weights(r, j):
                    act.wait_ge(loaded[j // 2], r * LOADS + LOADS)
                    act.wait_ge(lowered, at(r, j))
                    act.activation(w[0][:, j // 2, :], we[:, j // 2, :], ACT.Copy).then_inc(w_high, 1)

                def take_lowered(r, j):
                    act.wait_ge(lowered, at(r, j) + (2 * XR + 1))
                    wait_from(act, stored[j % 4], (r * 2 + j // 4) * 16)
                    act.activation(ye[:, j % 4, :, :], down_ps[:, 0:RH, :], ACT.Copy).then_inc(y_out, 1)

                high_weights(0, 0)
                high_turned(0, 0)
                for r, j in units(act, U):
                    if not last(r, j):
                        high_turned(*moved(r, j, 1))
                    if j % 2 == 0 and not last(r, j + 1):
                        high_weights(*moved(r, j, 2))
                    act.wait_ge(lifted, at(r, j) + 1)
                    act.activation(sg[:, j % 2, :], gate_ps[:, j % 2, 0:HALF], ACT.Silu).then_inc(silu_out, 1)
                    if not is_first(r, j):
                        take_lowered(*moved(r, j, -1))
                take_lowered(U // UN - 1, UN - 1)

            @block.gpsimd
            def _(pool):
                for it in passes(pool, U // UN):
                    for j in range(UN):
                        wait_apart(pool, y_out, at(it, j) + 1, k.passed)
                        pool.dma_start(y_v[ds(it * (UN // 2) + j // 2, 1), j % 2, :, :, :].rearrange("a p r n -> p (a r) n"),
                                       ye[:, j % 4, :, :]).then_inc(stored[j % 4], 16)
                for s in range(4):
                    pool.wait_ge(stored[s], U // 4 * 16)


def combine(k, name, y, slots, gates, kn, softmax=False, out=None):
    nc = k.nc
    R = 4
    with ExitStack() as c:
        sb = lambda n, s, d: c.enter_context(nc.sbuf_tensor(f"{name}_{n}", s, d))
        sem = lambda n: k.sem(f"{name}_{n}")
        rows = sb("rows", [P, R, kn, D], F32)
        at_i = sb("at", [P, R, kn], U32)
        copied, added = sem("copied"), sem("added")
        if out is not None:
            stored = sem("stored")
        if softmax:
            z = sb("z", [P, NT], F32)
            shifted, exped, gated = sem("shifted"), sem("exped"), sem("gated")
        gathered = [sem(f"gathered{s}") for s in range(R)]
        with nc.Block() as block:
            @block.gpsimd
            def _(pool):
                for it in passes(pool, NT // R):
                    for s in range(R):
                        n = it * R + s
                        wait_apart(pool, added, n * kn + kn, k.passed)
                        pool.tensor_copy(at_i[:, s, :], slots[:, n, :]).then_inc(copied, 1)
                        wait_apart(pool, copied, n + 1, k.passed)
                        for i in range(kn):
                            pool.indirect_dma_start(rows[:, s, i, :], None, y, bass.IndirectOffsetOnAxis(ap=at_i[:, s, i:i + 1], axis=0)
                                                    ).then_inc(gathered[s], 16)

            @block.vector
            def _(dve):
                dve.sem_inc(added, R * kn)
                if softmax:
                    first = k.tops0[:, :, 0:1]
                    dve.tensor_tensor(k.logits0[:], k.logits0[:], first.to_broadcast([P, NT, E0]), ALU.subtract).then_inc(shifted, 1)
                    dve.tensor_tensor(gates[:], k.tops0[:], first.to_broadcast([P, NT, kn]), ALU.subtract).then_inc(shifted, 1)
                    dve.wait_ge(exped, 2)
                    shares = z[:, :, None].to_broadcast([P, NT, kn])
                    for i, step in enumerate((
                            lambda: dve.tensor_reduce(z[:], k.logits0[:], AX.X, ALU.add),
                            lambda: dve.reciprocal(z[:], z[:]),
                            lambda: dve.tensor_tensor(gates[:], gates[:], shares, ALU.mult),
                            lambda: dve.tensor_reduce(z[:], gates[:], AX.X, ALU.add),
                            lambda: dve.tensor_scalar(z[:], z[:], 1e-9, None, ALU.add),
                            lambda: dve.reciprocal(z[:], z[:]),
                            lambda: dve.tensor_tensor(gates[:], gates[:], shares, ALU.mult))):
                        step().then_inc(gated, 1)
                        dve.wait_ge(gated, i + 1)
                for it in passes(dve, NT // R):
                    for s in range(R):
                        n = it * R + s
                        dve.wait_ge(gathered[s], (it + 1) * (16 * kn))
                        for i in range(kn):
                            if i:
                                dve.wait_ge(added, n * kn + (R * kn + i))
                            dve.scalar_tensor_tensor(out=k.x[:, n, :], in0=rows[:, s, i, :], scalar=gates[:, n, i:i + 1], in1=k.x[:, n, :],
                                                     op0=ALU.mult, op1=ALU.add).then_inc(added, 1)

            @block.scalar
            def _(act):
                if softmax:
                    act.wait_ge(shifted, 2)
                    for t in (k.logits0, gates):
                        act.activation(t[:], t[:], ACT.Exp).then_inc(exped, 1)

            @block.sync
            def _(sp):
                if out is not None:
                    for it in passes(sp, NT // R):
                        sp.wait_ge(added, (it + 1) * (R * kn) + R * kn)
                        sp.dma_start(out.rearrange("(t p) d -> p t d", p=P)[:, ds(it * R, R), :], k.x[:, ds(it * R, R), :]).then_inc(stored, 16)
                    sp.wait_ge(stored, NT // R * 16)


def project(k, weight, bias):
    nc = k.nc
    GTR = 4
    NG = NT // GTR
    with ExitStack() as c:
        sb = lambda n, s, d: c.enter_context(nc.sbuf_tensor(f"p5b_{n}", s, d))
        ps = lambda n, s, d: c.enter_context(nc.psum_tensor(f"p5b_{n}", s, d))
        sem = lambda n: k.sem(f"p5b_{n}")
        w = sb("w", [P, DC, D], F32)
        b = sb("b", [P, D], F32)
        xn = sb("xn", [P, 2, GTR, D], F32)
        xt = sb("xt", [P, 2, DC, GTR * P], F32)
        g32 = sb("g32", [P, 2, GTR, D], F32)
        t_ps = ps("t_ps", [P, 2, DC, GTR * P], F32)
        h_ps = ps("h_ps", [P, 2, GTR, D], F32)
        loaded, normed, turned, xt_out, made, scaled, high, low, biased, rooted = [
            sem(n) for n in ("loaded", "normed", "turned", "xt_out", "made", "scaled", "high", "low", "biased", "rooted")]
        with nc.Block() as block:
            @block.sync
            def _(sp):
                sp.dma_start(w[:], weight.rearrange("(c p) o -> p c o", p=P)).then_inc(loaded, 16)
                sp.dma_start(b[:], bias.rearrange("(a e) -> a e", a=1).to_broadcast([P, D])).then_inc(loaded, 16)

            @block.gpsimd
            def _(pool):
                pool.tensor_tensor(k.dinv[:], k.deg[:], k.minus_half[:], ALU.pow).then_inc(rooted, 1)

            @block.vector
            def _(dve):
                dve.wait_ge(loaded, 32)
                dve.wait_ge(rooted, 1)
                for it in passes(dve, NG // 2):
                    for s in range(2):
                        n = it * 2 + s
                        wait_from(dve, turned, n)
                        for t in range(GTR):
                            tile = n * GTR + t
                            dve.tensor_scalar(xn[:, s, t, :], k.x[:, tile, :], k.mean[:, ds(tile, 1)], k.rstd[:, ds(tile, 1)],
                                              ALU.subtract, ALU.mult).then_inc(normed, 1)
                        dve.wait_ge(normed, (n + 1) * GTR)
                        dve.tensor_tensor(k.x[:, ds(n * GTR, GTR), :], k.x[:, ds(n * GTR, GTR), :],
                                          b[:, None, :].to_broadcast([P, GTR, D]), ALU.add).then_inc(biased, 1)
                        dve.wait_ge(made, n + 1)
                        dve.tensor_tensor(g32[:, s, :, :], h_ps[:, s, :, :], k.dinv[:, ds(n * GTR, GTR), None].to_broadcast([P, GTR, D]),
                                          ALU.mult).then_inc(scaled, 1)
                        dve.wait_ge(high, n + 1)
                        dve.tensor_tensor(k.g_low[:, ds(n * GTR, GTR), :], g32[:, s, :, :], k.g_high[:, ds(n * GTR, GTR), :].bitcast(F32),
                                          ALU.subtract).then_inc(low, 1)

            @block.scalar
            def _(act):
                for it in passes(act, NG // 2):
                    for s in range(2):
                        n = it * 2 + s
                        act.wait_ge(turned, n + 1)
                        act.activation(xt[:, s, :, :], t_ps[:, s, :, :], ACT.Copy).then_inc(xt_out, 1)
                        wait_apart(act, scaled, n + 1, k.passed)
                        act.activation(k.g_high[:, ds(n * GTR, GTR), :], g32[:, s, :, :], ACT.Copy).then_inc(high, 1)

            @block.tensor
            def _(pe):
                pe.wait_ge(loaded, 32)
                for it in passes(pe, NG // 2):
                    for s in range(2):
                        n = it * 2 + s
                        pe.wait_ge(normed, (n + 1) * GTR)
                        for t in range(GTR):
                            for d in range(DC):
                                m = pe.transpose(t_ps[:, s, d, t * P:(t + 1) * P], xn[:, s, t, d * P:(d + 1) * P], k.ident[:])
                        m.then_inc(turned, 1)
                        pe.wait_ge(xt_out, n + 1)
                        for t in range(GTR):
                            for d in range(DC):
                                m = pe.matmul(h_ps[:, s, t, :], xt[:, s, d, t * P:(t + 1) * P], w[:, d, :],
                                              start=(d == 0 and t % 2 == 0), stop=(d == DC - 1), skip_group_check=True)
                        m.then_inc(made, 1)


def route1(k, router, bias, xs1):
    nc = k.nc
    GTR = 4
    NG = NT // GTR
    with ExitStack() as c:
        sb = lambda n, s, d: c.enter_context(nc.sbuf_tensor(f"p7_{n}", s, d))
        ps = lambda n, s, d: c.enter_context(nc.psum_tensor(f"p7_{n}", s, d))
        sem = lambda n: k.sem(f"p7_{n}")
        wr = sb("wr", [P, DC, E1], F32)
        bias_sb = sb("bias", [P, E1], F32)
        xn = sb("xn", [P, NT, D], F32)
        xt = sb("xt", [P, 2, DC, GTR * P], F32)
        logits = sb("logits", [P, NT, E1], F32)
        top = sb("top", [P, NT, 8], F32)
        topi = sb("topi", [P, NT, 8], U32)
        idx = sb("idx", [P, NT, K1], F32)
        onehot = sb("onehot", [P, K1, NT, E1], F32)
        prod = sb("prod", [P, K1, NT, E1], F32)
        mask = sb("mask", [P, NT, E1], BF16)
        prefix = [sb(f"prefix{i}", [P, NT + 1, E1], BF16) for i in range(2)]
        count = sb("count", [P, E1], F32)
        count_i = sb("count_i", [P, E1], I32)
        tiles_i = sb("tiles_i", [P, E1], I32)
        ends = [sb(f"ends{i}", [P, E1 + 1], F32) for i in range(2)]
        ordinal = sb("ordinal", [P, NT1], F32)
        beyond = sb("beyond", [P, NT1, E1], F32)
        owner = sb("owner", [P, NT1], F32)
        base = sb("base", [P, E1], F32)
        place = sb("place", [P, NT, E1], F32)
        slot = sb("slot", [P, NT, K1], F32)
        z = sb("z", [P, NT], F32)
        t_ps = ps("t_ps", [P, 2, DC, GTR * P], F32)
        lg_ps = ps("lg_ps", [P, 2, 512], F32)
        rank_ps, count_ps = ps("rank_ps", [P, 512], F32), ps("count_ps", [P, 512], F32)
        loaded, normed, turned, xt_out, logged, scored = [sem(n) for n in ("loaded", "normed", "turned", "xt_out", "logged", "scored")]
        chain, masked, ranked, placed, scattered, numbered, shifted, exped = [
            sem(n) for n in ("chain", "masked", "ranked", "placed", "scattered", "numbered", "shifted", "exped")]
        with nc.Block() as block:
            MASKED = 2 * NT + 1 + K1 + 5 + 1 + 2 * 5

            @block.sync
            def _(sp):
                sp.dma_start(wr[:], router.rearrange("(c p) e -> p c e", p=P)).then_inc(loaded, 16)
                sp.dma_start(bias_sb[:], bias.rearrange("(a e) -> a e", a=1).to_broadcast([P, E1])).then_inc(loaded, 16)

            @block.scalar
            def _(act):
                for it in passes(act, NG // 2):
                    for s in range(2):
                        n = it * 2 + s
                        act.wait_ge(turned, n + 1)
                        act.activation(xt[:, s, :, :], t_ps[:, s, :, :], ACT.Copy).then_inc(xt_out, 1)
                act.wait_ge(shifted, 1)
                act.activation(k.gates1[:], k.gates1[:], ACT.Exp).then_inc(exped, 1)

            @block.tensor
            def _(pe):
                pe.wait_ge(loaded, 32)
                for it in passes(pe, NG // 2):
                    for s in range(2):
                        n = it * 2 + s
                        pe.wait_ge(normed, (n + 1) * GTR)
                        for t in range(GTR):
                            for d in range(DC):
                                m = pe.transpose(t_ps[:, s, d, t * P:(t + 1) * P], k.xring[:, s, t, d * P:(d + 1) * P], k.ident[:])
                        m.then_inc(turned, 1)
                        pe.wait_ge(xt_out, n + 1)
                        for t in range(GTR):
                            for d in range(DC):
                                m = pe.matmul(lg_ps[:, s, t * E1:(t + 1) * E1], xt[:, s, d, t * P:(t + 1) * P], wr[:, d, :],
                                              start=(t == 0 and d == 0), stop=(d == DC - 1), skip_group_check=True)
                        m.then_inc(logged, 1)
                pe.wait_ge(chain, MASKED)
                flat = lambda a: a.rearrange("p t e -> p (t e)")
                pe.matmul(rank_ps[:, 0:NT * E1], k.tri[:], flat(mask[:]), start=True, stop=False)
                pe.matmul(rank_ps[:, 0:NT * E1], k.onesb[:], flat(prefix[1][:, 0:NT, :]), start=False, stop=True).then_inc(ranked, 1)
                pe.matmul(count_ps[:, 0:E1], k.onesb[:], prefix[1][:, NT, :], start=True, stop=True).then_inc(ranked, 1)

            @block.vector
            def _(dve):
                dve.wait_ge(loaded, 32)
                for it in passes(dve, NG // 2):
                    for s in range(2):
                        n = it * 2 + s
                        wait_from(dve, turned, n)
                        for t in range(GTR):
                            tile = n * GTR + t
                            dve.tensor_scalar(k.xring[:, s, t, :], k.x[:, tile, :], k.mean[:, ds(tile, 1)], k.rstd[:, ds(tile, 1)],
                                              ALU.subtract, ALU.mult).then_inc(normed, 1)
                        dve.wait_ge(normed, (n + 1) * GTR)
                        dve.tensor_copy(xn[:, ds(n * GTR, GTR), :], k.xring[:, s, :, :]).then_inc(scored, 1)
                        dve.wait_ge(logged, n + 1)
                        dve.tensor_tensor(logits[:, ds(n * GTR, GTR), :], lg_ps[:, s, 0:GTR * E1].rearrange("p (t e) -> p t e", e=E1),
                                          bias_sb[:, None, :].to_broadcast([P, GTR, E1]), ALU.add).then_inc(scored, 1)
                dve.wait_ge(scored, 2 * NG)
                links = 0

                def link(*steps):
                    nonlocal links
                    for step in steps:
                        step.then_inc(chain, 1)
                    links += len(steps)
                    dve.wait_ge(chain, links)

                link(*[dve.max(top[:, t, :], logits[:, t, :]) for t in range(NT)])
                link(*[dve.max_index(topi[:, t, :], top[:, t, :], logits[:, t, :]) for t in range(NT)])
                link(dve.tensor_copy(idx[:], topi[:, :, 0:K1]))
                link(*[dve.tensor_tensor(onehot[:, i, :, :], k.iota[:, None, 0:E1].to_broadcast([P, NT, E1]),
                                         idx[:, :, i:i + 1].to_broadcast([P, NT, E1]), ALU.is_equal) for i in range(K1)])
                link(dve.tensor_tensor(mask[:], onehot[:, 0, :, :], onehot[:, 1, :, :], ALU.add), dve.memset(prefix[0][:, 0:1, :], 0.0),
                     dve.memset(prefix[1][:, 0:1, :], 0.0), dve.memset(ends[0][:, 0:1], 0.0), dve.memset(ends[1][:, 0:1], 0.0))
                link(dve.tensor_copy(prefix[0][:, 1:, :], mask[:]))
                for b in range(5):
                    a, z2, by = prefix[b % 2], prefix[(b + 1) % 2], 1 << b
                    link(dve.tensor_copy(z2[:, 1:1 + by, :], a[:, 1:1 + by, :]),
                         dve.tensor_tensor(z2[:, 1 + by:, :], a[:, 1 + by:, :], a[:, 1:NT + 1 - by, :], ALU.add))
                assert links == MASKED
                dve.wait_ge(ranked, 2)
                link(dve.tensor_scalar(count[:], count_ps[:, 0:E1], float(T1 - 1), None, ALU.add))
                link(dve.tensor_copy(count_i[:], count[:]))
                link(dve.tensor_single_scalar(tiles_i[:], count_i[:], T1.bit_length() - 1, ALU.arith_shift_right))
                link(dve.tensor_copy(ends[0][:, 1:], tiles_i[:]))
                for b in range(3):
                    a, z2, by = ends[b % 2], ends[(b + 1) % 2], 1 << b
                    link(dve.tensor_copy(z2[:, 1:1 + by], a[:, 1:1 + by]),
                         dve.tensor_tensor(z2[:, 1 + by:], a[:, 1 + by:], a[:, 1:E1 + 1 - by], ALU.add))
                end = ends[1]
                dve.wait_ge(numbered, 1)
                link(dve.tensor_tensor(beyond[:], ordinal[:, :, None].to_broadcast([P, NT1, E1]), end[:, None, 1:].to_broadcast([P, NT1, E1]), ALU.is_ge),
                     dve.tensor_scalar(base[:], end[:, 0:E1], float(T1), None, ALU.mult))
                link(dve.tensor_reduce(owner[:], beyond[:], AX.X, ALU.add),
                     dve.tensor_tensor(place[:], rank_ps[:, 0:NT * E1].rearrange("p (t e) -> p t e", e=E1),
                                       base[:, None, :].to_broadcast([P, NT, E1]), ALU.add))
                link(dve.tensor_scalar(owner[:], owner[:], float(E1 - 1), None, ALU.min),
                     dve.tensor_tensor(prod[:], onehot[:], place[:, None, :, :].to_broadcast([P, K1, NT, E1]), ALU.mult))
                link(dve.tensor_copy(k.owner1[:], owner[:]), dve.tensor_reduce(slot[:].rearrange("p t k -> p k t"), prod[:], AX.X, ALU.add))
                dve.tensor_copy(k.slots1[:], slot[:]).then_inc(placed, 1)
                dve.tensor_tensor(k.gates1[:], top[:, :, 0:K1], top[:, :, 0:1].to_broadcast([P, NT, K1]), ALU.subtract).then_inc(shifted, 1)
                dve.wait_ge(exped, 1)
                link(dve.tensor_reduce(z[:], k.gates1[:], AX.X, ALU.add))
                link(dve.reciprocal(z[:], z[:]))
                link(dve.tensor_tensor(k.gates1[:], k.gates1[:], z[:, :, None].to_broadcast([P, NT, K1]), ALU.mult))

            @block.gpsimd
            def _(pool):
                pool.iota(ordinal[:], pattern=[[1, NT1]], base=0, channel_multiplier=0, allow_small_or_imprecise_dtypes=True).then_inc(numbered, 1)
                pool.wait_ge(placed, 1)
                for t in range(NT):
                    for i in range(K1):
                        pool.indirect_dma_start(xs1, bass.IndirectOffsetOnAxis(ap=k.slots1[:, t, i:i + 1], axis=0), xn[:, t, :], None,
                                                bounds_check=SLOTS1 - 1, oob_is_err=False).then_inc(scattered, 16)
                pool.wait_ge(scattered, 16 * NT * K1)


def experts1(k, weights, b1, b2, xs1, y1):
    nc = k.nc
    UT = 4
    TR = T1 // P
    W1, W2 = DC * F1, FB1 * D
    PAIRS = FB1 // 2
    with ExitStack() as c:
        sb = lambda n, s, d: c.enter_context(nc.sbuf_tensor(f"p8_{n}", s, d))
        ps = lambda n, s, d: c.enter_context(nc.psum_tensor(f"p8_{n}", s, d))
        sem = lambda n: k.sem(f"p8_{n}")
        pair = lambda n, s: [sb(n + "_high", s, F32R), sb(n + "_low", s, F32R)]
        raw1, raw2 = sb("raw1", [P, 2, W1], F32), sb("raw2", [P, 2, W2], F32)
        w1, w2 = pair("w1", [P, 2, W1]), pair("w2", [P, 2, W2])
        bias1, bias2 = sb("bias1", [P, UT, FB1], F32), sb("bias2", [P, UT, D], F32)
        x = sb("x", [P, 2, TR, D], F32)
        xt = pair("xt", [P, 2, DC, T1])
        h = sb("h", [P, PAIRS, 2, T1], F32)
        h_parts = pair("h_parts", [P, 2, PAIRS, 2, T1])
        y = sb("y", [P, 2, TR, D], F32)
        t_ps, h_ps, down_ps = ps("t_ps", [P, DC, T1], F32), ps("h_ps", [P, PAIRS, 2, T1], F32), ps("down_ps", [P, 2, TR, D], F32)
        rows_loaded, w1_loaded, w2_loaded, stored = [[sem(f"{n}{s}") for s in range(2)]
                                                     for n in ("rows_loaded", "w1_loaded", "w2_loaded", "stored")]
        bias_loaded = [sem(f"bias_loaded{s}") for s in range(UT)]
        turned, xt_high, xt_low, w1_high, w1_low, w2_high, w2_low, lifted, relu_out, h_high, h_low, lowered, y_out = [
            sem(n) for n in ("turned", "xt_high", "xt_low", "w1_high", "w1_low", "w2_high", "w2_low", "lifted", "relu_out",
                             "h_high", "h_low", "lowered", "y_out")]
        xs_v = xs1.rearrange("(n p r) d -> n p (r d)", p=P, r=TR)
        y_v = y1.rearrange("(n p r) d -> n p (r d)", p=P, r=TR)

        def uses(r, j):
            return r * (UT // 2) + j // 2 + 1

        def last(r, j):
            return isinstance(r, int) and r * UT + j == NT1 - 1

        def first(r, j):
            return isinstance(r, int) and r == 0 and j == 0

        with nc.Block() as block:
            @block.sync
            def _(sp):
                for r, j in units(sp, NT1, UT):
                    m, s = r * UT + j, j % 2
                    tile = ds(m, 1)
                    owner = sp.value_load(k.owner1[0:1, tile], min_val=0, max_val=E1 - 1)
                    expert = ds(owner, 1)
                    fresh = {}
                    if not isinstance(r, int) or m >= 2:
                        before = sp.value_load(k.owner1[0:1, ds(m - 2, 1)], min_val=0, max_val=E1 - 1)
                        fresh = dict(bounds_check="skip_entire_dma", cond=(owner != before))
                        wait_apart(sp, turned, m - 1, k.passed)
                    sp.dma_start(x[:, s, :, :].rearrange("p r d -> p (r d)"), xs_v[tile, :, :].rearrange("a p n -> p (a n)")).then_inc(rows_loaded[s], 16)
                    if fresh:
                        wait_apart(sp, w1_low, 2 * m - 2, k.passed)
                    sp.dma_start(raw1[:, s, :], weights[expert, :, 0:W1].rearrange("a p n -> p (a n)"), **fresh).then_inc(w1_loaded[s], 16)
                    if not isinstance(r, int) or m >= UT:
                        wait_apart(sp, y_out, m - (UT - 1), k.passed)
                    sp.dma_start(bias1[:, j, :], b1[expert, :, :].rearrange("a p n -> p (a n)")).then_inc(bias_loaded[j], 16)
                    sp.dma_start(bias2[:, j, :], b2[expert, :].to_broadcast([P, D])).then_inc(bias_loaded[j], 16)
                    if fresh:
                        wait_apart(sp, w2_low, m - 1, k.passed)
                    sp.dma_start(raw2[:, s, :], weights[expert, :, W1:].rearrange("a p n -> p (a n)"), **fresh).then_inc(w2_loaded[s], 16)

            @block.tensor
            def _(pe):
                def turn(r, j):
                    m, s = r * UT + j, j % 2
                    pe.wait_ge(rows_loaded[s], uses(r, j) * 16)
                    wait_from(pe, xt_low, m)
                    for i in range(TR):
                        for d in range(DC):
                            t = pe.transpose(t_ps[:, d, i * P:(i + 1) * P], x[:, s, i, d * P:(d + 1) * P], k.ident[:])
                    t.then_inc(turned, 1)

                def lift(r, j):
                    m, s = r * UT + j, j % 2
                    pe.wait_ge(w1_low, 2 * m + 2)
                    pe.wait_ge(xt_low, m + 1)
                    for p in range(PAIRS):
                        if not first(r, j):
                            pe.wait_ge(relu_out, m * PAIRS + (p + 1 - PAIRS))
                        for q in range(2):
                            f = p * 2 + q
                            for d in range(DC):
                                t = split_products(pe, h_ps[:, p, q, :], [a[:, s, d * F1 + f * P:d * F1 + (f + 1) * P] for a in w1],
                                                   [a[:, s, d, :] for a in xt], d == 0 and q == 0, d == DC - 1)
                        t.then_inc(lifted, 1)

                def lower(r, j):
                    m, s = r * UT + j, j % 2
                    pe.wait_ge(w2_low, m + 1)
                    if not isinstance(r, int) or m >= 2:
                        pe.wait_ge(y_out, m - 1)
                    for p in range(PAIRS):
                        pe.wait_ge(h_low, m * PAIRS + (p + 1))
                        for q in range(2):
                            f = p * 2 + q
                            for i in range(TR):
                                t = split_products(pe, down_ps[:, s, i, :], [a[:, s, p, q, i * P:(i + 1) * P] for a in h_parts],
                                                   [a[:, s, f * D:(f + 1) * D] for a in w2], f == 0 and i == 0, f == FB1 - 1)
                    t.then_inc(lowered, 1)

                turn(0, 0)
                for r, j in units(pe, NT1, UT):
                    if not last(r, j):
                        turn(*moved(r, j, 1, UT))
                    lift(r, j)
                    if not first(r, j):
                        lower(*moved(r, j, -1, UT))
                lower(NT1 // UT - 1, UT - 1)

            @block.scalar
            def _(act):
                def high_w1(r, j):
                    m, s = r * UT + j, j % 2
                    act.wait_ge(w1_loaded[s], uses(r, j) * 16)
                    if not isinstance(r, int) or m >= 2:
                        act.wait_ge(lifted, m * PAIRS - PAIRS)
                    for d in range(DC):
                        part = slice(d * F1, (d + 1) * F1)
                        act.activation(w1[0][:, s, part], raw1[:, s, part], ACT.Copy).then_inc(w1_high, 1)

                def high_turned(r, j):
                    act.wait_ge(turned, r * UT + (j + 1))
                    act.activation(xt[0][:, j % 2, :, :], t_ps[:], ACT.Copy).then_inc(xt_high, 1)

                def relus(r, j):
                    m = r * UT + j
                    act.wait_ge(bias_loaded[j], r * 32 + 32)
                    for p in range(PAIRS):
                        act.wait_ge(lifted, m * PAIRS + (p + 1))
                        if not first(r, j):
                            act.wait_ge(h_low, m * PAIRS + (p + 1 - PAIRS))
                        for q in range(2):
                            t = act.activation(h[:, p, q, :], h_ps[:, p, q, :], ACT.Relu, bias=bias1[:, j, p * 2 + q:p * 2 + q + 1])
                        t.then_inc(relu_out, 1)

                def high_w2(r, j):
                    m, s = r * UT + j, j % 2
                    act.wait_ge(w2_loaded[s], uses(r, j) * 16)
                    if not isinstance(r, int) or m >= 2:
                        act.wait_ge(lowered, m - 1)
                    act.activation(w2[0][:, s, :], raw2[:, s, :], ACT.Copy).then_inc(w2_high, 1)

                high_w1(0, 0)
                high_turned(0, 0)
                for r, j in units(act, NT1, UT):
                    if not last(r, j):
                        high_w1(*moved(r, j, 1, UT))
                        high_turned(*moved(r, j, 1, UT))
                    relus(r, j)
                    high_w2(r, j)

            @block.vector
            def _(dve):
                def low_w1(r, j):
                    m, s = r * UT + j, j % 2
                    for d in range(DC):
                        part = slice(d * F1, (d + 1) * F1)
                        dve.wait_ge(w1_high, m * DC + (d + 1))
                        dve.tensor_tensor(w1[1][:, s, part], raw1[:, s, part], w1[0][:, s, part].bitcast(F32), ALU.subtract).then_inc(w1_low, 1)

                def low_turned(r, j):
                    dve.wait_ge(xt_high, r * UT + (j + 1))
                    dve.tensor_tensor(xt[1][:, j % 2, :, :], t_ps[:], xt[0][:, j % 2, :, :].bitcast(F32), ALU.subtract).then_inc(xt_low, 1)

                def split_hidden(r, j):
                    m, s = r * UT + j, j % 2
                    for p in range(PAIRS):
                        dve.wait_ge(relu_out, m * PAIRS + (p + 1))
                        dve.tensor_copy(h_parts[0][:, s, p, :, :], h[:, p, :, :]).then_inc(h_high, 1)
                        dve.wait_ge(h_high, m * PAIRS + (p + 1))
                        dve.tensor_tensor(h_parts[1][:, s, p, :, :], h[:, p, :, :], h_parts[0][:, s, p, :, :].bitcast(F32), ALU.subtract).then_inc(h_low, 1)

                def low_w2(r, j):
                    s = j % 2
                    dve.wait_ge(w2_high, r * UT + (j + 1))
                    dve.tensor_tensor(w2[1][:, s, :], raw2[:, s, :], w2[0][:, s, :].bitcast(F32), ALU.subtract).then_inc(w2_low, 1)

                def results(r, j):
                    m, s = r * UT + j, j % 2
                    dve.wait_ge(lowered, m + 1)
                    dve.wait_ge(bias_loaded[j], r * 32 + 32)
                    if not isinstance(r, int) or m >= 2:
                        dve.wait_ge(stored[s], uses(r, j) * 16 - 16)
                    dve.tensor_tensor(y[:, s, :, :], down_ps[:, s, :, :], bias2[:, j, None, :].to_broadcast([P, TR, D]), ALU.add).then_inc(y_out, 1)

                low_w1(0, 0)
                low_turned(0, 0)
                for r, j in units(dve, NT1, UT):
                    if not isinstance(r, int) or r * UT + j >= 2:
                        results(*moved(r, j, -2, UT))
                    if not last(r, j):
                        low_w1(*moved(r, j, 1, UT))
                        low_turned(*moved(r, j, 1, UT))
                    split_hidden(r, j)
                    low_w2(r, j)
                results(NT1 // UT - 1, UT - 2)
                results(NT1 // UT - 1, UT - 1)

            @block.gpsimd
            def _(pool):
                for it in passes(pool, NT1 // 2):
                    for s in range(2):
                        wait_apart(pool, y_out, it * 2 + (s + 1), k.passed)
                        pool.dma_start(y_v[ds(it * 2 + s, 1), :, :].rearrange("a p n -> p (a n)"), y[:, s, :, :].rearrange("p r d -> p (r d)")).then_inc(stored[s], 16)
                for s in range(2):
                    pool.wait_ge(stored[s], NT1 // 2 * 16)


def build(nc, a, out, stop=99):
    xs0 = nc.dram_tensor("sent0", [SLOTS0, D], F32).ap()
    y0 = nc.dram_tensor("results0", [RESULTS0 + P, D], F32).ap()
    xs1 = nc.dram_tensor("sent1", [SLOTS1, D], F32).ap()
    y1 = nc.dram_tensor("results1", [SLOTS1, D], F32).ap()
    with ExitStack() as ctx:
        k = Kernel(nc, ctx)
        k.spread_calls = 0
        make_constants(k)
        sb = lambda c, n, s, d: c.enter_context(nc.sbuf_tensor(n, s, d))
        k.mean, k.rstd = sb(ctx, "mean", [P, NT], F32), sb(ctx, "rstd", [P, NT], F32)
        with ExitStack() as c:
            k.xw = sb(c, "xw", [P, NT, D], F32R)
            sign_features(k, a["x"], a["gnn0_t"], xs0, xs1, y0)

            def add_rows(dve, q, rows, finished):
                x = k.x[:, q * GT:(q + 1) * GT, :]
                dve.tensor_tensor(x, x, rows, ALU.add).then_inc(finished, 1)

            gnn(k, "p2", a["adj_t"], [k.xw], add_rows, True, fill=None)
        with ExitStack() as c:
            k.rows0 = sb(c, "rows0", [P, E0], I32)
            k.slots0, k.gates0 = sb(c, "slots0", [P, NT, K0], U32), sb(c, "gates0", [P, NT, K0], F32)
            k.logits0, k.tops0, k.zrow = sb(c, "logits0", [P, NT, E0], F32), sb(c, "tops0", [P, NT, K0], F32), sb(c, "zrow", [P, D], F32)
            spreads(k, "p3a")
            route0(k, a["router0_t"], a["bias0"], a["shared0"], xs0, y0)
            experts0(k, a["experts0"], xs0, y0)
            combine(k, "p5", y0, k.slots0, k.gates0, K0, softmax=True)
        with ExitStack() as c:
            k.g_high, k.g_low = sb(c, "g_high", [P, NT, D], F32R), sb(c, "g_low", [P, NT, D], F32R)
            spreads(k, "p5a")
            project(k, a["gnn1"], a["gnn1_bias"])

            def add_scaled(dve, q, rows, finished):
                for t in range(GT):
                    tile = q * GT + t
                    m = dve.scalar_tensor_tensor(out=k.x[:, tile, :], in0=rows[:, t, :], scalar=k.dinv[:, tile:tile + 1], in1=k.x[:, tile, :],
                                                 op0=ALU.mult, op1=ALU.add)
                m.then_inc(finished, 1)

            gnn(k, "p6", a["adj"], [k.g_high, k.g_low], add_scaled, False, fill=[xs1])
        with ExitStack() as c:
            k.slots1, k.gates1 = sb(c, "slots1", [P, NT, K1], U32), sb(c, "gates1", [P, NT, K1], F32)
            k.owner1, k.xring = sb(c, "owner1", [P, NT1], I32), sb(c, "xring", [P, 2, 4, D], F32)
            spreads(k, "p7a")
            route1(k, a["router1"], a["bias1"], xs1)
            experts1(k, a["experts1"], a["b1"], a["b2"], xs1, y1)
            combine(k, "p9", y1, k.slots1, k.gates1, K1, out=out)


def kernel(**inputs):
    import concourse.bacc as bacc
    from concourse.bass_utils import run_bass_kernel_spmd

    i = {name: np.asarray(v) for name, v in inputs.items()}
    chunks = lambda w: w.transpose(0, 2, 1).reshape(w.shape[0], DC, P, -1).transpose(0, 2, 1, 3).reshape(w.shape[0], P, -1)
    swiglu = lambda g, u, d: np.concatenate([chunks(i[g]), chunks(i[u]), i[d].transpose(0, 2, 1)], axis=2)
    w1, w2 = i["L1_ffn_W1"], i["L1_ffn_W2"]
    arrays = {
        "x": i["x"],
        "adj": i["adj"],
        "adj_t": i["adj"].T,
        "gnn0_t": i["L0_gnn_weight"].T,
        "router0_t": i["L0_ffn_router_w"].T,
        "bias0": i["L0_ffn_bias"],
        "shared0": swiglu("L0_ffn_shared_w_gate", "L0_ffn_shared_w_up", "L0_ffn_shared_w_down"),
        "experts0": swiglu("L0_ffn_w_gate", "L0_ffn_w_up", "L0_ffn_w_down"),
        "gnn1": i["L1_gnn_weight"],
        "gnn1_bias": i["L1_gnn_bias"],
        "router1": i["L1_ffn_Wr"],
        "bias1": i["L1_ffn_br"],
        "experts1": np.concatenate([
            w1.reshape(E1, DC, P, F1).transpose(0, 2, 1, 3).reshape(E1, P, -1),
            w2.reshape(E1, FB1, P, D).transpose(0, 2, 1, 3).reshape(E1, P, -1)], axis=2),
        "b1": i["L1_ffn_b1"].reshape(E1, FB1, P).transpose(0, 2, 1),
        "b2": i["L1_ffn_b2"],
    }
    arrays = {f"in_{n}": np.ascontiguousarray(v) for n, v in arrays.items()}
    nc = bacc.Bacc("TRN2", target_bir_lowering=False, num_devices=1)
    aps = {n[3:]: nc.dram_tensor(n, v.shape, mybir.dt.from_np(v.dtype), kind="ExternalInput").ap() for n, v in arrays.items()}
    out = nc.dram_tensor("out", (N, D), F32, kind="ExternalOutput").ap()
    build(nc, aps, out)
    r = run_bass_kernel_spmd(nc, [arrays], core_ids=[0])
    return r.results[0]["out"]
```

```python
from contextlib import ExitStack

import numpy as np
import concourse.bass as bass
from concourse import mybir

F32 = mybir.dt.float32
F32R = mybir.dt.float32r
BF16 = mybir.dt.bfloat16
I32 = mybir.dt.int32
U32 = mybir.dt.uint32
ACT = mybir.ActivationFunctionType
ALU = mybir.AluOpType
AX = mybir.AxisListType
ds = bass.ds

P = 128
N, D = 4096, 256
NT = N // P
DC = D // P
EPS = 1e-5

E0, F0, K0 = 64, 128, 6
CAP = N * K0 * 2 // E0
RPP = CAP // P
HALF = CAP // 2
SPAN = CAP + P
SLOTS0 = E0 * SPAN + 2 * P
UNITS0 = 2 * E0
UG = 4
LISTED = UNITS0 + UG
RESULTS0 = E0 * CAP
SKIP = 1 << 17
E1, F1, K1 = 8, 1024, 2
FB1 = F1 // P
T1 = 256
NT1 = N * K1 // T1 + E1
LISTED1 = NT1 + 1
SLOTS1 = LISTED1 * T1

QW = 1024
NQ = N // QW
JS = 2
STEPS = NT // JS
RAW = 4
GR = STEPS // RAW
GT = QW // P


class Kernel:

    def __init__(self, nc, ctx):
        self.nc, self.ctx = nc, ctx
        self.passed = nc.alloc_semaphore(name="passed")
        self.sems = []

    def sem(self, name):
        s = self.nc.alloc_semaphore(name=name)
        self.sems.append(s)
        return s

    def clear_semaphores(self):
        self.nc.clear_and_free_semaphores(self.sems)
        self.nc.all_engine_barrier()
        self.sems = []


def wait_apart(eng, sem, value, passed):
    if not (isinstance(value, int) and value <= 0):
        eng.wait_ge(sem, value)
        eng.sem_inc(passed, 1)


def wait_from(eng, sem, value):
    if not (isinstance(value, int) and value <= 0):
        eng.wait_ge(sem, value)


def passes(eng, count):
    yield 0
    with eng.Fori(1, count) as it:
        yield it


def make_constants(k):
    nc, c = k.nc, k.ctx
    sb = lambda n, s, d: c.enter_context(nc.sbuf_tensor(n, s, d))
    k.ident = sb("ident", [P, P], F32)
    k.identb = sb("identb", [P, P], BF16)
    k.tri = sb("tri", [P, P], BF16)
    k.onesb = sb("onesb", [P, P], BF16)
    k.iota = sb("iota", [P, E0], F32)
    k.x = sb("x", [P, NT, D], F32)
    k.deg = sb("deg", [P, NT], F32)
    k.dinv = sb("dinv", [P, NT], F32)
    k.minus_half = sb("minus_half", [P, NT], F32)


def sign_features(k, x_in, w_t):
    nc = k.nc
    G = NT // GT
    with ExitStack() as c:
        sb = lambda n, s, d: c.enter_context(nc.sbuf_tensor(n, s, d))
        ps = lambda n, s, d: c.enter_context(nc.psum_tensor(n, s, d))
        w_raw = sb("p1_w", [P, DC, D], F32)
        neg = sb("p1_neg", [P, DC, D], F32)
        sign_w = sb("p1_sign_w", [P, DC, D], BF16)
        total = sb("p1_total", [P, NT], F32)
        mean = sb("p1_mean", [P, NT], F32)
        pos = sb("p1_pos", [P, 2, GT, D], BF16)
        pos_t = sb("p1_pos_t", [P, 2, DC, GT * P], BF16)
        t_ps = ps("p1_t_ps", [P, 2, DC, GT * P], BF16)
        xw_ps = ps("p1_xw_ps", [P, GT, D], F32)
        x_loaded, w_sem, consts, fill = [k.sem(f"x_loaded{g}") for g in range(G)], k.sem("p1_w_loaded"), k.sem("consts"), k.sem("p1_fill")
        signed, summed, averaged, positive = k.sem("p1_signed"), k.sem("p1_summed"), k.sem("p1_averaged"), k.sem("p1_positive")
        turned, turned_out, multiplied, xw_out = k.sem("p1_turned"), k.sem("p1_turned_out"), k.sem("p1_multiplied"), k.sem("p1_xw_out")

        with nc.Block() as block:
            @block.sync
            def _(sp):
                sp.dma_start(w_raw[:], w_t.rearrange("(c p) o -> p c o", p=P)).then_inc(w_sem, 16)
                for g in range(G):
                    sp.dma_start(k.x[:, g * GT:(g + 1) * GT, :],
                                 x_in[g * GT * P:(g + 1) * GT * P, :].rearrange("(t p) d -> p t d", p=P)).then_inc(x_loaded[g], 16)

            @block.gpsimd
            def _(pool):
                pool.memset(k.ident[:], 0.0).then_inc(fill, 1)
                pool.memset(k.identb[:], 0.0).then_inc(fill, 1)
                pool.memset(k.tri[:], 0.0).then_inc(fill, 1)
                pool.memset(k.onesb[:], 1.0).then_inc(consts, 1)
                pool.memset(k.minus_half[:], -0.5).then_inc(consts, 1)
                pool.iota(k.iota[:], pattern=[[1, E0]], base=0, channel_multiplier=0,
                          allow_small_or_imprecise_dtypes=True).then_inc(consts, 1)
                pool.wait_ge(fill, 3)
                for m in (k.ident, k.identb):
                    pool.affine_select(out=m[:], in_=m[:], compare_op=ALU.not_equal, fill=1.0, base=0,
                                       pattern=[[-1, P]], channel_multiplier=1).then_inc(consts, 1)
                pool.affine_select(out=k.tri[:], in_=k.tri[:], compare_op=ALU.is_ge, fill=1.0, base=0,
                                   pattern=[[-1, P]], channel_multiplier=1).then_inc(consts, 1)

            @block.vector
            def _(dve):
                dve.wait_ge(w_sem, 16)
                dve.tensor_scalar(neg[:], w_raw[:], 0.0, None, ALU.is_lt).then_inc(signed, 1)
                dve.wait_ge(signed, 1)
                dve.scalar_tensor_tensor(out=sign_w[:], in0=w_raw[:], scalar=0.0, in1=neg[:],
                                         op0=ALU.is_gt, op1=ALU.subtract).then_inc(signed, 1)
                for g in range(G):
                    tiles = slice(g * GT, (g + 1) * GT)
                    dve.wait_ge(x_loaded[g], 16)
                    dve.tensor_reduce(total[:, tiles], k.x[:, tiles, :], AX.X, ALU.add).then_inc(summed, 1)
                    dve.wait_ge(summed, g + 1)
                    dve.tensor_scalar(mean[:, tiles], total[:, tiles], 1.0 / D, None, ALU.mult).then_inc(averaged, 1)
                    dve.wait_ge(averaged, g + 1)
                    if g >= 2:
                        dve.wait_ge(turned, g - 1)
                    dve.tensor_tensor(pos[:, g % 2, :, :], k.x[:, tiles, :], mean[:, tiles, None].to_broadcast([P, GT, D]), ALU.is_gt).then_inc(positive, 1)

            @block.tensor
            def _(pe):
                def turn(g):
                    pe.wait_ge(positive, g + 1)
                    if g >= 2:
                        pe.wait_ge(turned_out, g - 1)
                    for t in range(GT):
                        for d in range(DC):
                            m = pe.transpose(t_ps[:, g % 2, d, t * P:(t + 1) * P], pos[:, g % 2, t, d * P:(d + 1) * P], k.identb[:])
                    m.then_inc(turned, 1)

                pe.wait_ge(consts, 6)
                pe.wait_ge(signed, 2)
                turn(0)
                for g in range(G):
                    if g + 1 < G:
                        turn(g + 1)
                    pe.wait_ge(turned_out, g + 1)
                    if g:
                        pe.wait_ge(xw_out, g)
                    for t in range(GT):
                        for d in range(DC):
                            m = pe.matmul(xw_ps[:, t, :], pos_t[:, g % 2, d, t * P:(t + 1) * P], sign_w[:, d, :],
                                          start=(d == 0 and t % 2 == 0), stop=(d == DC - 1), skip_group_check=True)
                    m.then_inc(multiplied, 1)

            @block.scalar
            def _(act):
                def out_turned(g):
                    act.wait_ge(turned, g + 1)
                    act.activation(pos_t[:, g % 2, :, :], t_ps[:, g % 2, :, :], ACT.Copy).then_inc(turned_out, 1)

                out_turned(0)
                for g in range(G):
                    if g + 1 < G:
                        out_turned(g + 1)
                    act.wait_ge(multiplied, g + 1)
                    act.activation(k.xw[:, g * GT:(g + 1) * GT, :], xw_ps[:], ACT.Copy).then_inc(xw_out, 1)


def gnn(k, name, graph, features, finish, sum_degrees, fill=None, acc=None):
    nc = k.nc
    Q0 = 0 if acc is None else 1
    PARTS = 4
    SLOTS = 2 if len(features) > 1 else RAW
    passes = [(f, part) for f in range(len(features)) for part in range(2) if f + part < 2]
    with ExitStack() as c:
        sb = lambda n, s, d: c.enter_context(nc.sbuf_tensor(f"{name}_{n}", s, d))
        ps = lambda n, s, d: c.enter_context(nc.psum_tensor(f"{name}_{n}", s, d))
        sem = lambda n: k.sem(f"{name}_{n}")
        raw = sb("raw", [P, SLOTS, JS, QW], F32)
        high = sb("high", [P, PARTS, JS, QW], F32R)
        low = sb("low", [P, PARTS, JS, QW], F32R)
        out_t = sb("out_t", [P, DC, QW], F32)
        sums = sb("sums", [P, NT, NQ], F32) if sum_degrees else None
        junk = sb("junk", [P, 2, QW], BF16) if sum_degrees else None
        if fill is not None:
            ZR = 6
            zero = sb("zero", [P, ZR * D], F32)
            zero_set, zero_stored = sem("zero_set"), sem("zero_stored")
        neg, squares, var, square_junk = sb("neg", [P, NT], F32), sb("squares", [P, NT], F32), sb("var", [P, NT], F32), sb("square_junk", [P, GT, D], BF16)
        row_summed, averaged, meant, squared, scaled, rooted = [
            sem(n) for n in ("row_summed", "averaged", "meant", "squared", "scaled", "rooted")]
        halves = [ps("acc0", [P, 4, 512], F32) if acc is None else acc, ps("acc1", [P, 4, 512], F32)]
        loaded = [sem(f"loaded{s}") for s in range(RAW)]
        summed, low_done, multiplied = sem("summed"), sem("low_done"), sem("multiplied")
        high_done, taken, turned, finished = sem("high_done"), sem("taken"), sem("turned"), sem("finished")
        if sum_degrees:
            halfway = sem("halfway")

        with nc.Block() as block:
            @block.sync
            def _(sp):
                with sp.Fori(Q0, NQ) as q, sp.Fori(0, GR) as g:
                    for s in range(RAW):
                        sp.wait_ge(low_done, (q * GR + g) * RAW + (s + 1 - Q0 * STEPS))
                        if sum_degrees:
                            sp.wait_ge(summed, (q * GR + g) * RAW + (s + 1))
                        sp.dma_start(raw[:, s % SLOTS, :, :],
                                     graph.rearrange("(j p) i -> p j i", p=P)[:, ds((g * RAW + s) * JS, JS), ds(q * QW, QW)]
                                     ).then_inc(loaded[s], 16)

            @block.scalar
            def _(act):
                def square_rows(q):
                    act.wait_ge(averaged, q + 1)
                    if q:
                        act.wait_ge(squared, q * GT)
                    for t in range(GT):
                        tile = q * GT + t
                        act.activation(square_junk[:, t, :], k.x[:, tile, :], ACT.Square, bias=neg[:, tile:tile + 1],
                                       accum_out=squares[:, tile:tile + 1]).then_inc(squared, 1)

                if sum_degrees:
                    act.sem_inc(summed, RAW)
                for q in range(NQ - Q0):
                    with act.Fori(0, GR) as g:
                        for s in range(RAW):
                            act.wait_ge(loaded[s], (g + (q * GR + 1)) * 16)
                            act.wait_ge(multiplied, g * RAW + (q * STEPS + s + 1))
                            act.activation(high[:, s % PARTS, :, :], raw[:, s % SLOTS, :, :], ACT.Copy).then_inc(high_done, 1)
                            if sum_degrees:
                                act.wait_ge(summed, g * RAW + (q * STEPS + s + RAW - 1))
                                act.activation(junk[:, s % 2, :], raw[:, s % SLOTS, 0, :], ACT.Copy,
                                               accum_out=sums[:, ds(g * (RAW * JS) + s * JS, 1), q]).then_inc(summed, 1)

                    if q + Q0:
                        square_rows(q + Q0 - 1)
                square_rows(NQ - 1)

            @block.vector
            def _(dve):
                dve.sem_inc(low_done, SLOTS)

                def take_quarter(q):
                    if q >= Q0:
                        dve.wait_ge(multiplied, PARTS + (q - Q0 + 1) * STEPS)
                    if q:
                        dve.wait_ge(turned, q)
                    half = halves[q % 2][:].rearrange("p (d b) n -> p d (b n)", d=DC)
                    if sum_degrees:
                        dve.tensor_scalar(out_t[:], half, 0.0, None, ALU.max).then_inc(taken, 1)
                    else:
                        dve.tensor_copy(out_t[:], half).then_inc(taken, 1)

                def finish_quarter(q):
                    dve.wait_ge(turned, q + 1)
                    finish(dve, q, halves[q % 2][:].rearrange("p b (t d) -> p (b t) d", d=D), finished)

                def average(q):
                    tiles = slice(q * GT, (q + 1) * GT)
                    dve.wait_ge(finished, q + 1)
                    dve.tensor_reduce(k.mean[:, tiles], k.x[:, tiles, :], AX.X, ALU.add).then_inc(row_summed, 1)
                    dve.wait_ge(row_summed, q + 1)
                    dve.tensor_scalar(neg[:, tiles], k.mean[:, tiles], -1.0 / D, None, ALU.mult).then_inc(averaged, 1)
                    dve.wait_ge(averaged, q + 1)
                    dve.tensor_scalar(k.mean[:, tiles], neg[:, tiles], -1.0, None, ALU.mult).then_inc(meant, 1)

                def variance(q):
                    tiles = slice(q * GT, (q + 1) * GT)
                    dve.wait_ge(squared, (q + 1) * GT)
                    dve.tensor_scalar(var[:, tiles], squares[:, tiles], 1.0 / D, EPS, ALU.mult, ALU.add).then_inc(scaled, 1)

                def low_parts(q, g, s, n):
                    if sum_degrees:
                        dve.wait_ge(loaded[s], (g + q * GR) * 16 + 16)
                        dve.tensor_reduce(sums[:, ds(g * (RAW * JS) + (s * JS + 1), 1), q], raw[:, s % SLOTS, 1, :], AX.X, ALU.add).then_inc(halfway, 1)
                    dve.wait_ge(high_done, n + 1)
                    m = dve.tensor_tensor(low[:, s % PARTS, :, :], raw[:, s % SLOTS, :, :], high[:, s % PARTS, :, :].bitcast(F32), ALU.subtract)
                    m.then_inc(low_done, 1)

                for q in range(Q0, NQ):
                    if q:
                        for g, then in ((0, take_quarter), (1, finish_quarter), (2, average)):
                            for s in range(RAW):
                                low_parts(q, g, s, g * RAW + (q - Q0) * STEPS + s)
                            if g == 0 and q >= 2:
                                variance(q - 2)
                            then(q - 1)
                    with dve.Fori(3 if q else 0, GR) as g:
                        for s in range(RAW):
                            low_parts(q, g, s, g * RAW + ((q - Q0) * STEPS + s))
                take_quarter(NQ - 1)
                finish_quarter(NQ - 1)
                average(NQ - 1)
                variance(NQ - 2)
                variance(NQ - 1)
                if sum_degrees:
                    dve.wait_ge(summed, RAW + NQ * STEPS)
                    dve.wait_ge(halfway, NQ * STEPS)
                    dve.tensor_reduce(k.deg[:], sums[:], AX.X, ALU.add).then_inc(finished, 1)

            @block.tensor
            def _(pe):
                def turn_back(q):
                    pe.wait_ge(taken, q + 1)
                    rows = halves[q % 2][:].rearrange("p b (t d) -> p (b t) d", d=D)
                    for t in range(GT):
                        for d in range(DC):
                            m = pe.transpose(rows[:, t, d * P:(d + 1) * P], out_t[:, d, t * P:(t + 1) * P], k.ident[:])
                    m.then_inc(turned, 1)

                pe.sem_inc(multiplied, PARTS)
                for q in range(Q0, NQ):
                    if q >= 2:
                        pe.wait_ge(finished, q - 1)
                    for n in range(STEPS):
                        pe.wait_ge(low_done, SLOTS + (q - Q0) * STEPS + n + 1)
                        for j in range(JS):
                            for d in range(DC):
                                for i, (f, part) in enumerate(passes):
                                    graph_part = (high, low)[part]
                                    for b in range(2):
                                        m = pe.matmul(halves[q % 2][:, d * 2 + b, :],
                                                      features[f][:, n * JS + j, d * P:(d + 1) * P],
                                                      graph_part[:, n % PARTS, j, b * 512:(b + 1) * 512],
                                                      start=(n == 0 and j == 0 and i == 0),
                                                      stop=(n == STEPS - 1 and j == JS - 1 and i == len(passes) - 1),
                                                      skip_group_check=True)
                        m.then_inc(multiplied, 1)
                        if n == 5 and q:
                            turn_back(q - 1)
                turn_back(NQ - 1)

            @block.gpsimd
            def _(pool):
                if fill is not None:
                    pool.memset(zero[:], 0.0).then_inc(zero_set, 1)
                    pool.wait_ge(zero_set, 1)
                    n = 0
                    for target in fill:
                        rows = target.shape[0]
                        while rows:
                            r = min(rows // P, ZR)
                            pool.dma_start(target[target.shape[0] - rows:target.shape[0] - rows + r * P, :].rearrange("(p r) d -> p (r d)", p=P),
                                           zero[:, 0:r * D]).then_inc(zero_stored, 16)
                            rows -= r * P
                            n += 1
                    pool.wait_ge(zero_stored, 16 * n)
                for q in range(NQ):
                    tiles = slice(q * GT, (q + 1) * GT)
                    pool.wait_ge(scaled, q + 1)
                    pool.tensor_tensor(k.rstd[:, tiles], var[:, tiles], k.minus_half[:, tiles], ALU.pow).then_inc(rooted, 1)



def route0(k, router_t, bias, shared, xs0, y0):
    nc = k.nc
    GTR = 4
    TOK = GTR * P
    KG = K0 * GTR
    with ExitStack() as c:
        sb = lambda n, s, d: c.enter_context(nc.sbuf_tensor(f"p3_{n}", s, d))
        ps = lambda n, s, d: c.enter_context(nc.psum_tensor(f"p3_{n}", s, d))
        sem = lambda n: k.sem(f"p3_{n}")
        wr = sb("wr", [P, DC, E0], F32)
        bias_sb = sb("bias", [P, E0], F32)
        wsh = sb("wsh", [P, 2, 3 * D], F32)
        counted, halves, step = sb("counted", [P, E0 + 1], F32), sb("halves", [P, E0], F32), sb("step", [P, E0], F32)
        ends = [sb(f"ends{i}", [P, E0 + 1], F32) for i in range(2)]
        ordinal, beyond = sb("ordinal", [P, LISTED], F32), sb("beyond", [P, LISTED, E0], F32)
        code, same, none = sb("code", [P, LISTED + 1], F32), sb("same", [P, LISTED], F32), sb("none", [P, LISTED], F32)
        group_end, group_end_i = sb("group_end", [P, 1], F32), sb("group_end_i", [P, 1], I32)
        xn = sb("xn", [P, 2, GTR, D], F32)
        xt = sb("xt", [P, 2, DC, TOK], F32)
        lg = sb("lg", [P, GTR, E0], F32)
        top = sb("top", [P, GTR, 8], F32)
        topi = sb("topi", [P, GTR, 8], U32)
        idx = sb("idx", [P, K0, GTR], F32)
        onehot = sb("onehot", [P, K0, GTR, E0], F32)
        prod = sb("prod", [P, K0, GTR, E0], F32)
        mask = sb("mask", [P, GTR, E0], BF16)
        before = sb("before", [P, GTR + 1, E0], BF16)
        rank = sb("rank", [P, K0, GTR], F32)
        slot = sb("slot", [P, K0, GTR], F32)
        full = sb("full", [P, K0, GTR], F32)
        where = sb("where", [P, K0, GTR], F32)
        slot_i = sb("slot_i", [P, 2, K0, GTR], U32)
        sg = sb("sg", [P, 2, TOK], F32)
        hid = sb("hid", [P, 2, TOK], F32)
        t_ps, lg_ps, rank_ps = ps("t_ps", [P, DC, TOK], F32), ps("lg_ps", [P, 512], F32), ps("rank_ps", [P, 512], F32)
        gate_ps, up_ps, down_ps = ps("gate_ps", [P, TOK], F32), ps("up_ps", [P, TOK], F32), ps("down_ps", [P, GTR, D], F32)
        lgv = lg_ps[:, 0:GTR * E0].rearrange("p (t e) -> p t e", e=E0)
        rkv = rank_ps[:, 0:GTR * E0].rearrange("p (t e) -> p t e", e=E0)
        w_loaded, zeroed, zero_out = sem("w_loaded"), sem("zeroed"), sem("zero_out")
        normed, turned, xt_out, logged, ranked, scored = sem("normed"), sem("turned"), sem("xt_out"), sem("logged"), sem("ranked"), sem("scored")
        gated, silu_out, hidden, lowered, shared_in = sem("gated"), sem("silu_out"), sem("hidden"), sem("lowered"), sem("shared_in")
        chain, maxed, slotted, placed, scattered = sem("chain"), sem("maxed"), sem("slotted"), sem("placed"), [sem("scattered0"), sem("scattered1")]
        totals, numbered, rows_known, padded = sem("totals"), sem("numbered"), sem("rows_known"), sem("padded")
        NG = NT // GTR
        LINKS = 11 + GTR
        MASKED = 5 + GTR

        def last(r, j):
            return isinstance(r, int) and r * 2 + j == NG - 1

        def pad(eng, first):
            eng.wait_ge(rows_known, 2)
            with eng.Fori(0, E0 // 2) as i:
                rows = eng.value_load(k.rows0[0:1, ds(i * 2 + first, 1)], min_val=0, max_val=CAP)
                eng.dma_start(xs0[ds((i * 2 + first) * SPAN + rows, P), :], k.zrow[:, 0, :]).then_inc(padded, 16)

        with nc.Block() as block:
            @block.sync
            def _(sp):
                sp.dma_start(wr[:], router_t.rearrange("(c p) e -> p c e", p=P)).then_inc(w_loaded, 16)
                sp.dma_start(bias_sb[:], bias.rearrange("(a e) -> a e", a=1).to_broadcast([P, E0])).then_inc(w_loaded, 16)
                sp.dma_start(wsh[:], shared.rearrange("s p n -> p s n")).then_inc(w_loaded, 16)
                sp.wait_ge(zeroed, 1)
                for i in range(HALF // P):
                    sp.dma_start(y0[RESULTS0 + i * P:RESULTS0 + (i + 1) * P, :], k.zrow[:, 0, :]).then_inc(zero_out, 16)
                sp.wait_ge(zero_out, HALF // P * 16)
                pad(sp, 0)
                sp.wait_ge(padded, E0 * 16)

            @block.vector
            def _(dve):
                dve.memset(k.zrow[:], 0.0).then_inc(zeroed, 1)
                dve.memset(before[:, GTR, :], 0.0).then_inc(zeroed, 1)
                dve.wait_ge(zeroed, 2)
                dve.wait_ge(w_loaded, 48)

                def layer_norm(r, j):
                    wait_apart(dve, scattered[j], r * (16 * KG), k.passed)
                    for t in range(GTR):
                        tile = (r * 2 + j) * GTR + t
                        dve.tensor_scalar(xn[:, j, t, :], k.x[:, tile, :], k.mean[:, ds(tile, 1)], k.rstd[:, ds(tile, 1)],
                                          ALU.subtract, ALU.mult).then_inc(normed, 1)

                def linker(links):
                    count = 0

                    def link(ins):
                        nonlocal count
                        count += 1
                        ins.then_inc(chain, 1)
                        dve.wait_ge(chain, links + count)
                    return link, lambda: count

                def choose(r, j):
                    n = r * 2 + j
                    link, count = linker(n * LINKS)
                    dve.wait_ge(logged, n + 1)
                    link(dve.tensor_tensor(lg[:], lgv, bias_sb[:, None, :].to_broadcast([P, GTR, E0]), ALU.add))
                    dve.tensor_copy(k.logits0[:, ds(n * GTR, GTR), :], lg[:]).then_inc(scored, 1)
                    for t in range(GTR):
                        dve.max(top[:, t, :], lg[:, t, :]).then_inc(maxed, 1)
                    wait_apart(dve, maxed, n * (2 * GTR) + GTR, k.passed)
                    for t in range(GTR):
                        dve.max_index(topi[:, t, :], top[:, t, :], lg[:, t, :]).then_inc(maxed, 1)
                    dve.tensor_copy(k.tops0[:, ds(n * GTR, GTR), :], top[:, :, 0:K0]).then_inc(scored, 1)
                    dve.wait_ge(maxed, (n + 1) * (2 * GTR))
                    link(dve.tensor_copy(idx[:], topi[:, :, 0:K0].rearrange("p t k -> p k t")))
                    link(dve.tensor_tensor(onehot[:], k.iota[:, None, None, :].to_broadcast([P, K0, GTR, E0]),
                                           idx[:, :, :, None].to_broadcast([P, K0, GTR, E0]), ALU.is_equal))
                    with nc.allow_low_precision(reason="zeros and ones are exact"):
                        link(dve.tensor_reduce(mask[:], onehot[:].rearrange("p k t e -> p t e k"), AX.X, ALU.add))
                    link(dve.tensor_copy(before[:, 0, :], before[:, GTR, :]))
                    for t in range(GTR):
                        link(dve.tensor_tensor(before[:, t + 1, :], before[:, t, :], mask[:, t, :], ALU.add))
                    assert count() == MASKED

                def place(r, j):
                    n = r * 2 + j
                    link, count = linker(n * LINKS + MASKED)
                    dve.wait_ge(ranked, n + 1)
                    link(dve.tensor_tensor(prod[:], onehot[:], rkv[:, None, :, :].to_broadcast([P, K0, GTR, E0]), ALU.mult))
                    link(dve.tensor_reduce(rank[:], prod[:], AX.X, ALU.add))
                    link(dve.tensor_scalar(full[:], rank[:], float(CAP), float(SKIP), ALU.is_ge, ALU.mult))
                    link(dve.tensor_tensor(rank[:], rank[:], full[:], ALU.add))
                    link(dve.scalar_tensor_tensor(out=slot[:], in0=idx[:], scalar=float(SPAN), in1=rank[:], op0=ALU.mult, op1=ALU.add))
                    dve.tensor_copy(slot_i[:, j, :, :], slot[:]).then_inc(slotted, 1)
                    link(dve.scalar_tensor_tensor(out=where[:], in0=idx[:], scalar=float(CAP), in1=rank[:], op0=ALU.mult, op1=ALU.add))
                    assert count() == LINKS - MASKED
                    dve.tensor_scalar(k.slots0[:, ds(n * GTR, GTR), :].rearrange("p t k -> p k t"), where[:], float(RESULTS0), None, ALU.min).then_inc(placed, 1)

                def hide(r, j, h):
                    n = r * 2 + j
                    dve.wait_ge(silu_out, n * 2 + (h + 1))
                    wait_from(dve, lowered, n)
                    dve.tensor_tensor(hid[:, h, :], sg[:, h, :], up_ps[:], ALU.mult).then_inc(hidden, 1)

                def add_shared(r, j):
                    n = r * 2 + j
                    dve.wait_ge(lowered, n + 1)
                    dve.scalar_tensor_tensor(out=k.x[:, ds(n * GTR, GTR), :], in0=down_ps[:], scalar=0.5, in1=k.x[:, ds(n * GTR, GTR), :],
                                             op0=ALU.mult, op1=ALU.add).then_inc(shared_in, 1)

                layer_norm(0, 0)
                for r, j in units(dve, NG, 2):
                    choose(r, j)
                    if not (isinstance(r, int) and r * 2 + j == 0):
                        add_shared(*moved(r, j, -1, 2))
                    place(r, j)
                    hide(r, j, 0)
                    if not last(r, j):
                        layer_norm(*moved(r, j, 1, 2))
                    hide(r, j, 1)
                    if last(r, j):
                        dve.wait_ge(totals, 1)
                        dve.tensor_scalar(counted[:, 0:E0], rank_ps[:, 0:E0], float(CAP), None, ALU.min).then_inc(rows_known, 1)
                        dve.wait_ge(rows_known, 1)
                        dve.tensor_copy(k.rows0[:], counted[:, 0:E0]).then_inc(rows_known, 1)
                add_shared(NG // 2 - 1, 1)
                ONE = 4096
                steps = NG * LINKS

                def link2(*instructions):
                    nonlocal steps
                    for ins in instructions:
                        ins.then_inc(chain, 1)
                    steps += len(instructions)
                    dve.wait_ge(chain, steps)

                link2(dve.memset(counted[:, E0:], 0.0),
                      dve.memset(ends[0][:, 0:1], 0.0), dve.memset(ends[1][:, 0:1], 0.0), dve.memset(code[:, 0:1], -1.0))
                link2(dve.tensor_scalar(halves[:], counted[:, 0:E0], 0.0, None, ALU.is_gt),
                      dve.scalar_tensor_tensor(out=step[:], in0=counted[:, 1:], scalar=float(ONE), in1=counted[:, 0:E0], op0=ALU.add, op1=ALU.subtract))
                link2(dve.scalar_tensor_tensor(out=ends[0][:, 1:], in0=counted[:, 0:E0], scalar=float(HALF), in1=halves[:], op0=ALU.is_gt, op1=ALU.add))
                for b in range(6):
                    u, v, by = ends[b % 2], ends[(b + 1) % 2], 1 << b
                    link2(dve.tensor_copy(v[:, 1:1 + by], u[:, 1:1 + by]),
                          dve.tensor_tensor(v[:, 1 + by:], u[:, 1 + by:], u[:, 1:E0 + 1 - by], ALU.add))
                dve.wait_ge(numbered, 1)
                link2(dve.tensor_tensor(beyond[:], ordinal[:, :, None].to_broadcast([P, LISTED, E0]),
                                        ends[0][:, None, 1:].to_broadcast([P, LISTED, E0]), ALU.is_ge),
                      dve.tensor_scalar(group_end[:], ends[0][:, E0:E0 + 1], -1.0, None, ALU.add))
                link2(dve.tensor_tensor(beyond[:], beyond[:], step[:, None, :].to_broadcast([P, LISTED, E0]), ALU.mult),
                      dve.tensor_copy(group_end_i[:], group_end[:]))
                dve.tensor_single_scalar(k.last_group0[:], group_end_i[:], UG.bit_length() - 1, ALU.arith_shift_right)
                link2(dve.tensor_reduce(code[:, 1:], beyond[:], AX.X, ALU.add))
                link2(dve.tensor_tensor(same[:], code[:, 1:], code[:, 0:LISTED], ALU.is_equal))
                link2(dve.tensor_scalar(code[:, 1:], code[:, 1:], counted[:, 0:1], None, ALU.add))
                link2(dve.tensor_scalar(none[:], code[:, 1:], float(E0 * ONE), None, ALU.is_ge))
                link2(dve.tensor_tensor(same[:], same[:], none[:], ALU.max))
                link2(dve.scalar_tensor_tensor(out=code[:, 1:], in0=same[:], scalar=float(ONE // 4), in1=code[:, 1:], op0=ALU.mult, op1=ALU.add))
                link2(dve.scalar_tensor_tensor(out=code[:, 1:], in0=none[:], scalar=-3.0 * ONE / 4, in1=code[:, 1:], op0=ALU.mult, op1=ALU.add))
                dve.tensor_copy(k.units0[:], code[:, 1:])

            @block.scalar
            def _(act):
                def out_turned(r, j):
                    act.wait_ge(turned, r * 2 + (j + 1))
                    act.activation(xt[:, j, :, :], t_ps[:], ACT.Copy).then_inc(xt_out, 1)

                out_turned(0, 0)
                for r, j in units(act, NG, 2):
                    n = r * 2 + j
                    for h in range(2):
                        act.wait_ge(gated, n * 2 + (h + 1))
                        wait_from(act, hidden, n * 2)
                        act.activation(sg[:, h, :], gate_ps[:], ACT.Silu).then_inc(silu_out, 1)
                    if not last(r, j):
                        out_turned(*moved(r, j, 1, 2))
                pad(act, 1)

            @block.tensor
            def _(pe):
                def turn(r, j):
                    n = r * 2 + j
                    pe.wait_ge(normed, n * GTR + GTR)
                    wait_from(pe, xt_out, n)
                    for t in range(GTR):
                        for d in range(DC):
                            m = pe.transpose(t_ps[:, d, t * P:(t + 1) * P], xn[:, j, t, d * P:(d + 1) * P], k.ident[:])
                    m.then_inc(turned, 1)

                def logits(r, j):
                    n = r * 2 + j
                    pe.wait_ge(xt_out, n + 1)
                    wait_from(pe, scored, n * 2)
                    for t in range(GTR):
                        for d in range(DC):
                            m = pe.matmul(lgv[:, t, :], xt[:, j, d, t * P:(t + 1) * P], wr[:, d, :],
                                          start=(t == 0 and d == 0), stop=(d == DC - 1), skip_group_check=True)
                    m.then_inc(logged, 1)

                def lift(r, j, h):
                    wait_from(pe, hidden, (r * 2 + j) * 2 + h)
                    for (out, at) in ((gate_ps, 0), (up_ps, DC * F0)):
                        for d in range(DC):
                            m = pe.matmul(out[:], wsh[:, h, at + d * F0:at + (d + 1) * F0], xt[:, j, d, :],
                                          start=(d == 0), stop=(d == DC - 1))
                    m.then_inc(gated, 1)

                def ranks(r, j):
                    n = r * 2 + j
                    pe.wait_ge(chain, n * LINKS + MASKED)
                    wait_from(pe, placed, n)
                    pe.matmul(rank_ps[:, 0:GTR * E0], k.tri[:], mask[:].rearrange("p t e -> p (t e)"), start=True, stop=False)
                    pe.matmul(rank_ps[:, 0:GTR * E0], k.onesb[:], before[:, 0:GTR, :].rearrange("p t e -> p (t e)"),
                              start=False, stop=True).then_inc(ranked, 1)

                def lower(r, j):
                    n = r * 2 + j
                    pe.wait_ge(hidden, n * 2 + 2)
                    wait_from(pe, shared_in, n)
                    for t in range(GTR):
                        for h in range(2):
                            m = pe.matmul(down_ps[:, t, :], hid[:, h, t * P:(t + 1) * P], wsh[:, h, 2 * DC * F0:],
                                          start=(h == 0 and t % 2 == 0), stop=(h == 1), skip_group_check=True)
                    m.then_inc(lowered, 1)

                pe.wait_ge(w_loaded, 48)
                turn(0, 0)
                logits(0, 0)
                for r, j in units(pe, NG, 2):
                    lift(r, j, 0)
                    ranks(r, j)
                    lift(r, j, 1)
                    if not last(r, j):
                        turn(*moved(r, j, 1, 2))
                        logits(*moved(r, j, 1, 2))
                    else:
                        pe.wait_ge(placed, NG)
                        pe.matmul(rank_ps[:, 0:E0], k.onesb[:], before[:, GTR, :], start=True, stop=True).then_inc(totals, 1)
                    lower(r, j)

            @block.gpsimd
            def _(pool):
                pool.iota(ordinal[:], pattern=[[1, LISTED]], base=0, channel_multiplier=0, allow_small_or_imprecise_dtypes=True).then_inc(numbered, 1)
                for it in passes(pool, NG // 2):
                    for s in range(2):
                        n = it * 2 + s
                        wait_apart(pool, slotted, n + 1, k.passed)
                        for kk in range(K0):
                            for t in range(GTR):
                                pool.indirect_dma_start(xs0, bass.IndirectOffsetOnAxis(ap=slot_i[:, s, kk, t:t + 1], axis=0),
                                                        xn[:, s, t, :], None, bounds_check=SLOTS0 - 1, oob_is_err=False
                                                        ).then_inc(scattered[s], 16)
                for s in range(2):
                    pool.wait_ge(scattered[s], NG // 2 * KG * 16)


def units(eng, total, un):
    for j in range(un):
        yield 0, j
    with eng.Fori(1, total // un - 1) as it:
        for j in range(un):
            yield it, j
    for j in range(un):
        yield total // un - 1, j


def moved(r, j, by, un):
    return r + (j + by) // un, (j + by) % un


def split_products(pe, out, left, right, first, last):
    for n, (a, b) in enumerate(((0, 0), (0, 1), (1, 0))):
        m = pe.matmul(out, left[a], right[b], start=(first and n == 0), stop=(last and n == 2), skip_group_check=True)
    return m


def listed_units(eng, last, total=UNITS0):
    for j in range(UG):
        yield 0, j
    with eng.Fori(1, total // UG) as it:
        with eng.If(it <= last):
            for j in range(UG):
                yield it, j


def experts0(k, weights, xs0, y0):
    nc = k.nc
    RH = HALF // P
    WN = 3 * D
    LOADS = (1 + RH) * 16
    with ExitStack() as c:
        sb = lambda n, s, d: c.enter_context(nc.sbuf_tensor(f"p4_{n}", s, d))
        ps = lambda n, s, d: c.enter_context(nc.psum_tensor(f"p4_{n}", s, d))
        sem = lambda n: k.sem(f"p4_{n}")
        pair = lambda n, s: [sb(n + "_high", s, F32R), sb(n + "_low", s, F32R)]
        xe = sb("xe", [P, UG, RH, D], F32)
        we = sb("we", [P, UG, WN], F32)
        w = pair("w", [P, UG, WN])
        xt = pair("xt", [P, 2, DC, HALF])
        sg = sb("sg", [P, 2, HALF], F32)
        hid = sb("hid", [P, 2, HALF], F32)
        hid_parts = pair("hid_parts", [P, 2, HALF])
        ye = sb("ye", [P, UG, RH, D], F32)
        t_ps = ps("t_ps", [P, DC, 512], F32)
        gate_ps, up_ps = ps("gate_ps", [P, 2, 512], F32), ps("up_ps", [P, 2, 512], F32)
        down_ps = ps("down_ps", [P, 4, D], F32)
        loaded, stored = [[sem(f"{n}{s}") for s in range(UG)] for n in ("loaded", "stored")]
        turned, xt_high, xt_low, w_high, w_low, lifted, silu_out, hidden, hid_high, hid_low, lowered, y_out, cleared, zeros_out = [
            sem(n) for n in ("turned", "xt_high", "xt_low", "w_high", "w_low", "lifted", "silu_out", "hidden", "hid_high",
                             "hid_low", "lowered", "y_out", "cleared", "zeros_out")]
        xs_v = xs0.rearrange("(n p) d -> n p d", p=P)
        y_v = y0.rearrange("(n i p) d -> n p i d", i=RH, p=P)
        number = lambda r, j: r * UG + j
        after = lambda r, j: moved(r, j, 1, UG)
        second = lambda r, j: moved(r, j, 2, UG)

        def last_group(eng):
            return eng.value_load(k.last_group0[0:1, 0:1], min_val=0, max_val=UNITS0 // UG - 1)

        def unit(eng, m):
            code = eng.value_load(k.units0[0:1, ds(m, 1)], min_val=0, max_val=E0 * 4096 - 1)
            return (code >> 12).with_bounds(min_val=0, max_val=E0 - 1), ((code >> 10) & 3).with_bounds(min_val=0, max_val=2), (code & 1023).with_bounds(min_val=0, max_val=CAP)

        with nc.Block() as block:
            @block.sync
            def _(sp):
                last = last_group(sp)

                def load(r, j):
                    m = number(r, j)
                    e, half, rows = unit(sp, m)
                    if not isinstance(r, int) or r >= 1:
                        wait_apart(sp, turned, m - (UG - 1), k.passed)
                        wait_apart(sp, w_low, m - (UG - 1), k.passed)
                    sp.dma_start(we[:, j, :], weights[ds(e, 1), :, :].rearrange("a p n -> p (a n)")).then_inc(loaded[j], 16)
                    for i in range(RH):
                        sp.dma_start(xe[:, j, i, :], xs_v[ds(e * (SPAN // P) + half * RH + i, 1), :, :].rearrange("a p n -> p (a n)"),
                                     bounds_check="skip_entire_dma", cond=(rows > half * HALF + i * P)).then_inc(loaded[j], 16)

                sp.wait_ge(cleared, 1)
                load(0, 0)
                load(0, 1)
                for r, j in listed_units(sp, last):
                    load(*second(r, j))

            @block.tensor
            def _(pe):
                last = last_group(pe)

                def turn(r, j):
                    m = number(r, j)
                    pe.wait_ge(loaded[j], r * LOADS + LOADS)
                    wait_from(pe, xt_low, m)
                    for i in range(RH):
                        for d in range(DC):
                            t = pe.transpose(t_ps[:, d, i * P:(i + 1) * P], xe[:, j, i, d * P:(d + 1) * P], k.ident[:])
                    t.then_inc(turned, 1)

                def lift(r, j):
                    m = number(r, j)
                    pe.wait_ge(w_low, m + 1)
                    pe.wait_ge(xt_low, m + 1)
                    for out, w0 in ((gate_ps, 0), (up_ps, DC * F0)):
                        for d in range(DC):
                            t = split_products(pe, out[:, j % 2, 0:HALF], [a[:, j, w0 + d * F0:w0 + (d + 1) * F0] for a in w],
                                               [a[:, j % 2, d, :] for a in xt], d == 0, d == DC - 1)
                    t.then_inc(lifted, 1)

                def lower(r, j):
                    m = number(r, j)
                    pe.wait_ge(hid_low, m + 1)
                    wait_from(pe, y_out, m)
                    for i in range(RH):
                        t = split_products(pe, down_ps[:, i, :], [a[:, j % 2, i * P:(i + 1) * P] for a in hid_parts],
                                           [a[:, j, 2 * DC * F0:] for a in w], i % 2 == 0, True)
                    t.then_inc(lowered, 1)

                turn(0, 0)
                for r, j in listed_units(pe, last):
                    turn(*after(r, j))
                    lift(r, j)
                    if not (isinstance(r, int) and j == 0):
                        lower(*moved(r, j, -1, UG))
                lower(last, UG - 1)

            @block.vector
            def _(dve):
                dve.memset(xe[:], 0.0).then_inc(cleared, 1)
                last = last_group(dve)

                def low_turned(r, j):
                    dve.wait_ge(xt_high, number(r, j) + 1)
                    dve.tensor_tensor(xt[1][:, j % 2, :, :], t_ps[:, :, 0:HALF], xt[0][:, j % 2, :, :].bitcast(F32), ALU.subtract).then_inc(xt_low, 1)

                def low_weights(r, j):
                    dve.wait_ge(w_high, number(r, j) + 1)
                    dve.tensor_tensor(w[1][:, j, :], we[:, j, :], w[0][:, j, :].bitcast(F32), ALU.subtract).then_inc(w_low, 1)

                low_weights(0, 0)
                low_turned(0, 0)
                low_weights(0, 1)
                for r, j in listed_units(dve, last):
                    m = number(r, j)
                    low_turned(*after(r, j))
                    dve.wait_ge(silu_out, m + 1)
                    dve.tensor_tensor(hid[:, j % 2, :], sg[:, j % 2, :], up_ps[:, j % 2, 0:HALF], ALU.mult).then_inc(hidden, 1)
                    dve.wait_ge(hidden, m + 1)
                    dve.tensor_copy(hid_parts[0][:, j % 2, :], hid[:, j % 2, :]).then_inc(hid_high, 1)
                    dve.wait_ge(hid_high, m + 1)
                    dve.tensor_tensor(hid_parts[1][:, j % 2, :], hid[:, j % 2, :], hid_parts[0][:, j % 2, :].bitcast(F32), ALU.subtract).then_inc(hid_low, 1)
                    low_weights(*second(r, j))

            @block.scalar
            def _(act):
                last = last_group(act)

                def high_turned(r, j):
                    act.wait_ge(turned, number(r, j) + 1)
                    act.activation(xt[0][:, j % 2, :, :], t_ps[:, :, 0:HALF], ACT.Copy).then_inc(xt_high, 1)

                def high_weights(r, j):
                    act.wait_ge(loaded[j], r * LOADS + LOADS)
                    if not isinstance(r, int) or r >= 1:
                        act.wait_ge(lowered, number(r, j) - (UG - 1))
                    act.activation(w[0][:, j, :], we[:, j, :], ACT.Copy).then_inc(w_high, 1)

                def take_lowered(r, j):
                    act.wait_ge(lowered, number(r, j) + 1)
                    wait_from(act, stored[j], r * 16)
                    act.activation(ye[:, j, :, :], down_ps[:, 0:RH, :], ACT.Copy).then_inc(y_out, 1)

                high_weights(0, 0)
                high_turned(0, 0)
                high_weights(0, 1)
                for r, j in listed_units(act, last):
                    high_turned(*after(r, j))
                    high_weights(*second(r, j))
                    act.wait_ge(lifted, number(r, j) + 1)
                    act.activation(sg[:, j % 2, :], gate_ps[:, j % 2, 0:HALF], ACT.Silu).then_inc(silu_out, 1)
                    if not (isinstance(r, int) and j == 0):
                        take_lowered(*moved(r, j, -1, UG))
                take_lowered(last, UG - 1)

            @block.gpsimd
            def _(pool):
                last = last_group(pool)

                def zero(g):
                    for i in range(UG // 2):
                        e = g * (UG // 2) + i
                        rows = pool.value_load(k.rows0[0:1, ds(e, 1)], min_val=0, max_val=CAP)
                        for half in range(2):
                            pool.dma_start(y_v[ds(e * 2 + half, 1), :, :, :].rearrange("a p i n -> p (a i) n"), k.zrow[:],
                                           bounds_check="skip_entire_dma", cond=(rows < half * HALF + 1)).then_inc(zeros_out, 16)

                def store(r, j):
                    e, half, _ = unit(pool, number(r, j))
                    wait_apart(pool, y_out, number(r, j) + 1, k.passed)
                    pool.dma_start(y_v[ds(e * 2 + half, 1), :, :, :].rearrange("a p i n -> p (a i) n"), ye[:, j, :, :],
                                   bounds_check="skip_entire_dma", cond=(half < 2)).then_inc(stored[j], 16)

                zero(0)
                zero(1)
                for j in range(UG):
                    store(0, j)
                for begin, end in ((1, UNITS0 // UG // 2), (UNITS0 // UG // 2, UNITS0 // UG)):
                    with pool.Fori(begin, end) as it:
                        if begin == 1:
                            zero(it * 2)
                            zero(it * 2 + 1)
                        with pool.If(it <= last):
                            for j in range(UG):
                                store(it, j)
                for s in range(UG):
                    wait_apart(pool, stored[s], last * 16 + 16, k.passed)
                pool.wait_ge(zeros_out, UNITS0 * 16)


def combine_and_project(k, y, a, acc):
    nc = k.nc
    GTR = 4
    NG = NT // GTR
    SG = GTR // JS
    with ExitStack() as c:
        sb = lambda n, s, d: c.enter_context(nc.sbuf_tensor(f"p5_{n}", s, d))
        ps = lambda n, s, d: c.enter_context(nc.psum_tensor(f"p5_{n}", s, d))
        sem = lambda n: k.sem(f"p5_{n}")
        z = sb("z", [P, NT], F32)
        rows = sb("rows", [P, GTR, K0, D], F32)
        at_i = sb("at", [P, GTR, K0], U32)
        w, b = sb("w", [P, DC, D], F32), sb("b", [P, D], F32)
        neg, squares, junk, var = sb("neg", [P, NT], F32), sb("squares", [P, NT], F32), sb("junk", [P, GTR, D], F32), sb("var", [P, NT], F32)
        xn, xt, g32 = sb("xn", [P, GTR, D], F32), sb("xt", [P, DC, GTR * P], F32), sb("g32", [P, GTR, D], F32)
        raw, high, low = [sb(n, [P, SG, JS, QW], t) for n, t in (("raw", F32), ("high", F32R), ("low", F32R))]
        t_ps, h_ps = ps("t_ps", [P, DC, GTR * P], F32), ps("h_ps", [P, GTR, D], F32)
        shifted, exped, gated = sem("shifted"), sem("exped"), sem("gated")
        copied, gathered, added = sem("copied"), [sem(f"gathered{t}") for t in range(GTR)], sem("added")
        w_loaded, dinv_out, rstd_out = sem("w_loaded"), sem("dinv_out"), sem("rstd_out")
        summed, averaged, meant, squared, scaled, normed, biased = [
            sem(n) for n in ("summed", "averaged", "meant", "squared", "scaled", "normed", "biased")]
        turned, xt_out, projected, made, made_high, made_low = [
            sem(n) for n in ("turned", "xt_out", "projected", "made", "made_high", "made_low")]
        graph_loaded, graph_high, graph_low, multiplied = [sem(f"graph_loaded{i}") for i in range(SG)], sem("graph_high"), sem("graph_low"), sem("multiplied")

        def tiles(m):
            return ds(m * GTR, GTR)

        with nc.Block() as block:
            @block.sync
            def _(sp):
                sp.dma_start(w[:], a["gnn1"].rearrange("(c p) o -> p c o", p=P)).then_inc(w_loaded, 16)
                sp.dma_start(b[:], a["gnn1_bias"].rearrange("(a e) -> a e", a=1).to_broadcast([P, D])).then_inc(w_loaded, 16)
                for m in passes(sp, NG):
                    for i in range(SG):
                        if not isinstance(m, int):
                            sp.wait_ge(graph_low, m * SG + (i + 1 - SG))
                        sp.dma_start(raw[:, i, :, :],
                                     a["adj"].rearrange("(j p) i -> p j i", p=P)[:, ds((m * SG + i) * JS, JS), 0:QW]).then_inc(graph_loaded[i], 16)

            @block.gpsimd
            def _(pool):
                pool.tensor_tensor(k.dinv[:], k.deg[:], k.minus_half[:], ALU.pow).then_inc(dinv_out, 1)

                def gather(n, t):
                    if not isinstance(n, int):
                        wait_apart(pool, added, n * (GTR * K0) + (t // 2 * 2 + 2 - GTR) * K0, k.passed)
                    pool.tensor_copy(at_i[:, t, :], k.slots0[:, n * GTR + t, :]).then_inc(copied, 1)
                    wait_apart(pool, copied, n * GTR + (t + 1), k.passed)
                    for i in range(K0):
                        pool.indirect_dma_start(rows[:, t, i, :], None, y, bass.IndirectOffsetOnAxis(ap=at_i[:, t, i:i + 1], axis=0)
                                                ).then_inc(gathered[t], 16)

                def root(m):
                    wait_apart(pool, scaled, m + 1, k.passed)
                    pool.tensor_tensor(k.rstd[:, tiles(m)], var[:, tiles(m)], k.minus_half[:, 0:GTR], ALU.pow).then_inc(rstd_out, 1)

                for n in passes(pool, NG):
                    for t in range(GTR):
                        gather(n, t)
                        if t == 1 and not isinstance(n, int):
                            root(n - 1)
                root(NG - 1)

            @block.vector
            def _(dve):
                first = k.tops0[:, :, 0:1]
                shares = z[:, :, None].to_broadcast([P, NT, K0])
                dve.tensor_tensor(k.logits0[:], k.logits0[:], first.to_broadcast([P, NT, E0]), ALU.subtract).then_inc(shifted, 1)
                dve.tensor_tensor(k.gates0[:], k.tops0[:], first.to_broadcast([P, NT, K0]), ALU.subtract).then_inc(shifted, 1)
                dve.wait_ge(exped, 2)
                dve.tensor_reduce(z[:], k.logits0[:], AX.X, ALU.add).then_inc(gated, 1)
                dve.wait_ge(gated, 1)
                dve.reciprocal(z[:], z[:]).then_inc(gated, 1)
                dve.wait_ge(gated, 2)
                dve.tensor_tensor(k.gates0[:], k.gates0[:], shares, ALU.mult).then_inc(gated, 1)
                dve.wait_ge(gated, 3)
                dve.tensor_reduce(z[:], k.gates0[:], AX.X, ALU.add).then_inc(gated, 1)
                dve.wait_ge(gated, 4)
                dve.tensor_scalar(z[:], z[:], 1e-9, None, ALU.add).then_inc(gated, 1)
                dve.wait_ge(gated, 5)
                dve.reciprocal(z[:], z[:]).then_inc(gated, 1)
                dve.wait_ge(gated, 6)
                dve.tensor_tensor(k.gates0[:], k.gates0[:], shares, ALU.mult).then_inc(gated, 1)
                dve.wait_ge(gated, 7)
                dve.wait_ge(w_loaded, 32)
                dve.wait_ge(dinv_out, 1)

                def combine(n, t):
                    for u in (t, t + 1):
                        dve.wait_ge(gathered[u], n * (16 * K0) + 16 * K0)
                    for i in range(K0):
                        for u in (t, t + 1):
                            tile = n * GTR + u
                            if i:
                                dve.wait_ge(added, n * (GTR * K0) + (t * K0 + i * 2 + (u - t) - 1))
                            dve.scalar_tensor_tensor(out=k.x[:, tile, :], in0=rows[:, u, i, :], scalar=k.gates0[:, tile, i:i + 1], in1=k.x[:, tile, :],
                                                     op0=ALU.mult, op1=ALU.add).then_inc(added, 1)

                def average(m):
                    dve.wait_ge(added, m * (GTR * K0) + GTR * K0)
                    dve.tensor_reduce(k.mean[:, tiles(m)], k.x[:, tiles(m), :], AX.X, ALU.add).then_inc(summed, 1)
                    dve.wait_ge(summed, m + 1)
                    dve.tensor_scalar(neg[:, tiles(m)], k.mean[:, tiles(m)], -1.0 / D, None, ALU.mult).then_inc(averaged, 1)
                    dve.wait_ge(averaged, m + 1)
                    dve.tensor_scalar(k.mean[:, tiles(m)], neg[:, tiles(m)], -1.0, None, ALU.mult).then_inc(meant, 1)

                def variance(m):
                    dve.wait_ge(squared, m * GTR + GTR)
                    dve.tensor_scalar(var[:, tiles(m)], squares[:, tiles(m)], 1.0 / D, EPS, ALU.mult, ALU.add).then_inc(scaled, 1)

                def layer_norm(m):
                    dve.wait_ge(meant, m + 1)
                    dve.wait_ge(rstd_out, m + 1)
                    for t in range(GTR):
                        tile = m * GTR + t
                        dve.tensor_scalar(xn[:, t, :], k.x[:, tile, :], k.mean[:, ds(tile, 1)], k.rstd[:, ds(tile, 1)],
                                          ALU.subtract, ALU.mult).then_inc(normed, 1)
                    dve.wait_ge(normed, m * GTR + GTR)
                    dve.tensor_tensor(k.x[:, tiles(m), :], k.x[:, tiles(m), :], b[:, None, :].to_broadcast([P, GTR, D]), ALU.add).then_inc(biased, 1)

                def low_graph(m, i):
                    dve.wait_ge(graph_high, m * SG + (i + 1))
                    dve.tensor_tensor(low[:, i, :, :], raw[:, i, :, :], high[:, i, :, :].bitcast(F32), ALU.subtract).then_inc(graph_low, 1)

                def scale(m):
                    dve.wait_ge(projected, m + 1)
                    dve.tensor_tensor(g32[:], h_ps[:], k.dinv[:, tiles(m), None].to_broadcast([P, GTR, D]), ALU.mult).then_inc(made, 1)

                def low_made(m):
                    dve.wait_ge(made_high, m + 1)
                    dve.tensor_tensor(k.g_low[:, tiles(m), :], g32[:], k.g_high[:, tiles(m), :].bitcast(F32), ALU.subtract).then_inc(made_low, 1)

                def before(m):
                    average(m)
                    variance(m)
                    low_graph(m, 0)
                    layer_norm(m)

                def after(m):
                    low_graph(m, 1)
                    scale(m)
                    low_made(m)

                combine(0, 0)
                combine(0, 2)
                with dve.Fori(1, NG) as n:
                    before(n - 1)
                    combine(n, 0)
                    after(n - 1)
                    combine(n, 2)
                before(NG - 1)
                after(NG - 1)

            @block.scalar
            def _(act):
                act.wait_ge(shifted, 2)
                for t in (k.logits0, k.gates0):
                    act.activation(t[:], t[:], ACT.Exp).then_inc(exped, 1)

                def high_graph(m, i):
                    act.wait_ge(graph_loaded[i], m * 16 + 16)
                    if not isinstance(m, int):
                        act.wait_ge(multiplied, m * SG + (i + 1 - SG))
                    act.activation(high[:, i, :, :], raw[:, i, :, :], ACT.Copy).then_inc(graph_high, 1)

                for m in passes(act, NG):
                    wait_from(act, squared, m * GTR)
                    wait_apart(act, averaged, m + 1, k.passed)
                    for t in range(GTR):
                        tile = m * GTR + t
                        act.activation(junk[:, t, :], k.x[:, tile, :], ACT.Square, bias=neg[:, ds(tile, 1)],
                                       accum_out=squares[:, ds(tile, 1)]).then_inc(squared, 1)
                    high_graph(m, 0)
                    act.wait_ge(turned, m + 1)
                    act.activation(xt[:], t_ps[:], ACT.Copy).then_inc(xt_out, 1)
                    high_graph(m, 1)
                    wait_apart(act, made, m + 1, k.passed)
                    act.activation(k.g_high[:, tiles(m), :], g32[:], ACT.Copy).then_inc(made_high, 1)

            @block.tensor
            def _(pe):
                pe.wait_ge(w_loaded, 32)

                def multiply(m):
                    pe.wait_ge(made_low, m + 1)
                    for i in range(SG):
                        pe.wait_ge(graph_low, m * SG + i + 1)
                        for j in range(JS):
                            tile = m * GTR + i * JS + j
                            for d in range(DC):
                                for g, part in ((k.g_high, high), (k.g_high, low), (k.g_low, high)):
                                    for h in range(2):
                                        t = pe.matmul(acc[:, d * 2 + h, :], g[:, tile, d * P:(d + 1) * P], part[:, i, j, h * 512:(h + 1) * 512],
                                                      start=(tile == 0 and g is k.g_high and part is high), stop=(tile == NT - 1 and g is k.g_low),
                                                      skip_group_check=True)
                        t.then_inc(multiplied, 1)

                for m in range(NG):
                    if m:
                        multiply(m - 1)
                    pe.wait_ge(normed, (m + 1) * GTR)
                    for t in range(GTR):
                        for d in range(DC):
                            i = pe.transpose(t_ps[:, d, t * P:(t + 1) * P], xn[:, t, d * P:(d + 1) * P], k.ident[:])
                    i.then_inc(turned, 1)
                    pe.wait_ge(xt_out, m + 1)
                    for t in range(GTR):
                        for d in range(DC):
                            i = pe.matmul(h_ps[:, t, :], xt[:, d, t * P:(t + 1) * P], w[:, d, :],
                                          start=(d == 0 and t % 2 == 0), stop=(d == DC - 1), skip_group_check=True)
                    i.then_inc(projected, 1)
                multiply(NG - 1)


def combine(k, y, out):
    nc = k.nc
    R = 4
    with ExitStack() as c:
        sb = lambda n, s, d: c.enter_context(nc.sbuf_tensor(f"p9_{n}", s, d))
        sem = lambda n: k.sem(f"p9_{n}")
        rows = sb("rows", [P, R, K1, D], F32)
        at_i = sb("at", [P, R, K1], U32)
        copied, added, stored = sem("copied"), sem("added"), sem("stored")
        gathered = [sem(f"gathered{s}") for s in range(R)]
        with nc.Block() as block:
            @block.gpsimd
            def _(pool):
                for it in passes(pool, NT // R):
                    for s in range(R):
                        n = it * R + s
                        wait_apart(pool, added, n * K1 + K1, k.passed)
                        pool.tensor_copy(at_i[:, s, :], k.slots1[:, n, :]).then_inc(copied, 1)
                        wait_apart(pool, copied, n + 1, k.passed)
                        for i in range(K1):
                            pool.indirect_dma_start(rows[:, s, i, :], None, y, bass.IndirectOffsetOnAxis(ap=at_i[:, s, i:i + 1], axis=0)
                                                    ).then_inc(gathered[s], 16)

            @block.vector
            def _(dve):
                dve.sem_inc(added, R * K1)
                for it in passes(dve, NT // R):
                    for s in range(R):
                        n = it * R + s
                        dve.wait_ge(gathered[s], (it + 1) * (16 * K1))
                        for i in range(K1):
                            if i:
                                dve.wait_ge(added, n * K1 + (R * K1 + i))
                            dve.scalar_tensor_tensor(out=k.x[:, n, :], in0=rows[:, s, i, :], scalar=k.gates1[:, n, i:i + 1], in1=k.x[:, n, :],
                                                     op0=ALU.mult, op1=ALU.add).then_inc(added, 1)

            @block.sync
            def _(sp):
                for it in passes(sp, NT // R):
                    sp.wait_ge(added, (it + 1) * (R * K1) + R * K1)
                    sp.dma_start(out.rearrange("(t p) d -> p t d", p=P)[:, ds(it * R, R), :], k.x[:, ds(it * R, R), :]).then_inc(stored, 16)
                sp.wait_ge(stored, NT // R * 16)


def route1(k, router, bias, xs1):
    nc = k.nc
    GTR = 4
    NG = NT // GTR
    with ExitStack() as c:
        sb = lambda n, s, d: c.enter_context(nc.sbuf_tensor(f"p7_{n}", s, d))
        ps = lambda n, s, d: c.enter_context(nc.psum_tensor(f"p7_{n}", s, d))
        sem = lambda n: k.sem(f"p7_{n}")
        wr = sb("wr", [P, DC, E1], F32)
        bias_sb = sb("bias", [P, E1], F32)
        xn = sb("xn", [P, NT, D], F32)
        xt = sb("xt", [P, 2, DC, GTR * P], F32)
        logits = sb("logits", [P, NT, E1], F32)
        top = sb("top", [P, NT, 8], F32)
        topi = sb("topi", [P, NT, 8], U32)
        idx = sb("idx", [P, NT, K1], F32)
        onehot = sb("onehot", [P, K1, NT, E1], F32)
        prod = sb("prod", [P, K1, NT, E1], F32)
        mask = sb("mask", [P, NT, E1], BF16)
        prefix = [sb(f"prefix{i}", [P, NT + 1, E1], BF16) for i in range(2)]
        count = sb("count", [P, E1], F32)
        count_i = sb("count_i", [P, E1], I32)
        tiles_i = sb("tiles_i", [P, E1], I32)
        ends = [sb(f"ends{i}", [P, E1 + 1], F32) for i in range(2)]
        ordinal = sb("ordinal", [P, LISTED1], F32)
        beyond = sb("beyond", [P, LISTED1, E1], F32)
        owner = sb("owner", [P, LISTED1], F32)
        group_end, group_end_i = sb("group_end", [P, 1], F32), sb("group_end_i", [P, 1], I32)
        base = sb("base", [P, E1], F32)
        place = sb("place", [P, NT, E1], F32)
        slot = sb("slot", [P, NT, K1], F32)
        z = sb("z", [P, NT], F32)
        t_ps = ps("t_ps", [P, 2, DC, GTR * P], F32)
        lg_ps = ps("lg_ps", [P, 2, 512], F32)
        rank_ps, count_ps = ps("rank_ps", [P, 512], F32), ps("count_ps", [P, 512], F32)
        loaded, normed, turned, xt_out, logged, scored = [sem(n) for n in ("loaded", "normed", "turned", "xt_out", "logged", "scored")]
        chain, ranked, placed, scattered, numbered, shifted, exped = [
            sem(n) for n in ("chain", "ranked", "placed", "scattered", "numbered", "shifted", "exped")]
        with nc.Block() as block:
            MASKED = 2 * NT + 1 + K1 + 5 + 1 + 2 * 5

            def last(r, j):
                return isinstance(r, int) and r * 2 + j == NG - 1

            @block.sync
            def _(sp):
                sp.dma_start(wr[:], router.rearrange("(c p) e -> p c e", p=P)).then_inc(loaded, 16)
                sp.dma_start(bias_sb[:], bias.rearrange("(a e) -> a e", a=1).to_broadcast([P, E1])).then_inc(loaded, 16)

            @block.scalar
            def _(act):
                for it in passes(act, NG // 2):
                    for s in range(2):
                        n = it * 2 + s
                        act.wait_ge(turned, n + 1)
                        act.activation(xt[:, s, :, :], t_ps[:, s, :, :], ACT.Copy).then_inc(xt_out, 1)
                act.wait_ge(shifted, 1)
                act.activation(k.gates1[:], k.gates1[:], ACT.Exp).then_inc(exped, 1)

            @block.tensor
            def _(pe):
                pe.wait_ge(loaded, 32)

                def turn(r, j):
                    pe.wait_ge(normed, (r * 2 + j) * GTR + GTR)
                    for t in range(GTR):
                        for d in range(DC):
                            m = pe.transpose(t_ps[:, j, d, t * P:(t + 1) * P], k.xring[:, j, t, d * P:(d + 1) * P], k.ident[:])
                    m.then_inc(turned, 1)

                turn(0, 0)
                for r, j in units(pe, NG, 2):
                    n = r * 2 + j
                    if not last(r, j):
                        turn(*moved(r, j, 1, 2))
                    pe.wait_ge(xt_out, n + 1)
                    wait_from(pe, scored, n * 2)
                    for t in range(GTR):
                        for d in range(DC):
                            m = pe.matmul(lg_ps[:, j, t * E1:(t + 1) * E1], xt[:, j, d, t * P:(t + 1) * P], wr[:, d, :],
                                          start=(t == 0 and d == 0), stop=(d == DC - 1), skip_group_check=True)
                    m.then_inc(logged, 1)
                pe.wait_ge(chain, MASKED)
                flat = lambda a: a.rearrange("p t e -> p (t e)")
                pe.matmul(rank_ps[:, 0:NT * E1], k.tri[:], flat(mask[:]), start=True, stop=False)
                pe.matmul(rank_ps[:, 0:NT * E1], k.onesb[:], flat(prefix[1][:, 0:NT, :]), start=False, stop=True).then_inc(ranked, 1)
                pe.matmul(count_ps[:, 0:E1], k.onesb[:], prefix[1][:, NT, :], start=True, stop=True).then_inc(ranked, 1)

            @block.vector
            def _(dve):
                dve.wait_ge(loaded, 32)

                def layer_norm(r, j):
                    n = r * 2 + j
                    if not isinstance(r, int) or n >= 2:
                        dve.wait_ge(turned, n - 1)
                    for t in range(GTR):
                        tile = n * GTR + t
                        dve.tensor_scalar(k.xring[:, j, t, :], k.x[:, tile, :], k.mean[:, ds(tile, 1)], k.rstd[:, ds(tile, 1)],
                                          ALU.subtract, ALU.mult).then_inc(normed, 1)
                    dve.wait_ge(normed, n * GTR + GTR)
                    dve.tensor_copy(xn[:, ds(n * GTR, GTR), :], k.xring[:, j, :, :]).then_inc(scored, 1)

                layer_norm(0, 0)
                layer_norm(0, 1)
                for r, j in units(dve, NG, 2):
                    n = r * 2 + j
                    if not (isinstance(r, int) and r == NG // 2 - 1):
                        layer_norm(r + 1, j)
                    dve.wait_ge(logged, n + 1)
                    dve.tensor_tensor(logits[:, ds(n * GTR, GTR), :], lg_ps[:, j, 0:GTR * E1].rearrange("p (t e) -> p t e", e=E1),
                                      bias_sb[:, None, :].to_broadcast([P, GTR, E1]), ALU.add).then_inc(scored, 1)
                dve.wait_ge(scored, 2 * NG)
                links = 0

                def link(*steps):
                    nonlocal links
                    for step in steps:
                        step.then_inc(chain, 1)
                    links += len(steps)
                    dve.wait_ge(chain, links)

                link(*[dve.max(top[:, t, :], logits[:, t, :]) for t in range(NT)])
                link(*[dve.max_index(topi[:, t, :], top[:, t, :], logits[:, t, :]) for t in range(NT)])
                link(dve.tensor_copy(idx[:], topi[:, :, 0:K1]))
                link(*[dve.tensor_tensor(onehot[:, i, :, :], k.iota[:, None, 0:E1].to_broadcast([P, NT, E1]),
                                         idx[:, :, i:i + 1].to_broadcast([P, NT, E1]), ALU.is_equal) for i in range(K1)])
                link(dve.tensor_tensor(mask[:], onehot[:, 0, :, :], onehot[:, 1, :, :], ALU.add), dve.memset(prefix[0][:, 0:1, :], 0.0),
                     dve.memset(prefix[1][:, 0:1, :], 0.0), dve.memset(ends[0][:, 0:1], 0.0), dve.memset(ends[1][:, 0:1], 0.0))
                link(dve.tensor_copy(prefix[0][:, 1:, :], mask[:]))
                for b in range(5):
                    a, z2, by = prefix[b % 2], prefix[(b + 1) % 2], 1 << b
                    link(dve.tensor_copy(z2[:, 1:1 + by, :], a[:, 1:1 + by, :]),
                         dve.tensor_tensor(z2[:, 1 + by:, :], a[:, 1 + by:, :], a[:, 1:NT + 1 - by, :], ALU.add))
                assert links == MASKED
                dve.wait_ge(ranked, 2)
                link(dve.tensor_scalar(count[:], count_ps[:, 0:E1], float(T1 - 1), None, ALU.add))
                link(dve.tensor_copy(count_i[:], count[:]))
                link(dve.tensor_single_scalar(tiles_i[:], count_i[:], T1.bit_length() - 1, ALU.arith_shift_right))
                link(dve.tensor_copy(ends[0][:, 1:], tiles_i[:]))
                for b in range(3):
                    a, z2, by = ends[b % 2], ends[(b + 1) % 2], 1 << b
                    link(dve.tensor_copy(z2[:, 1:1 + by], a[:, 1:1 + by]),
                         dve.tensor_tensor(z2[:, 1 + by:], a[:, 1 + by:], a[:, 1:E1 + 1 - by], ALU.add))
                end = ends[1]
                dve.wait_ge(numbered, 1)
                link(dve.tensor_tensor(beyond[:], ordinal[:, :, None].to_broadcast([P, LISTED1, E1]), end[:, None, 1:].to_broadcast([P, LISTED1, E1]), ALU.is_ge),
                     dve.tensor_scalar(base[:], end[:, 0:E1], float(T1), None, ALU.mult),
                     dve.tensor_scalar(group_end[:], end[:, E1:], -1.0, None, ALU.add))
                link(dve.tensor_copy(group_end_i[:], group_end[:]), dve.tensor_reduce(owner[:], beyond[:], AX.X, ALU.add),
                     dve.tensor_tensor(place[:], rank_ps[:, 0:NT * E1].rearrange("p (t e) -> p t e", e=E1),
                                       base[:, None, :].to_broadcast([P, NT, E1]), ALU.add))
                link(dve.tensor_scalar(owner[:], owner[:], float(E1 - 1), None, ALU.min),
                     dve.tensor_tensor(prod[:], onehot[:], place[:, None, :, :].to_broadcast([P, K1, NT, E1]), ALU.mult))
                link(dve.tensor_single_scalar(k.last_group1[:], group_end_i[:], UG.bit_length() - 1, ALU.arith_shift_right),
                     dve.tensor_copy(k.owner1[:], owner[:]), dve.tensor_reduce(slot[:].rearrange("p t k -> p k t"), prod[:], AX.X, ALU.add))
                dve.tensor_copy(k.slots1[:], slot[:]).then_inc(placed, 1)
                dve.tensor_tensor(k.gates1[:], top[:, :, 0:K1], top[:, :, 0:1].to_broadcast([P, NT, K1]), ALU.subtract).then_inc(shifted, 1)
                dve.wait_ge(exped, 1)
                link(dve.tensor_reduce(z[:], k.gates1[:], AX.X, ALU.add))
                link(dve.reciprocal(z[:], z[:]))
                link(dve.tensor_tensor(k.gates1[:], k.gates1[:], z[:, :, None].to_broadcast([P, NT, K1]), ALU.mult))

            @block.gpsimd
            def _(pool):
                pool.iota(ordinal[:], pattern=[[1, LISTED1]], base=0, channel_multiplier=0, allow_small_or_imprecise_dtypes=True).then_inc(numbered, 1)
                pool.wait_ge(placed, 1)
                for t in range(NT):
                    for i in range(K1):
                        pool.indirect_dma_start(xs1, bass.IndirectOffsetOnAxis(ap=k.slots1[:, t, i:i + 1], axis=0), xn[:, t, :], None,
                                                bounds_check=SLOTS1 - 1, oob_is_err=False).then_inc(scattered, 16)
                pool.wait_ge(scattered, 16 * NT * K1)


def experts1(k, weights, b1, b2, xs1, y1):
    nc = k.nc
    UT = UG
    TR = T1 // P
    W1, W2 = DC * F1, FB1 * D
    PAIRS = FB1 // 2
    with ExitStack() as c:
        sb = lambda n, s, d: c.enter_context(nc.sbuf_tensor(f"p8_{n}", s, d))
        ps = lambda n, s, d: c.enter_context(nc.psum_tensor(f"p8_{n}", s, d))
        sem = lambda n: k.sem(f"p8_{n}")
        pair = lambda n, s: [sb(n + "_high", s, F32R), sb(n + "_low", s, F32R)]
        raw1, raw2 = sb("raw1", [P, 2, W1], F32), sb("raw2", [P, 2, W2], F32)
        w1, w2 = pair("w1", [P, 2, W1]), pair("w2", [P, 2, W2])
        bias1, bias2 = sb("bias1", [P, UT, FB1], F32), sb("bias2", [P, UT, D], F32)
        x = sb("x", [P, 2, TR, D], F32)
        xt = pair("xt", [P, 2, DC, T1])
        h = sb("h", [P, PAIRS, 2, T1], F32)
        h_parts = pair("h_parts", [P, 2, PAIRS, 2, T1])
        y = sb("y", [P, 2, TR, D], F32)
        t_ps, h_ps, down_ps = ps("t_ps", [P, DC, T1], F32), ps("h_ps", [P, PAIRS, 2, T1], F32), ps("down_ps", [P, 2, TR, D], F32)
        rows_loaded, w1_loaded, w2_loaded, stored = [[sem(f"{n}{s}") for s in range(2)]
                                                     for n in ("rows_loaded", "w1_loaded", "w2_loaded", "stored")]
        zero, zeroed, zeros_out = sb("zero", [P, TR * D], F32), sem("zeroed"), sem("zeros_out")
        bias_loaded = [sem(f"bias_loaded{s}") for s in range(UT)]
        turned, xt_high, xt_low, w1_high, w1_low, w2_high, w2_low, lifted, relu_out, h_high, h_low, lowered, y_out = [
            sem(n) for n in ("turned", "xt_high", "xt_low", "w1_high", "w1_low", "w2_high", "w2_low", "lifted", "relu_out",
                             "h_high", "h_low", "lowered", "y_out")]
        xs_v = xs1.rearrange("(n p r) d -> n p (r d)", p=P, r=TR)
        y_v = y1.rearrange("(n p r) d -> n p (r d)", p=P, r=TR)

        def uses(r, j):
            return r * (UT // 2) + j // 2 + 1

        def last_group(eng):
            return eng.value_load(k.last_group1[0:1, 0:1], min_val=0, max_val=NT1 // UT - 1)

        def first(r, j):
            return isinstance(r, int) and r == 0 and j == 0

        with nc.Block() as block:
            @block.sync
            def _(sp):
                last = last_group(sp)

                def load(r, j):
                    m, s = r * UT + j, j % 2
                    tile = ds(m, 1)
                    owner = sp.value_load(k.owner1[0:1, tile], min_val=0, max_val=E1 - 1)
                    expert = ds(owner, 1)
                    fresh = {}
                    if not isinstance(r, int) or m >= 2:
                        before = sp.value_load(k.owner1[0:1, ds(m - 2, 1)], min_val=0, max_val=E1 - 1)
                        fresh = dict(bounds_check="skip_entire_dma", cond=(owner != before))
                        wait_apart(sp, turned, m - 1, k.passed)
                    sp.dma_start(x[:, s, :, :].rearrange("p r d -> p (r d)"), xs_v[tile, :, :].rearrange("a p n -> p (a n)")).then_inc(rows_loaded[s], 16)
                    if fresh:
                        wait_apart(sp, w1_low, 2 * m - 2, k.passed)
                    sp.dma_start(raw1[:, s, :], weights[expert, :, 0:W1].rearrange("a p n -> p (a n)"), **fresh).then_inc(w1_loaded[s], 16)
                    if not isinstance(r, int) or m >= UT:
                        wait_apart(sp, y_out, m - (UT - 1), k.passed)
                    sp.dma_start(bias1[:, j, :], b1[expert, :, :].rearrange("a p n -> p (a n)")).then_inc(bias_loaded[j], 16)
                    sp.dma_start(bias2[:, j, :], b2[expert, :].to_broadcast([P, D])).then_inc(bias_loaded[j], 16)
                    if fresh:
                        wait_apart(sp, w2_low, m - 1, k.passed)
                    sp.dma_start(raw2[:, s, :], weights[expert, :, W1:].rearrange("a p n -> p (a n)"), **fresh).then_inc(w2_loaded[s], 16)

                load(0, 0)
                for r, j in listed_units(sp, last, NT1):
                    load(*moved(r, j, 1, UT))
                wait_apart(sp, bias_loaded[0], last * 32 + 64, k.passed)
                wait_apart(sp, w2_loaded[0], last * 32 + 48, k.passed)

            @block.tensor
            def _(pe):
                def turn(r, j):
                    m, s = r * UT + j, j % 2
                    pe.wait_ge(rows_loaded[s], uses(r, j) * 16)
                    wait_from(pe, xt_low, m)
                    for i in range(TR):
                        for d in range(DC):
                            t = pe.transpose(t_ps[:, d, i * P:(i + 1) * P], x[:, s, i, d * P:(d + 1) * P], k.ident[:])
                    t.then_inc(turned, 1)

                def lift(r, j):
                    m, s = r * UT + j, j % 2
                    pe.wait_ge(w1_low, 2 * m + 2)
                    pe.wait_ge(xt_low, m + 1)
                    for p in range(PAIRS):
                        if not first(r, j):
                            pe.wait_ge(relu_out, m * PAIRS + (p + 1 - PAIRS))
                        for q in range(2):
                            f = p * 2 + q
                            for d in range(DC):
                                t = split_products(pe, h_ps[:, p, q, :], [a[:, s, d * F1 + f * P:d * F1 + (f + 1) * P] for a in w1],
                                                   [a[:, s, d, :] for a in xt], d == 0 and q == 0, d == DC - 1)
                        t.then_inc(lifted, 1)

                def lower(r, j):
                    m, s = r * UT + j, j % 2
                    pe.wait_ge(w2_low, m + 1)
                    if not isinstance(r, int) or m >= 2:
                        pe.wait_ge(y_out, m - 1)
                    for p in range(PAIRS):
                        pe.wait_ge(h_low, m * PAIRS + (p + 1))
                        for q in range(2):
                            f = p * 2 + q
                            for i in range(TR):
                                t = split_products(pe, down_ps[:, s, i, :], [a[:, s, p, q, i * P:(i + 1) * P] for a in h_parts],
                                                   [a[:, s, f * D:(f + 1) * D] for a in w2], f == 0 and i == 0, f == FB1 - 1)
                    t.then_inc(lowered, 1)

                last = last_group(pe)
                turn(0, 0)
                for r, j in listed_units(pe, last, NT1):
                    turn(*moved(r, j, 1, UT))
                    lift(r, j)
                    if not first(r, j):
                        lower(*moved(r, j, -1, UT))
                lower(last, UT - 1)

            @block.scalar
            def _(act):
                def high_w1(r, j):
                    m, s = r * UT + j, j % 2
                    act.wait_ge(w1_loaded[s], uses(r, j) * 16)
                    if not isinstance(r, int) or m >= 2:
                        act.wait_ge(lifted, m * PAIRS - PAIRS)
                    for d in range(DC):
                        part = slice(d * F1, (d + 1) * F1)
                        act.activation(w1[0][:, s, part], raw1[:, s, part], ACT.Copy).then_inc(w1_high, 1)

                def high_turned(r, j):
                    act.wait_ge(turned, r * UT + (j + 1))
                    act.activation(xt[0][:, j % 2, :, :], t_ps[:], ACT.Copy).then_inc(xt_high, 1)

                def relus(r, j):
                    m = r * UT + j
                    act.wait_ge(bias_loaded[j], r * 32 + 32)
                    for p in range(PAIRS):
                        act.wait_ge(lifted, m * PAIRS + (p + 1))
                        if not first(r, j):
                            act.wait_ge(h_low, m * PAIRS + (p + 1 - PAIRS))
                        for q in range(2):
                            t = act.activation(h[:, p, q, :], h_ps[:, p, q, :], ACT.Relu, bias=bias1[:, j, p * 2 + q:p * 2 + q + 1])
                        t.then_inc(relu_out, 1)

                def high_w2(r, j):
                    m, s = r * UT + j, j % 2
                    act.wait_ge(w2_loaded[s], uses(r, j) * 16)
                    if not isinstance(r, int) or m >= 2:
                        act.wait_ge(lowered, m - 1)
                    act.activation(w2[0][:, s, :], raw2[:, s, :], ACT.Copy).then_inc(w2_high, 1)

                last = last_group(act)
                high_w1(0, 0)
                high_turned(0, 0)
                for r, j in listed_units(act, last, NT1):
                    high_w1(*moved(r, j, 1, UT))
                    high_turned(*moved(r, j, 1, UT))
                    relus(r, j)
                    high_w2(r, j)

            @block.vector
            def _(dve):
                def low_w1(r, j):
                    m, s = r * UT + j, j % 2
                    for d in range(DC):
                        part = slice(d * F1, (d + 1) * F1)
                        dve.wait_ge(w1_high, m * DC + (d + 1))
                        dve.tensor_tensor(w1[1][:, s, part], raw1[:, s, part], w1[0][:, s, part].bitcast(F32), ALU.subtract).then_inc(w1_low, 1)

                def low_turned(r, j):
                    dve.wait_ge(xt_high, r * UT + (j + 1))
                    dve.tensor_tensor(xt[1][:, j % 2, :, :], t_ps[:], xt[0][:, j % 2, :, :].bitcast(F32), ALU.subtract).then_inc(xt_low, 1)

                def split_hidden(r, j):
                    m, s = r * UT + j, j % 2
                    for p in range(PAIRS):
                        dve.wait_ge(relu_out, m * PAIRS + (p + 1))
                        dve.tensor_copy(h_parts[0][:, s, p, :, :], h[:, p, :, :]).then_inc(h_high, 1)
                        dve.wait_ge(h_high, m * PAIRS + (p + 1))
                        dve.tensor_tensor(h_parts[1][:, s, p, :, :], h[:, p, :, :], h_parts[0][:, s, p, :, :].bitcast(F32), ALU.subtract).then_inc(h_low, 1)

                def low_w2(r, j):
                    s = j % 2
                    dve.wait_ge(w2_high, r * UT + (j + 1))
                    dve.tensor_tensor(w2[1][:, s, :], raw2[:, s, :], w2[0][:, s, :].bitcast(F32), ALU.subtract).then_inc(w2_low, 1)

                def results(r, j):
                    m, s = r * UT + j, j % 2
                    dve.wait_ge(lowered, m + 1)
                    dve.wait_ge(bias_loaded[j], r * 32 + 32)
                    if not isinstance(r, int) or m >= 2:
                        dve.wait_ge(stored[s], uses(r, j) * 16 - 16)
                    dve.tensor_tensor(y[:, s, :, :], down_ps[:, s, :, :], bias2[:, j, None, :].to_broadcast([P, TR, D]), ALU.add).then_inc(y_out, 1)

                last = last_group(dve)
                low_w1(0, 0)
                low_turned(0, 0)
                for r, j in listed_units(dve, last, NT1):
                    if not isinstance(r, int) or r * UT + j >= 2:
                        results(*moved(r, j, -2, UT))
                    low_w1(*moved(r, j, 1, UT))
                    low_turned(*moved(r, j, 1, UT))
                    split_hidden(r, j)
                    low_w2(r, j)
                results(last, UT - 2)
                results(last, UT - 1)

            @block.gpsimd
            def _(pool):
                last = last_group(pool)
                pool.memset(zero[:], 0.0).then_inc(zeroed, 1)
                pool.wait_ge(zeroed, 1)
                with pool.Fori(UG, NT1) as n:
                    pool.dma_start(y_v[ds(n, 1), :, :].rearrange("a p n -> p (a n)"), zero[:],
                                   bounds_check="skip_entire_dma", cond=(last * UG + UG <= n)).then_inc(zeros_out, 16)
                for r, j in listed_units(pool, last, NT1):
                    wait_apart(pool, y_out, r * UT + (j + 1), k.passed)
                    pool.dma_start(y_v[ds(r * UT + j, 1), :, :].rearrange("a p n -> p (a n)"),
                                   y[:, j % 2, :, :].rearrange("p r d -> p (r d)")).then_inc(stored[j % 2], 16)
                for s in range(2):
                    wait_apart(pool, stored[s], last * 32 + 32, k.passed)
                pool.wait_ge(zeros_out, (NT1 - UG) * 16)


def build(nc, a, out):
    xs0 = nc.dram_tensor("sent0", [SLOTS0, D], F32).ap()
    y0 = nc.dram_tensor("results0", [RESULTS0 + HALF, D], F32).ap()
    xs1 = nc.dram_tensor("sent1", [SLOTS1, D], F32).ap()
    y1 = nc.dram_tensor("results1", [NT1 * T1, D], F32).ap()
    with ExitStack() as ctx:
        k = Kernel(nc, ctx)
        make_constants(k)
        sb = lambda c, n, s, d: c.enter_context(nc.sbuf_tensor(n, s, d))
        k.mean, k.rstd = sb(ctx, "mean", [P, NT], F32), sb(ctx, "rstd", [P, NT], F32)
        with ExitStack() as c:
            k.xw = sb(c, "xw", [P, NT, D], F32R)
            sign_features(k, a["x"], a["gnn0_t"])

            def add_rows(dve, q, rows, finished):
                x = k.x[:, q * GT:(q + 1) * GT, :]
                dve.tensor_tensor(x, x, rows, ALU.add).then_inc(finished, 1)

            gnn(k, "p2", a["adj_t"], [k.xw], add_rows, True)
        with ExitStack() as c2, ExitStack() as c:
            k.g_high, k.g_low = sb(c2, "g_high", [P, NT, D], F32R), sb(c2, "g_low", [P, NT, D], F32R)
            k.rows0 = sb(c, "rows0", [P, E0], I32)
            k.slots0, k.gates0 = sb(c, "slots0", [P, NT, K0], U32), sb(c, "gates0", [P, NT, K0], F32)
            k.logits0, k.tops0, k.zrow = sb(c, "logits0", [P, NT, E0], F32), sb(c, "tops0", [P, NT, K0], F32), sb(c, "zrow", [P, RPP // 2, D], F32)
            k.units0, k.last_group0 = sb(c, "units0", [P, LISTED], I32), sb(c, "last_group0", [P, 1], I32)
            route0(k, a["router0_t"], a["bias0"], a["shared0"], xs0, y0)
            experts0(k, a["experts0"], xs0, y0)
            k.clear_semaphores()
            acc = c2.enter_context(nc.psum_tensor("acc", [P, 4, 512], F32))
            combine_and_project(k, y0, a, acc)
            c.close()

            def add_scaled(dve, q, rows, finished):
                for t in range(GT):
                    tile = q * GT + t
                    m = dve.scalar_tensor_tensor(out=k.x[:, tile, :], in0=rows[:, t, :], scalar=k.dinv[:, tile:tile + 1], in1=k.x[:, tile, :],
                                                 op0=ALU.mult, op1=ALU.add)
                m.then_inc(finished, 1)

            gnn(k, "p6", a["adj"], [k.g_high, k.g_low], add_scaled, False, fill=[xs1], acc=acc)
        with ExitStack() as c:
            k.slots1, k.gates1 = sb(c, "slots1", [P, NT, K1], U32), sb(c, "gates1", [P, NT, K1], F32)
            k.owner1, k.last_group1, k.xring = sb(c, "owner1", [P, LISTED1], I32), sb(c, "last_group1", [P, 1], I32), sb(c, "xring", [P, 2, 4, D], F32)
            route1(k, a["router1"], a["bias1"], xs1)
            experts1(k, a["experts1"], a["b1"], a["b2"], xs1, y1)
            combine(k, y1, out)


def kernel(**inputs):
    import concourse.bacc as bacc
    from concourse.bass_utils import run_bass_kernel_spmd

    i = {name: np.asarray(v) for name, v in inputs.items()}
    chunks = lambda w: w.transpose(0, 2, 1).reshape(w.shape[0], DC, P, -1).transpose(0, 2, 1, 3).reshape(w.shape[0], P, -1)
    swiglu = lambda g, u, d: np.concatenate([chunks(i[g]), chunks(i[u]), i[d].transpose(0, 2, 1)], axis=2)
    w1, w2 = i["L1_ffn_W1"], i["L1_ffn_W2"]
    arrays = {
        "x": i["x"],
        "adj": i["adj"],
        "adj_t": i["adj"].T,
        "gnn0_t": i["L0_gnn_weight"].T,
        "router0_t": i["L0_ffn_router_w"].T,
        "bias0": i["L0_ffn_bias"],
        "shared0": swiglu("L0_ffn_shared_w_gate", "L0_ffn_shared_w_up", "L0_ffn_shared_w_down"),
        "experts0": swiglu("L0_ffn_w_gate", "L0_ffn_w_up", "L0_ffn_w_down"),
        "gnn1": i["L1_gnn_weight"],
        "gnn1_bias": i["L1_gnn_bias"],
        "router1": i["L1_ffn_Wr"],
        "bias1": i["L1_ffn_br"],
        "experts1": np.concatenate([
            w1.reshape(E1, DC, P, F1).transpose(0, 2, 1, 3).reshape(E1, P, -1),
            w2.reshape(E1, FB1, P, D).transpose(0, 2, 1, 3).reshape(E1, P, -1)], axis=2),
        "b1": i["L1_ffn_b1"].reshape(E1, FB1, P).transpose(0, 2, 1),
        "b2": i["L1_ffn_b2"],
    }
    arrays = {f"in_{n}": np.ascontiguousarray(v) for n, v in arrays.items()}
    nc = bacc.Bacc("TRN2", target_bir_lowering=False, num_devices=1)
    aps = {n[3:]: nc.dram_tensor(n, v.shape, mybir.dt.from_np(v.dtype), kind="ExternalInput").ap() for n, v in arrays.items()}
    out = nc.dram_tensor("out", (N, D), F32, kind="ExternalOutput").ap()
    build(nc, aps, out)
    r = run_bass_kernel_spmd(nc, [arrays], core_ids=[0])
    return r.results[0]["out"]
```
